# Optimizing a Trainium2 kernel written in Bass

```python
import numpy as np
import jax
import jax.numpy as jnp

def _softmax(x, axis=-1):
    return jax.nn.softmax(x, axis=axis)

def _gelu(x):
    return jax.nn.gelu(x, approximate=True)

def _silu(x):
    return jax.nn.silu(x)

def _sigmoid(x):
    return jax.nn.sigmoid(x)

def _layernorm(x, axis=-1, eps=1e-05):
    m = jnp.mean(x, axis=axis, keepdims=True)
    v = jnp.var(x, axis=axis, keepdims=True)
    return (x - m) / jnp.sqrt(v + eps)

def _scatter_add(tgt, idx, src, axis=0):
    return tgt.at[idx].add(src)

def _segment_sum(src, seg, n):
    return jax.ops.segment_sum(src, seg, n)
kernel_name = 'mk_decoder_preln_d1_seqx_r4_866df9'

def setup_inputs(seed: int=0):
    np.random.seed(seed)
    _w = jnp.asarray

    def _rec_inputs():
        import jax
        import jax.numpy as jnp
        _rk = jax.random.key(seed)
        x = -0.0002928 + 1 * jax.random.normal(jax.random.fold_in(_rk, 1), (16, 256, 256), jnp.float32)
        _lenS = 256 - jax.random.randint(jax.random.fold_in(_rk, 7), (16,), 0, max(1, 256 // 4) + 1, jnp.int32)
        _lenS2 = 256 - jax.random.randint(jax.random.fold_in(_rk, 8), (16,), 0, max(1, 256 // 4) + 1, jnp.int32)
        _ctx_1024P = jax.random.normal(jax.random.fold_in(_rk, 11), (16, 16, 256), jnp.float32)
        _ctx_1024c = jax.random.dirichlet(jax.random.fold_in(_rk, 511), 0.3 * jnp.ones((16,), jnp.float32), (16, 256))
        _ctx_1024t = jnp.einsum('bsk,bkd->bsd', _ctx_1024c, _ctx_1024P)
        _ctx_1024t = _ctx_1024t * jax.lax.rsqrt(jnp.mean(jnp.square(_ctx_1024t)) + 1e-12) * 0.953939
        ctx_1024 = -1.39393e-06 + 0.999914 * (_ctx_1024t + 0.3 * jax.random.normal(jax.random.fold_in(_rk, 611), (16, 256, 256), jnp.float32))
        return (x, ctx_1024)
    x, ctx_1024 = _rec_inputs()

    def _L0_attn_setup():
        import jax, jax.numpy as jnp
        import numpy as np
        import math
        EMBED = 256
        HEADS = 16
        HEAD_DIM = EMBED // HEADS
        HIDDEN = 1024
        NUM_BUCKETS = 32
        MAX_DISTANCE = 128
        LN_EPS = 1e-06
        KQ_EPS = 1e-06

        def _rms_norm(xs, weight):
            xf = xs.astype(jnp.float32)
            var = jnp.mean(jnp.square(xf), axis=-1, keepdims=True)
            ys = xs * jax.lax.rsqrt(var + LN_EPS) * weight
            return ys.astype(xs.dtype)

        def _normalize_kq(kq):
            ss = jnp.sum(jnp.square(kq), axis=-1, keepdims=True)
            return kq * jax.lax.rsqrt(ss + KQ_EPS)

        def _rel_position_bucket(rp):
            rp = -jnp.minimum(rp, 0)
            max_exact = NUM_BUCKETS // 2
            is_small = rp < max_exact
            safe = jnp.maximum(rp, 1).astype(jnp.float32)
            large = max_exact + (jnp.log(safe / max_exact) / math.log(MAX_DISTANCE / max_exact) * (NUM_BUCKETS - max_exact)).astype(jnp.int32)
            large = jnp.minimum(large, NUM_BUCKETS - 1)
            return jnp.where(is_small, rp, large)
        key = jax.random.key(seed)
        ks = jax.random.split(key, 8)
        B, S = (2, 512)
        w = 0.02
        return {'x': jax.random.normal(ks[0], (B, S, EMBED), dtype=jnp.float32), 'ln1_w': jnp.ones((EMBED,), jnp.float32), 'Wq': jax.random.normal(ks[1], (EMBED, EMBED), jnp.float32) * w, 'Wk': jax.random.normal(ks[2], (EMBED, EMBED), jnp.float32) * w, 'Wv': jax.random.normal(ks[3], (EMBED, EMBED), jnp.float32) * w, 'rel_bias': jax.random.normal(ks[4], (NUM_BUCKETS, HEADS), jnp.float32) * w, 'scale': jnp.ones((HEADS,), jnp.float32), 'Wo': jax.random.normal(ks[5], (EMBED, EMBED), jnp.float32) * w, 'ln2_w': jnp.ones((EMBED,), jnp.float32), 'W1': jax.random.normal(ks[6], (EMBED, HIDDEN), jnp.float32) * w, 'W2': jax.random.normal(ks[7], (HIDDEN, EMBED), jnp.float32) * w}
    _L0_attn_all = _L0_attn_setup()
    _L0_attn_in = {k: v for k, v in _L0_attn_all.items() if k in ('ln1_w', 'Wq', 'Wk', 'Wv', 'rel_bias', 'scale', 'Wo', 'ln2_w', 'W1', 'W2')}
    del _L0_attn_all

    def _L0_xattn_setup():
        import jax, jax.numpy as jnp
        import numpy as np
        import math
        D_MODEL = 256
        NUM_HEADS = 8
        D_HEAD = D_MODEL // NUM_HEADS
        D_FF = 4 * D_MODEL
        LN_EPS = 1e-05

        def _layer_norm(x, g, b):
            mu = jnp.mean(x, axis=-1, keepdims=True)
            var = jnp.mean((x - mu) ** 2, axis=-1, keepdims=True)
            return (x - mu) * jax.lax.rsqrt(var + LN_EPS) * g + b
        key = jax.random.key(seed)
        ks = jax.random.split(key, 16)
        B, Sq, Sk = (2, 512, 512)
        s = 1.0 / math.sqrt(D_MODEL)
        inp = {'query': jax.random.normal(ks[0], (B, Sq, D_MODEL), jnp.float32), 'key': jax.random.normal(ks[1], (B, Sk, D_MODEL), jnp.float32), 'value': jax.random.normal(ks[2], (B, Sk, D_MODEL), jnp.float32), 'Wq': jax.random.normal(ks[3], (D_MODEL, D_MODEL), jnp.float32) * s, 'Wk': jax.random.normal(ks[4], (D_MODEL, D_MODEL), jnp.float32) * s, 'Wv': jax.random.normal(ks[5], (D_MODEL, D_MODEL), jnp.float32) * s, 'Wo': jax.random.normal(ks[6], (D_MODEL, D_MODEL), jnp.float32) * s, 'lambda_param': jnp.asarray(0.8, jnp.float32), 'ln1_g': jnp.ones((D_MODEL,), jnp.float32), 'ln1_b': jnp.zeros((D_MODEL,), jnp.float32), 'ln2_g': jnp.ones((D_MODEL,), jnp.float32), 'ln2_b': jnp.zeros((D_MODEL,), jnp.float32), 'ffn_w1': jax.random.normal(ks[7], (D_MODEL, D_FF), jnp.float32) * s, 'ffn_b1': jnp.zeros((D_FF,), jnp.float32), 'ffn_w2': jax.random.normal(ks[8], (D_FF, D_MODEL), jnp.float32) * (1.0 / math.sqrt(D_FF)), 'ffn_b2': jnp.zeros((D_MODEL,), jnp.float32)}
        return inp
    _L0_xattn_all = _L0_xattn_setup()
    _L0_xattn_in = {k: v for k, v in _L0_xattn_all.items() if k in ('Wq', 'Wk', 'Wv', 'Wo', 'lambda_param', 'ln1_g', 'ln1_b', 'ln2_g', 'ln2_b', 'ffn_w1', 'ffn_b1', 'ffn_w2', 'ffn_b2')}
    del _L0_xattn_all

    def _L0_ffn_setup():
        import jax, jax.numpy as jnp
        import numpy as np
        EPS = 1e-06
        N_EXPERTS = 8

        def _rms_norm(x, scale, eps=EPS):
            mean_sq = jnp.mean(x.astype(jnp.float32) ** 2, axis=-1, keepdims=True)
            s = scale.astype(jnp.float32) * jax.lax.rsqrt(mean_sq + eps)
            return x * s.astype(x.dtype)

        def _dist2(x, y):
            nx = jnp.sum(x ** 2, axis=-1)[..., :, None]
            ny = jnp.sum(y ** 2, axis=-1)[..., None, :]
            return nx + ny - 2.0 * (x @ y.T)
        key = jax.random.key(seed)
        ks = jax.random.split(key, 5)
        dim, hidden, E = (256, 512, N_EXPERTS)
        x = jax.random.normal(ks[0], (4, 512, dim), dtype=jnp.float32)
        scale = jnp.ones((dim,), dtype=jnp.float32)
        centroids = jax.random.normal(ks[1], (E, dim), dtype=jnp.float32)
        up_w = jax.random.normal(ks[2], (E, dim, hidden * 2), dtype=jnp.float32) * dim ** (-0.5)
        down_w = jax.random.normal(ks[3], (E, hidden, dim), dtype=jnp.float32) * hidden ** (-0.5)
        return {'x': x, 'scale': scale, 'centroids': centroids, 'up_w': up_w, 'down_w': down_w}
    _L0_ffn_all = _L0_ffn_setup()
    _L0_ffn_in = {k: v for k, v in _L0_ffn_all.items() if k in ('scale', 'centroids', 'up_w', 'down_w')}
    del _L0_ffn_all
    return {'x': x, 'ctx_1024': ctx_1024, 'L0_attn_ln1_w': _L0_attn_in['ln1_w'], 'L0_attn_Wq': _L0_attn_in['Wq'], 'L0_attn_Wk': _L0_attn_in['Wk'], 'L0_attn_Wv': _L0_attn_in['Wv'], 'L0_attn_rel_bias': _L0_attn_in['rel_bias'], 'L0_attn_scale': _L0_attn_in['scale'], 'L0_attn_Wo': _L0_attn_in['Wo'], 'L0_attn_ln2_w': _L0_attn_in['ln2_w'], 'L0_attn_W1': _L0_attn_in['W1'], 'L0_attn_W2': _L0_attn_in['W2'], 'L0_xattn_Wq': _L0_xattn_in['Wq'], 'L0_xattn_Wk': _L0_xattn_in['Wk'], 'L0_xattn_Wv': _L0_xattn_in['Wv'], 'L0_xattn_Wo': _L0_xattn_in['Wo'], 'L0_xattn_lambda_param': _L0_xattn_in['lambda_param'], 'L0_xattn_ln1_g': _L0_xattn_in['ln1_g'], 'L0_xattn_ln1_b': _L0_xattn_in['ln1_b'], 'L0_xattn_ln2_g': _L0_xattn_in['ln2_g'], 'L0_xattn_ln2_b': _L0_xattn_in['ln2_b'], 'L0_xattn_ffn_w1': _L0_xattn_in['ffn_w1'], 'L0_xattn_ffn_b1': _L0_xattn_in['ffn_b1'], 'L0_xattn_ffn_w2': _L0_xattn_in['ffn_w2'], 'L0_xattn_ffn_b2': _L0_xattn_in['ffn_b2'], 'L0_ffn_scale': _L0_ffn_in['scale'], 'L0_ffn_centroids': _L0_ffn_in['centroids'], 'L0_ffn_up_w': _L0_ffn_in['up_w'], 'L0_ffn_down_w': _L0_ffn_in['down_w']}

def reference(x, ctx_1024, L0_attn_ln1_w, L0_attn_Wq, L0_attn_Wk, L0_attn_Wv, L0_attn_rel_bias, L0_attn_scale, L0_attn_Wo, L0_attn_ln2_w, L0_attn_W1, L0_attn_W2, L0_xattn_Wq, L0_xattn_Wk, L0_xattn_Wv, L0_xattn_Wo, L0_xattn_lambda_param, L0_xattn_ln1_g, L0_xattn_ln1_b, L0_xattn_ln2_g, L0_xattn_ln2_b, L0_xattn_ffn_w1, L0_xattn_ffn_b1, L0_xattn_ffn_w2, L0_xattn_ffn_b2, L0_ffn_scale, L0_ffn_centroids, L0_ffn_up_w, L0_ffn_down_w):
    import jax
    import jax.numpy as jnp

    def _L0_attn_ref(x, ln1_w, Wq, Wk, Wv, rel_bias, scale, Wo, ln2_w, W1, W2):
        import jax, jax.numpy as jnp
        import numpy as np
        import math
        EMBED = 256
        HEADS = 16
        HEAD_DIM = EMBED // HEADS
        HIDDEN = 1024
        NUM_BUCKETS = 32
        MAX_DISTANCE = 128
        LN_EPS = 1e-06
        KQ_EPS = 1e-06

        def _rms_norm(xs, weight):
            xf = xs.astype(jnp.float32)
            var = jnp.mean(jnp.square(xf), axis=-1, keepdims=True)
            ys = xs * jax.lax.rsqrt(var + LN_EPS) * weight
            return ys.astype(xs.dtype)

        def _normalize_kq(kq):
            ss = jnp.sum(jnp.square(kq), axis=-1, keepdims=True)
            return kq * jax.lax.rsqrt(ss + KQ_EPS)

        def _rel_position_bucket(rp):
            rp = -jnp.minimum(rp, 0)
            max_exact = NUM_BUCKETS // 2
            is_small = rp < max_exact
            safe = jnp.maximum(rp, 1).astype(jnp.float32)
            large = max_exact + (jnp.log(safe / max_exact) / math.log(MAX_DISTANCE / max_exact) * (NUM_BUCKETS - max_exact)).astype(jnp.int32)
            large = jnp.minimum(large, NUM_BUCKETS - 1)
            return jnp.where(is_small, rp, large)
        B, S, E = x.shape
        xn = _rms_norm(x, ln1_w)
        q = (xn @ Wq).reshape(B, S, HEADS, HEAD_DIM)
        k = (xn @ Wk).reshape(B, S, HEADS, HEAD_DIM)
        v = (xn @ Wv).reshape(B, S, HEADS, HEAD_DIM)
        q = _normalize_kq(q)
        k = _normalize_kq(k)
        pos = jnp.arange(S, dtype=jnp.int32)
        bucket = _rel_position_bucket(pos[None, :] - pos[:, None])
        bias = rel_bias[bucket]
        bias = jnp.transpose(bias, (2, 0, 1))[None]
        attn = jnp.einsum('bqhd,bkhd->bhqk', q, k) + bias
        attn = attn * scale[None, :, None, None]
        causal = pos[None, :] - pos[:, None] < 0
        attn = jnp.where(causal[None, None], attn, -1000000.0)
        attn = jax.nn.softmax(attn, axis=-1)
        y = jnp.einsum('bhqk,bkhd->bqhd', attn, v).reshape(B, S, E)
        y = y @ Wo + x
        z = _rms_norm(y, ln2_w)
        z = jax.nn.relu(z @ W1) @ W2
        return z + y

    def _L0_xattn_ref(query, key, value, Wq, Wk, Wv, Wo, lambda_param, ln1_g, ln1_b, ln2_g, ln2_b, ffn_w1, ffn_b1, ffn_w2, ffn_b2):
        import jax, jax.numpy as jnp
        import numpy as np
        import math
        D_MODEL = 256
        NUM_HEADS = 8
        D_HEAD = D_MODEL // NUM_HEADS
        D_FF = 4 * D_MODEL
        LN_EPS = 1e-05

        def _layer_norm(x, g, b):
            mu = jnp.mean(x, axis=-1, keepdims=True)
            var = jnp.mean((x - mu) ** 2, axis=-1, keepdims=True)
            return (x - mu) * jax.lax.rsqrt(var + LN_EPS) * g + b
        B, Sq, _ = query.shape
        Sk = key.shape[1]
        Q = (query @ Wq).reshape(B, Sq, NUM_HEADS, D_HEAD)
        K = (key @ Wk).reshape(B, Sk, NUM_HEADS, D_HEAD)
        V = (value @ Wv).reshape(B, Sk, NUM_HEADS, D_HEAD)
        scale = 1.0 / math.sqrt(D_HEAD)
        scores = jnp.einsum('bqhd,bkhd->bhqk', Q, K) * scale
        attn1 = jax.nn.softmax(scores, axis=-1)
        attn2 = jax.nn.softmax(scores - 1.0, axis=-1)
        lam = jax.nn.sigmoid(lambda_param)
        attn = attn1 - lam * attn2
        attn_out = jnp.einsum('bhqk,bkhd->bqhd', attn, V).reshape(B, Sq, D_MODEL)
        attn_out = attn_out @ Wo
        q_enh = _layer_norm(query + attn_out, ln1_g, ln1_b)
        ffn = jax.nn.relu(q_enh @ ffn_w1 + ffn_b1) @ ffn_w2 + ffn_b2
        return _layer_norm(q_enh + ffn, ln2_g, ln2_b)

    def _L0_ffn_ref(x, scale, centroids, up_w, down_w):
        import jax, jax.numpy as jnp
        import numpy as np
        EPS = 1e-06
        N_EXPERTS = 8

        def _rms_norm(x, scale, eps=EPS):
            mean_sq = jnp.mean(x.astype(jnp.float32) ** 2, axis=-1, keepdims=True)
            s = scale.astype(jnp.float32) * jax.lax.rsqrt(mean_sq + eps)
            return x * s.astype(x.dtype)

        def _dist2(x, y):
            nx = jnp.sum(x ** 2, axis=-1)[..., :, None]
            ny = jnp.sum(y ** 2, axis=-1)[..., None, :]
            return nx + ny - 2.0 * (x @ y.T)
        skip = x
        xn = _rms_norm(x, scale)
        ids = jnp.argmin(_dist2(xn, centroids), axis=-1)
        out = jnp.zeros_like(x)
        for e in range(N_EXPERTS):
            h = jnp.einsum('bsd,dh->bsh', xn, up_w[e])
            a, g = jnp.split(h, 2, axis=-1)
            y = jnp.einsum('bsh,hd->bsd', a * jax.nn.silu(g), down_w[e])
            out = jnp.where((ids == e)[..., None], y, out)
        return out + skip
    x = x + _L0_attn_ref(_layernorm(x, axis=-1), L0_attn_ln1_w, L0_attn_Wq, L0_attn_Wk, L0_attn_Wv, L0_attn_rel_bias, L0_attn_scale, L0_attn_Wo, L0_attn_ln2_w, L0_attn_W1, L0_attn_W2)
    x = x + _L0_xattn_ref(_layernorm(x, axis=-1), ctx_1024, ctx_1024, L0_xattn_Wq, L0_xattn_Wk, L0_xattn_Wv, L0_xattn_Wo, L0_xattn_lambda_param, L0_xattn_ln1_g, L0_xattn_ln1_b, L0_xattn_ln2_g, L0_xattn_ln2_b, L0_xattn_ffn_w1, L0_xattn_ffn_b1, L0_xattn_ffn_w2, L0_xattn_ffn_b2)
    x = x + _L0_ffn_ref(_layernorm(x, axis=-1), L0_ffn_scale, L0_ffn_centroids, L0_ffn_up_w, L0_ffn_down_w)
    return x

_drawn_inputs = setup_inputs


def setup_inputs(seed=0):
    import zlib

    import numpy as np

    out = dict(_drawn_inputs(seed))
    spreads = {'L0_attn_ln1_w': (1.0, 0.6),
     'L0_attn_scale': (1.0, 0.6),
     'L0_attn_ln2_w': (1.0, 0.577),
     'L0_xattn_ln1_g': (1.0, 0.2),
     'L0_xattn_ln1_b': (0.0, 0.1),
     'L0_xattn_ln2_g': (1.0, 0.2),
     'L0_xattn_ln2_b': (0.0, 0.1),
     'L0_xattn_ffn_b1': (0.0, 0.1),
     'L0_xattn_ffn_b2': (0.0, 0.1),
     'L0_ffn_scale': (1.0, 0.2)}
    factors = {'L0_attn_Wq': 7.077,
     'L0_attn_Wk': 7.762,
     'L0_attn_Wv': 3.378,
     'L0_attn_rel_bias': 8.0,
     'L0_attn_Wo': 3.962}
    for name, (base, spread) in spreads.items():
        noise = np.random.default_rng([zlib.crc32(name.encode()), seed]).standard_normal(out[name].shape)
        drawn = base * np.exp(spread * noise) if base else spread * noise
        out[name] = jnp.asarray(drawn.astype(out[name].dtype))
    for name, factor in factors.items():
        out[name] = (out[name] * factor).astype(out[name].dtype)
    return out
```

```python
from contextlib import ExitStack

import numpy as np

import concourse.bass as bass
import concourse.mybir as mybir

F32 = mybir.dt.float32
F32R = mybir.dt.float32r
F16 = mybir.dt.float16
BF16 = mybir.dt.bfloat16
I32 = mybir.dt.int32
U32 = mybir.dt.uint32
ALU = mybir.AluOpType
ACT = mybir.ActivationFunctionType
AX_X = mybir.AxisListType.X

P = 128
B, S, D = 16, 256, 256
T = S // P
C = D // P
H0, D0 = 16, 16
H1, D1 = 8, 32
HID = 1024
J = HID // P
E = 8
EH = 512
EJ = EH // P
BUCKETS = 32
NT = B * T
TILES_MAX = NT + E - 1
RW = 2 * D + 1
ROUTE_POS = 21
ROUTE_ALL = ROUTE_POS + 3
RING = 8

SCOLS = S + P

HEADS = []
for _h in range(H1):
    HEADS += [("A", 3 * _h + n) for n in range(3) if 3 * _h + n < H0] + [("B", _h)]

TR = ["A.xn", "B.x", "B.ctx", "C.xn", "A.q0", "A.k0", "A.q1", "A.k1", "B.max", "A.y", "B.y", "A.z", "B.q"]
SC = ["A.v", "B.k", "B.v", "B.q_"] + [f"B.m{n}" for n in range(8)] + [f"{st}.s{h}" for st, h in HEADS] \
    + [f"A.h{n}" for n in range(4)] + [f"B.h{n}" for n in range(4)]
MM = ["A.qk0", "A.qk1", "C.dist", "A.o0", "A.o1", "A.wo", "B.wo"]
AC = ["B.o0", "B.o1", "A.out", "B.out"]
UNSIGNALLED = ("A.o0", "A.o1", "B.o0", "B.o1")

BANKS, BANK_OF = {}, {}
for _g, _jobs in enumerate((TR, SC, MM, AC)):
    for _n, _job in enumerate(_jobs):
        BANK_OF[_job] = 2 * _g + _n % 2
        BANKS.setdefault(2 * _g + _n % 2, []).append(_job)
PHASES = [(0, 1, "A"), (1, 1, "AB"), (2, B - 2, "ABC"), (B, 1, "BC"), (B + 1, 1, "C")]


class Turn:

    def __init__(self, phase, k):
        self.first, self.count, self.stages = PHASES[phase]
        self.phase, self.k = phase, k

    def batch(self, stage):
        return self.k + (self.first - "ABC".index(stage))

    def _before(self, job, counted):
        bank = [j for j in BANKS[BANK_OF[job]] if counted(j)]
        before = sum(n * sum(j[0] in st for j in bank) for _, n, st in PHASES[:self.phase])
        mine = [j for j in bank if j[0] in self.stages]
        return self.k * len(mine) + (before + mine.index(job))

    def used(self, job):
        return self._before(job, lambda j: True)

    def signalled(self, job):
        return self._before(job, lambda j: j not in UNSIGNALLED)


def build(nc, d):
    ctx = ExitStack()
    with ctx:
        _build(nc, d, ctx)


def _build(nc, d, ctx):
    def sem(name):
        return ctx.enter_context(nc.semaphore(name))

    def sbuf(stack, name, shape, dt=F32):
        return stack.enter_context(nc.sbuf_tensor(name, shape, dt))

    LONE = (mybir.EngineType.Pool, mybir.EngineType.SP)
    s_passed = {e: sem(f"waits_passed_{n}") for n, e in enumerate(LONE + (mybir.EngineType.DVE,))}

    def wait(eng, s, value, lone=False):
        if isinstance(value, int):
            if value > 0:
                eng.wait_ge(s, value)
            return
        eng.wait_ge(s, value)
        if lone or eng.engine in LONE:
            eng.sem_inc(s_passed[eng.engine], 1)

    toep = nc.dram_tensor("toep", (H0, P, 4 * P), F32, kind="Internal")
    mrow = nc.dram_tensor("mrow", (H0, S), F32, kind="Internal")
    rows_lin = nc.dram_tensor("rows_lin", (B * S, RW), F32, kind="Internal")
    rows_srt = nc.dram_tensor("rows_srt", (TILES_MAX * P, RW), F32, kind="Internal")

    bank = [ctx.enter_context(nc.psum_tensor(f"bank{n}", [P, 512], F32)) for n in range(8)]
    bank_full = [sem(f"bank_full{n}") for n in range(8)]
    bank_free = [sem(f"bank_free{n}") for n in range(8)]

    def claim(pe, turn, job):
        wait(pe, bank_free[BANK_OF[job]], turn.used(job))
        return bank[BANK_OF[job]]

    def full(eng, turn, job):
        wait(eng, bank_full[BANK_OF[job]], turn.signalled(job) + 1)
        return bank[BANK_OF[job]]

    def taken(eng, turn, job, lone=False):
        wait(eng, bank_free[BANK_OF[job]], turn.used(job) + 1, lone)

    def f_sem(job):
        return bank_full[BANK_OF[job]]

    def e_sem(job):
        return bank_free[BANK_OF[job]]

    ident = sbuf(ctx, "ident", [P, P])
    ident16 = sbuf(ctx, "ident16", [P, P], F16)
    ones = sbuf(ctx, "ones", [P, P])
    ones_r = sbuf(ctx, "ones_r", [P, P], F32R)
    tri = sbuf(ctx, "tri", [P, P])
    first_col = sbuf(ctx, "first_col", [P, P])
    mhalf = sbuf(ctx, "mhalf", [P, 64])
    expert_of = sbuf(ctx, "expert_of", [P, NT])
    pos = sbuf(ctx, "pos", [P, NT], I32)
    tile_expert = sbuf(ctx, "tile_expert", [P, 64], I32)

    s_const = sem("const_made")
    s_setup_dma = sem("setup_loaded")
    s_w = sem("weights_scaled")
    s_zero = sem("scratch_cleared")

    p1 = ExitStack()
    w0qk = sbuf(p1, "w0qk", [P, C, 2 * D])
    w0v = sbuf(p1, "w0v", [P, C, D])
    w0o = sbuf(p1, "w0o", [P, C, D])
    w01 = sbuf(p1, "w01", [P, C, HID])
    w02 = sbuf(p1, "w02", [P, J, D])
    w1q = sbuf(p1, "w1q", [P, C, D])
    w1k = sbuf(p1, "w1k", [P, C, D])
    w1v = sbuf(p1, "w1v", [P, C, D])
    w1o = sbuf(p1, "w1o", [P, C, D])
    w11 = sbuf(p1, "w11", [P, C, HID])
    w12 = sbuf(p1, "w12", [P, J, D])
    b11 = sbuf(p1, "b11", [P, J])
    ln0 = sbuf(p1, "ln0", [P, 2, C])
    vecs = sbuf(p1, "vecs", [P, 6, D])
    G1, B1, G2, B2, FB2, FSC = range(6)
    eb = sbuf(p1, "eb", [P, H0, SCOLS])
    qscale = sbuf(p1, "qscale", [P, T, 2 * H0])
    cent = sbuf(p1, "cent", [E, D])
    cent_t = sbuf(p1, "cent_t", [P, C, E])
    cent_sq = sbuf(p1, "cent_sq", [P, C, E])
    cnorm = sbuf(p1, "cnorm", [P, E])
    lam = sbuf(p1, "lam", [P, 3])

    x_in = sbuf(p1, "x_in", [P, T, D])
    x_keep = sbuf(p1, "x_keep", [P, T, D])
    a_xl = sbuf(p1, "a_xl", [P, T, D])
    a_xn = sbuf(p1, "a_xn", [P, T, D])
    a_xnT = sbuf(p1, "a_xnT", [P, C, S])
    a_sq = sbuf(p1, "a_sq", [P, T, 2 * D])
    a_hat = sbuf(p1, "a_hat", [P, T, 2 * D])
    a_split = sbuf(p1, "a_split", [P, T, 2 * H0, 4, D0], F16)
    a_qT = sbuf(p1, "a_qT", [P, H0 // 2, S], F16)
    a_kT = sbuf(p1, "a_kT", [P, H0 // 2, S], F16)
    a_v = sbuf(p1, "a_v", [P, T, H0, D0 + 1])
    NPR = 3
    a_p = sbuf(p1, "a_p", [P, NPR, SCOLS])
    a_y = sbuf(p1, "a_y", [P, T, D])
    a_yT = sbuf(p1, "a_yT", [P, C, S])
    a_r = sbuf(p1, "a_r", [P, T, D])
    a_hT = sbuf(p1, "a_hT", [P, J, S])
    a_st = sbuf(p1, "a_st", [P, T, 6])
    a_mv = sbuf(p1, "a_mv", [P, T, 2])
    a_sc = sbuf(p1, "a_sc", [P, 8, T])
    a_ss = sbuf(p1, "a_ss", [P, T, 2 * H0])
    a_rn = sbuf(p1, "a_rn", [P, T, 2 * H0])
    a_rec = sbuf(p1, "a_rec", [P, T, H0])
    a_ms = sbuf(p1, "a_ms", [P, T])
    a_rz = sbuf(p1, "a_rz", [P, 2, T])
    junk = sbuf(p1, "junk", [P, 2 * T, D])
    x1 = sbuf(p1, "x1", [P, T, D])
    c_in = sbuf(p1, "c_in", [P, T, D])
    b_ctxT = sbuf(p1, "b_ctxT", [P, C, S])
    b_xl = sbuf(p1, "b_xl", [P, T, D])
    b_xT = sbuf(p1, "b_xT", [P, C, S])
    b_kT = sbuf(p1, "b_kT", [P, C, S])
    b_qT = sbuf(p1, "b_qT", [P, C, S])
    b_kTb = sbuf(p1, "b_kTb", [P, C, S], BF16)
    b_qTb = sbuf(p1, "b_qTb", [P, C, S], BF16)
    b_v = sbuf(p1, "b_v", [P, T, H1, D1 + 1])
    b_nm = sbuf(p1, "b_nm", [P, T, C, 4, 32])
    b_nmT = sbuf(p1, "b_nmT", [P, C, S], F32R)
    b_p = sbuf(p1, "b_p", [P, NPR, T, S])
    b_y = sbuf(p1, "b_y", [P, T, D])
    b_yT = sbuf(p1, "b_yT", [P, C, S])
    b_q = sbuf(p1, "b_q", [P, T, D])
    b_hT = sbuf(p1, "b_hT", [P, J, S])
    b_st = sbuf(p1, "b_st", [P, T, 6])
    b_mv = sbuf(p1, "b_mv", [P, T, 2])
    b_rs = sbuf(p1, "b_rs", [P, 2, T])
    b_mv2 = sbuf(p1, "b_mv2", [P, T, 2])
    b_rs2 = sbuf(p1, "b_rs2", [P, 2, T])
    b_rec = sbuf(p1, "b_rec", [P, T, H1])
    x1_keep = sbuf(p1, "x1_keep", [P, T, D])
    b_f = sbuf(p1, "b_f", [P, T, D])
    c_x2 = sbuf(p1, "c_x2", [P, T, D])
    c_n = sbuf(p1, "c_n", [P, T, D])
    c_rows = sbuf(p1, "c_rows", [P, T, 2 * D])
    zrow = sbuf(p1, "zrow", [P, RW])
    idcol = sbuf(p1, "idcol", [P, NT], I32)
    c_xnT = sbuf(p1, "c_xnT", [P, C, S])
    c_st = sbuf(p1, "c_st", [P, T, 6])
    c_mv = sbuf(p1, "c_mv", [P, T, 2])
    c_rs = sbuf(p1, "c_rs", [P, 2, T])
    c_mv2 = sbuf(p1, "c_mv2", [P, T, 2])
    c_sc = sbuf(p1, "c_sc", [P, 8, T])
    c_nx = sbuf(p1, "c_nx", [P, T])
    c_tmp = sbuf(p1, "c_tmp", [P, T, E])
    c_nd = sbuf(p1, "c_nd", [P, T, E])
    c_mx = sbuf(p1, "c_mx", [P, T, 8])
    c_ix = sbuf(p1, "c_ix", [P, T, 8], U32)
    bias_b = b_hT
    onehot = sbuf(p1, "onehot", [BUCKETS, S])
    relb = sbuf(p1, "relb", [BUCKETS, H0])
    sc16 = sbuf(p1, "sc16", [H0, 1])
    bd = sbuf(p1, "bd", [H0, 4 * P])
    bmax = sbuf(p1, "bmax", [H0, S])

    PER_BATCH = {
        "a_loaded": 16, "a_stats": T, "a_mv": T, "a_norms": 7, "a_xn": T, "a_xl": T, "a_kept": 1,
        "a_squares": T, "a_sumsq": T, "a_rn": 3 * T, "a_hi": 2 * T, "a_lo": 2 * T, "a_p": H0, "a_p_used": H0,
        "a_rec": T, "a_ms": T, "a_rz": 2, "a_xy": 1, "a_z": T,
        "b_loaded": 16, "b_stats": T, "b_mv": T, "b_norm": 2, "x1_kept": 1, "b_xl": T, "b_kb": 1, "b_qb": 1,
        "b_p_used": H1, "b_rec": T, "b_stats2": T, "b_mv2": T, "b_norm2": 2, "b_n": T, "b_gain": 1, "b_q": 1,
        "b_qb2": 1,
        "c_stats": T, "c_mv": T, "c_norm": 2, "c_n": T, "c_gain": 1, "c_out": 1, "c_x2": 1, "c_stats2": T,
        "c_mv2": T, "c_norms": 7, "c_xl": T, "c_xs": T, "c_rows": 2, "c_stored": 16, "c_nx": T, "c_tmp": T,
        "c_max8": T, "c_index": T, "c_expert": 1,
    }
    sig = {name: sem(name) for name in PER_BATCH}

    def after(eng, name, batch, n=None, lone=False):
        per = PER_BATCH[name]
        wait(eng, sig[name], batch * per + (per if n is None else n), lone)

    s_ids, s_toep, s_tp, s_bd, s_bmax, s_eb, s_cent, s_lam, s_pe_setup, s_sc = map(sem, (
        "ids_stored", "toeplitz_written", "toeplitz_read", "bias_by_distance", "bias_prefix_max", "eb_made",
        "centroid_norms", "lambda_chain", "pe_setup", "qscale_made"))

    def bc(ap, n):
        return ap.unsqueeze(len(ap.shape)).to_broadcast(list(ap.shape) + [n])

    def over_t(ap):
        return ap.unsqueeze(1).to_broadcast([P, T, D])

    def tok(t):
        return slice(t * P, (t + 1) * P)

    block = ctx.enter_context(nc.Block())
    ctx.enter_context(nc.allow_non_contiguous_dma(reason="a few vectors laid over partitions, once"))

    def w_view(ap):
        return ap.rearrange("(c p) n -> p c n", p=P)

    def on_all(ap):
        return ap.rearrange("(o n) -> o n", o=1).to_broadcast([P, ap.shape[0]])

    setup_loads = [
        (w0qk[:, :, 0:D], w_view(d["L0_attn_Wq"])), (w0qk[:, :, D:], w_view(d["L0_attn_Wk"])),
        (ln0[:, 0, :], d["L0_attn_ln1_w"].rearrange("(c p) -> p c", p=P)),
        (ln0[:, 1, :], d["L0_attn_ln2_w"].rearrange("(c p) -> p c", p=P)),
        (onehot[:], d["bucket_onehot"]), (relb[:], d["L0_attn_rel_bias"]),
        (sc16[:], d["L0_attn_scale"].rearrange("(h o) -> h o", o=1)),
        (lam[:, 0:1], d["L0_xattn_lambda_param"].to_broadcast([P, 1])),
        (cent[:], d["L0_ffn_centroids"]),
        (w0v[:], w_view(d["L0_attn_Wv"])), (w0o[:], w_view(d["L0_attn_Wo"])),
        (w01[:], w_view(d["L0_attn_W1"])), (w02[:], w_view(d["L0_attn_W2"])),
        (w1q[:], w_view(d["L0_xattn_Wq"])), (w1k[:], w_view(d["L0_xattn_Wk"])),
        (w1v[:], w_view(d["L0_xattn_Wv"])), (w1o[:], w_view(d["L0_xattn_Wo"])),
        (w11[:], w_view(d["L0_xattn_ffn_w1"])), (w12[:], w_view(d["L0_xattn_ffn_w2"])),
        (b11[:], d["L0_xattn_ffn_b1"].rearrange("(j p) -> p j", p=P)),
    ]
    setup_loads += [(vecs[:, n, :], on_all(d[name])) for n, name in enumerate((
        "L0_xattn_ln1_g", "L0_xattn_ln1_b", "L0_xattn_ln2_g", "L0_xattn_ln2_b", "L0_xattn_ffn_b2", "L0_ffn_scale"))]
    setup_loads += [(qscale[:, t, 0:H0], on_all(d["L0_attn_scale"])) for t in range(T)]
    ALL_LOADED = 16 * len(setup_loads)
    CONSTS = 15

    x_tiles = d["x"].rearrange("b (t p) n -> b p t n", p=P)
    ctx_tiles = d["ctx_1024"].rearrange("b (t p) n -> b p t n", p=P)
    lin_tiles = rows_lin.ap().rearrange("(b t p) n -> b p t n", p=P, t=T)

    def of_batch(tiles, b):
        one = tiles[b:b + 1] if isinstance(b, int) else tiles[bass.ds(b, 1)]
        return one.rearrange("o p t n -> (o p) t n")

    def each(eng, body):
        for phase, (_, count, _) in enumerate(PHASES):
            if count == 1:
                body(Turn(phase, 0))
            else:
                with eng.Fori(0, count) as k:
                    body(Turn(phase, k))

    s_route, s_pp, s_wmoe = map(sem, ("routing_chain", "prefixes_made", "experts_loaded"))
    rows_back = [sem(f"rows_back{n}") for n in range(RING)]
    rows_placed = [sem(f"rows_placed{n}") for n in range(RING)]

    p1.close()
    up = sbuf(ctx, "up", [P, E, C, 2 * EH])
    down = sbuf(ctx, "down", [P, E, EJ, D])
    ring = sbuf(ctx, "ring", [P, RING, RW])
    m_in = sbuf(ctx, "m_in", [P, 2, D])
    m_skip = sbuf(ctx, "m_skip", [P, 2, D + 1])
    m_xT = sbuf(ctx, "m_xT", [P, 2, C, P])
    m_sg = sbuf(ctx, "m_sg", [P, 2, EH])
    m_h = sbuf(ctx, "m_h", [P, 2, EH])
    m_hT = sbuf(ctx, "m_hT", [P, 2, EJ, P])
    m_out = sbuf(ctx, "m_out", [P, 2, D])
    oh = sbuf(ctx, "oh", [P, NT, E])
    r_pp = sbuf(ctx, "r_pp", [P, NT, E])
    r_tot = sbuf(ctx, "r_tot", [P, NT, E])
    r_cum = sbuf(ctx, "r_cum", [P, NT, E])
    r_a = sbuf(ctx, "r_a", [P, NT, E])
    r_cmp = sbuf(ctx, "r_cmp", [P, E, NT])
    r_nt = sbuf(ctx, "r_nt", [P, E])
    r_ct = sbuf(ctx, "r_ct", [P, E])
    r_base = sbuf(ctx, "r_base", [P, E])
    r_cmp2 = sbuf(ctx, "r_cmp2", [P, TILES_MAX, E])
    r_te = sbuf(ctx, "r_te", [P, TILES_MAX])
    r_posf = sbuf(ctx, "r_posf", [P, NT])
    io_e = sbuf(ctx, "io_e", [P, E])
    io_t = sbuf(ctx, "io_t", [P, NT])
    io_i = sbuf(ctx, "io_i", [P, TILES_MAX])
    ones_nt = sbuf(ctx, "ones_nt", [P, NT])
    s_iota = sem("iotas_made")
    BY_TILE = {"m_loaded": 16, "m_skip": 16, "m_x": 1, "m_xT": 1, "m_up": 1, "m_silu": 1, "m_h": 1, "m_ht": 1, "m_hT": 1,
               "m_down": 1, "m_out": 1, "m_stored": 16}
    mig = [{name: sem(f"{name}{u}") for name in BY_TILE} for u in range(2)]

    def after_tile(eng, name, k, u, n=1):
        wait(eng, mig[u][name], (k + n) * BY_TILE[name])

    def phase1_over(eng):
        after(eng, "c_expert", B - 1)
        after(eng, "c_rows", B - 1)
        after(eng, "c_stored", B - 1)

    PAIRS = (TILES_MAX - 1) // 2

    def tile_steps(eng, body):
        body(0, 2, 2)
        with eng.Fori(0, PAIRS - 2) as k:
            body(k + 1, 2, 2)
        body(PAIRS - 1, 2, TILES_MAX - 2 * PAIRS)
        if TILES_MAX > 2 * PAIRS:
            body(PAIRS, 1, 0)

    @block.sync
    def _(sp):
        sp.dma_start(x_in[:], of_batch(x_tiles, 0)).then_inc(sig["a_loaded"], 16)
        for dst, src in setup_loads:
            sp.dma_start(dst, src).then_inc(s_setup_dma, 16)
        sp.wait_ge(s_bd, 2)
        sp.dma_start(toep.ap(), bd[:].unsqueeze(1).to_broadcast([H0, P, 4 * P])).then_inc(s_toep, 16)
        sp.wait_ge(s_bmax, 2)
        sp.dma_start(mrow.ap(), bmax[:]).then_inc(s_toep, 16)
        sp.wait_ge(s_toep, 32)
        for cols in (slice(0, S), slice(S, SCOLS)):
            shifted = bass.AP(tensor=toep, offset=P, 
                              ap=[[4 * P - 1, P], [4 * P * P, H0], [1, cols.stop - cols.start]])
            sp.dma_start(eb[:, :, cols], shifted).then_inc(s_tp, 16)
        maxima = mrow.ap().rearrange("(o h) q -> o h q", o=1)
        for half in range(2):
            if half == 1:
                sp.wait_ge(s_eb, 2)
            sp.dma_start(bias_b[:], maxima[:, half * 8:(half + 1) * 8, :].to_broadcast([P, 8, S])).then_inc(s_tp, 16)
        sp.wait_ge(s_const, CONSTS)
        sp.dma_start(rows_srt.ap().rearrange("(n p) w -> p n w", p=P),
                     zrow[:].unsqueeze(1).to_broadcast([P, TILES_MAX, RW])).then_inc(s_zero, 16)
        sp.dma_start(rows_lin.ap().rearrange("(n p) w -> p n w", p=P)[:, :, 2 * D:],
                     idcol[:].bitcast(F32).unsqueeze(2)).then_inc(s_ids, 16)

        def turn(it):
            if "A" in it.stages and it.first > 0:
                b = it.batch("A")
                after(sp, "a_xn", b - 1)
                after(sp, "a_xl", b - 1)
                after(sp, "a_kept", b - 1)
                sp.dma_start(x_in[:], of_batch(x_tiles, b)).then_inc(sig["a_loaded"], 16)
            if "B" in it.stages:
                b = it.batch("B")
                if it.phase > 1:
                    after(sp, "b_p_used", b - 1)
                sp.dma_start(c_in[:], of_batch(ctx_tiles, b)).then_inc(sig["b_loaded"], 16)
            if "C" in it.stages:
                b = it.batch("C")
                after(sp, "c_rows", b)
                sp.dma_start(of_batch(lin_tiles, b)[:, :, 0:2 * D], c_rows[:]).then_inc(sig["c_stored"], 16)

        each(sp, turn)

        phase1_over(sp)
        for e in range(E):
            sp.dma_start(up[:, e], w_view(d["L0_ffn_up_w"][e])).then_inc(s_wmoe, 16)
            sp.dma_start(down[:, e], w_view(d["L0_ffn_down_w"][e])).then_inc(s_wmoe, 16)

        def load_tile(dst, cols, name, k, u):
            tile = rows_srt.ap().rearrange("(n p) w -> n p w", p=P)
            i = 2 * k + u
            one = tile[i:i + 1] if isinstance(i, int) else tile[bass.ds(i, 1)]
            sp.dma_start(dst[:, u], one.rearrange("o p w -> (o p) w")[:, cols]).then_inc(mig[u][name], 16)

        def load_pair(k, n):
            for u in range(n):
                after_tile(sp, "m_x", k, u, 0)
                load_tile(m_in, slice(0, D), "m_loaded", k, u)
            for u in range(n):
                after_tile(sp, "m_stored", k, u, 0)
                load_tile(m_skip, slice(D, RW), "m_skip", k, u)

        for slot in range(RING):
            sp.wait_ge(rows_placed[slot], 16 * (NT // RING))
        load_pair(0, 2)

        def step(k, n, nxt):
            load_pair(k + 1, nxt)

        tile_steps(sp, step)

    @block.scalar
    def _(act):
        copy = nc.scalar.copy

        def load_rows_back():
            phase1_over(act)
            act.wait_ge(s_ids, 16)
            tiles = rows_lin.ap().rearrange("(n p) w -> n p w", p=P)
            for n in range(NT):
                if n >= RING:
                    act.wait_ge(rows_placed[n % RING], 16 * (n // RING))
                act.dma_start(ring[:, n % RING], tiles[n]).then_inc(rows_back[n % RING], 16)

        act.wait_ge(s_setup_dma, ALL_LOADED)
        nc.scalar.activation(lam[:, 1:2], lam[:, 0:1], ACT.Exp, scale=-1.0).then_inc(s_lam, 1)
        act.wait_ge(s_eb, 4)
        nc.scalar.activation(eb[:].rearrange("p h n -> p (h n)"), eb[:].rearrange("p h n -> p (h n)"),
                             ACT.Exp).then_inc(s_eb, 1)

        def evacuate(it, job, dst, view=None):
            src = full(act, it, job)[:]
            copy(dst, src if view is None else view(src)).then_inc(e_sem(job), 1)

        def turn(it):
            A, Bb, Cc = (st in it.stages for st in "ABC")
            a, b, c = (it.batch(st) for st in "ABC")
            if A:
                evacuate(it, "A.xn", a_xnT[:].rearrange("p c s -> p (c s)"))
            if Bb:
                evacuate(it, "B.x", b_xT[:].rearrange("p c s -> p (c s)"))
                evacuate(it, "B.ctx", b_ctxT[:].rearrange("p c s -> p (c s)"))
            if A:
                for t in range(T):
                    ps = full(act, it, f"A.qk{t}")
                    nc.scalar.activation(a_sq[:, t], ps[:], ACT.Square).then_inc(sig["a_squares"], 1)
                evacuate(it, "A.v", a_v[:, :, :, 0:D0].rearrange("p t h d -> p (t h) d"),
                         lambda x: x.rearrange("p (n d) -> p n d", d=D0))
            if Bb:
                evacuate(it, "B.k", b_kT[:].rearrange("p c s -> p (c s)"))
                evacuate(it, "B.v", b_v[:, :, :, 0:D1].rearrange("p t h d -> p (t h) d"),
                         lambda x: x.rearrange("p (n d) -> p n d", d=D1))
                evacuate(it, "B.q_", b_qT[:].rearrange("p c s -> p (c s)"))
            if A:
                for t in range(T):
                    taken(act, it, f"A.qk{t}")
                    hat = a_hat[:, t].rearrange("p (h o d) -> p h o d", o=1, d=D0)
                    for lo, hi, slots in ((0, H0, slice(0, 4, 2)), (H0, 2 * H0, slice(0, 2))):
                        copy(a_split[:, t, lo:hi, slots, :],
                             hat[:, lo:hi].to_broadcast([P, H0, 2, D0])).then_inc(sig["a_hi"], 1)
            if Cc:
                after(act, "c_rows", c, 1)
                for t in range(T):
                    nc.scalar.activation(junk[:, T + t], c_rows[:, t, 0:D], ACT.Square,
                                         accum_out=c_nx[:, t:t + 1]).then_inc(sig["c_nx"], 1)
                evacuate(it, "C.xn", c_xnT[:].rearrange("p c s -> p (c s)"))
            if A:
                for t in range(T):
                    evacuate(it, f"A.k{t}", a_kT[:, :, tok(t)],
                             lambda x: x.bitcast(F16).rearrange("p (g s) -> p g s", s=P))
            if Bb:
                evacuate(it, "B.max", b_nmT[:].rearrange("p c s -> p (c s)"))
            for st, h in HEADS:
                if st == "A" and A:
                    ps = full(act, it, f"A.s{h}")
                    after(act, "a_p_used", a, h + 1 - NPR)
                    nc.scalar.activation(a_p[:, h % NPR], ps[:, 0:SCOLS], ACT.Exp).then_inc(e_sem(f"A.s{h}"), 1)
                if st == "B" and Bb:
                    ps = full(act, it, f"B.s{h}")
                    after(act, "b_p_used", b, h + 1 - NPR)
                    nc.scalar.activation(b_p[:, h % NPR].rearrange("p t s -> p (t s)"), ps[:],
                                         ACT.Exp).then_inc(e_sem(f"B.s{h}"), 1)
                if (st, h) == ("B", H1 - 2) and A:
                    evacuate(it, "A.y", a_yT[:].rearrange("p c s -> p (c s)"))
            if A:
                taken(act, it, "A.wo")
                for t in range(T):
                    nc.scalar.activation(junk[:, t], a_r[:, t], ACT.Square,
                                         accum_out=a_ms[:, t:t + 1]).then_inc(sig["a_ms"], 1)
            if Bb:
                evacuate(it, "B.y", b_yT[:].rearrange("p c s -> p (c s)"))
            if A:
                evacuate(it, "A.z", a_xnT[:].rearrange("p c s -> p (c s)"))
                for n in range(4):
                    ps = full(act, it, f"A.h{n}")
                    nc.scalar.activation(a_hT[:, 2 * n:2 * n + 2].rearrange("p j s -> p (j s)"), ps[:],
                                         ACT.Relu).then_inc(e_sem(f"A.h{n}"), 1)
            if Bb:
                evacuate(it, "B.q", b_xT[:].rearrange("p c s -> p (c s)"))
                for n in range(4):
                    ps = full(act, it, f"B.h{n}")
                    nc.scalar.activation(b_hT[:, 2 * n], ps[:, 0:S], ACT.Relu, bias=b11[:, 2 * n:2 * n + 1])
                    nc.scalar.activation(b_hT[:, 2 * n + 1], ps[:, S:], ACT.Relu,
                                         bias=b11[:, 2 * n + 1:2 * n + 2]).then_inc(e_sem(f"B.h{n}"), 1)

        each(act, turn)
        load_rows_back()

        def transposed(k, u):
            after_tile(act, "m_x", k, u)
            copy(m_xT[:, u].rearrange("p c s -> p (c s)"), bank[u][:, 0:C * P]).then_inc(mig[u]["m_xT"], 1)

        def step(k, n, nxt):
            for u in range(n):
                after_tile(act, "m_up", k, u)
                nc.scalar.activation(m_sg[:, u], bank[3 + 2 * u][:], ACT.Silu).then_inc(mig[u]["m_silu"], 1)
            for u in range(nxt):
                transposed(k + 1, u)
            for u in range(n):
                after_tile(act, "m_ht", k, u)
                copy(m_hT[:, u].rearrange("p j s -> p (j s)"), bank[6][:]).then_inc(mig[u]["m_hT"], 1)

        transposed(0, 0)
        transposed(0, 1)
        tile_steps(act, step)

    @block.gpsimd
    def _(pool):
        done = [0]

        def const(ins):
            ins.then_inc(s_const, 1)
            done[0] += 1

        const(pool.memset(ident[:], 0.0))
        const(pool.memset(ident16[:], 0.0))
        const(pool.memset(ones[:], 1.0))
        const(pool.memset(first_col[:], 0.0))
        pool.wait_ge(s_const, 4)
        for m in (ident, ident16):
            const(pool.affine_select(out=m[:], in_=m[:], compare_op=ALU.not_equal, fill=1.0, base=0,
                                     pattern=[[-1, P]], channel_multiplier=1))
        const(pool.affine_select(out=tri[:], in_=ones[:], compare_op=ALU.is_gt, fill=0.0, base=0,
                                 pattern=[[1, P]], channel_multiplier=-1))
        const(pool.memset(first_col[:, 0:1], 1.0))
        const(pool.tensor_copy(ones_r[:], ones[:]))
        const(pool.memset(mhalf[:], -0.5))
        const(pool.memset(a_v[:, :, :, D0:], 1.0))
        const(pool.memset(b_v[:, :, :, D1:], 1.0))
        const(pool.memset(b_nm[:], 0.0))
        const(pool.memset(zrow[:, 0:2 * D], 0.0))
        const(pool.iota(idcol[:], pattern=[[P, NT]], base=0, channel_multiplier=1))
        assert done[0] == CONSTS
        pool.wait_ge(s_eb, 5)
        pool.affine_select(out=eb[:, :, 0:S], in_=eb[:, :, 0:S], compare_op=ALU.is_gt, fill=0.0, base=0,
                           pattern=[[0, H0], [1, S]], channel_multiplier=-1).then_inc(s_eb, 1)
        pool.affine_select(out=eb[:, :, S:], in_=eb[:, :, S:], compare_op=ALU.is_gt, fill=0.0, base=0,
                           pattern=[[0, H0], [1, P]], channel_multiplier=-1).then_inc(s_eb, 1)
        pool.wait_ge(s_eb, 7)
        pool.memset(eb[:, :, 0:1], 1.0).then_inc(s_eb, 1)

        def power(out, in_, name):
            pool.tensor_tensor(out, in_, mhalf[:, 0:out.shape[-1]], ALU.pow).then_inc(sig[name], 1)

        def layer_then_rms(mv, sc, name, batch, eps):
            var = mv[:, :, 1]
            pool.tensor_scalar(sc[:, 0], var, eps, None, ALU.add).then_inc(sig[name], 1)
            after(pool, name, batch, 1)
            power(sc[:, 1], sc[:, 0], name)
            after(pool, name, batch, 2)
            pool.tensor_tensor(sc[:, 2], var, sc[:, 1], ALU.mult).then_inc(sig[name], 1)
            after(pool, name, batch, 3)
            pool.tensor_tensor(sc[:, 3], sc[:, 2], sc[:, 1], ALU.mult).then_inc(sig[name], 1)
            after(pool, name, batch, 4)
            pool.tensor_scalar(sc[:, 4], sc[:, 3], 1e-6, None, ALU.add).then_inc(sig[name], 1)
            after(pool, name, batch, 5)
            power(sc[:, 5], sc[:, 4], name)
            after(pool, name, batch, 6)
            pool.tensor_tensor(sc[:, 6], sc[:, 5], sc[:, 1], ALU.mult).then_inc(sig[name], 1)

        def layer(mv, rs, name, batch, eps):
            pool.tensor_scalar(rs[:, 0], mv[:, :, 1], eps, None, ALU.add).then_inc(sig[name], 1)
            after(pool, name, batch, 1)
            power(rs[:, 1], rs[:, 0], name)

        def turn(it):
            A, Bb, Cc = (st in it.stages for st in "ABC")
            a, b, c = (it.batch(st) for st in "ABC")
            if A:
                after(pool, "a_mv", a)
                layer_then_rms(a_mv, a_sc, "a_norms", a, 1e-5)
            if Cc:
                after(pool, "c_mv", c)
                layer(c_mv, c_rs, "c_norm", c, 1e-5)
                after(pool, "c_n", c)
                pool.tensor_tensor(c_n[:], c_n[:], over_t(vecs[:, G2]), ALU.mult).then_inc(sig["c_gain"], 1)
                after(pool, "c_gain", c)
                pool.tensor_tensor(c_n[:], c_n[:], over_t(vecs[:, B2]), ALU.add).then_inc(sig["c_out"], 1)
                after(pool, "c_out", c)
                pool.tensor_tensor(c_x2[:], x1_keep[:], c_n[:], ALU.add).then_inc(sig["c_x2"], 1)
            if Bb:
                after(pool, "b_stats", b)
                if Cc:
                    after(pool, "c_x2", c)
                pool.tensor_copy(x1_keep[:], x1[:]).then_inc(sig["x1_kept"], 1)
            if A:
                after(pool, "a_xn", a)
                pool.tensor_copy(x_keep[:], x_in[:]).then_inc(sig["a_kept"], 1)
            if Cc:
                after(pool, "c_mv2", c)
                layer_then_rms(c_mv2, c_sc, "c_norms", c, 1e-5)
            if Bb:
                taken(pool, it, "B.k")
                pool.tensor_copy(b_kTb[:], b_kT[:]).then_inc(sig["b_kb"], 1)
            if A:
                for t in range(T):
                    after(pool, "a_sumsq", a, t + 1)
                    rn = a_rn[:, t]
                    pool.tensor_scalar(rn, a_ss[:, t], 1e-6, None, ALU.add).then_inc(sig["a_rn"], 1)
                    after(pool, "a_rn", a, 3 * t + 1)
                    power(rn, rn, "a_rn")
                    after(pool, "a_rn", a, 3 * t + 2)
                    pool.tensor_tensor(rn, rn, qscale[:, t], ALU.mult).then_inc(sig["a_rn"], 1)
            if Bb:
                taken(pool, it, "B.q_")
                pool.tensor_copy(b_qTb[:], b_qT[:]).then_inc(sig["b_qb"], 1)
            if Cc:
                after(pool, "c_xs", c)
                pool.tensor_tensor(c_rows[:, :, 0:D], c_rows[:, :, 0:D], over_t(vecs[:, FSC]),
                                   ALU.mult).then_inc(sig["c_rows"], 1)
                after(pool, "c_xl", c)
                pool.tensor_tensor(c_rows[:, :, D:], c_x2[:], c_n[:], ALU.add).then_inc(sig["c_rows"], 1)
            if A:
                for t in range(T):
                    after(pool, "a_hi", a, 2 * t + 2)
                    hat = a_hat[:, t].rearrange("p (h d) -> p h d", d=D0)
                    for lo, hi, high, slots in ((0, H0, 0, (1, 3)), (H0, 2 * H0, 0, (2, 3))):
                        for n, slot in enumerate(slots):
                            ins = pool.tensor_tensor(a_split[:, t, lo:hi, slot, :], hat[:, lo:hi],
                                                     a_split[:, t, lo:hi, high, :], ALU.subtract)
                            if n == 1:
                                ins.then_inc(sig["a_lo"], 1)
                after(pool, "a_ms", a)
                pool.tensor_scalar(a_rz[:, 0], a_ms[:], 1.0 / D, 1e-6, ALU.mult, ALU.add).then_inc(sig["a_rz"], 1)
                after(pool, "a_rz", a, 1)
                power(a_rz[:, 1], a_rz[:, 0], "a_rz")
                taken(pool, it, "A.wo")
                after(pool, "a_kept", a)
                pool.tensor_tensor(x_keep[:], x_keep[:], a_r[:], ALU.add).then_inc(sig["a_xy"], 1)
            if Bb:
                after(pool, "b_mv2", b)
                layer(b_mv2, b_rs2, "b_norm2", b, 1e-5)
                after(pool, "b_n", b)
                pool.tensor_tensor(b_q[:], b_q[:], over_t(vecs[:, G1]), ALU.mult).then_inc(sig["b_gain"], 1)
                after(pool, "b_gain", b)
                pool.tensor_tensor(b_q[:], b_q[:], over_t(vecs[:, B1]), ALU.add).then_inc(sig["b_q"], 1)
                after(pool, "b_q", b)
                taken(pool, it, "B.q")
                pool.tensor_tensor(b_q[:], b_q[:], over_t(vecs[:, FB2]), ALU.add).then_inc(sig["b_qb2"], 1)
            if A:
                after(pool, "b_mv", a)
                layer(b_mv, b_rs, "b_norm", a, 1e-5)

        pool.wait_ge(s_setup_dma, ALL_LOADED)
        pool.wait_ge(s_sc, 2)
        each(pool, turn)

        phase1_over(pool)
        pool.iota(io_e[:], pattern=[[1, E]], base=0, channel_multiplier=0,
                  allow_small_or_imprecise_dtypes=True).then_inc(s_iota, 1)
        pool.iota(io_t[:], pattern=[[P, NT]], base=0, channel_multiplier=0,
                  allow_small_or_imprecise_dtypes=True).then_inc(s_iota, 1)
        pool.iota(io_i[:], pattern=[[1, TILES_MAX]], base=0, channel_multiplier=0,
                  allow_small_or_imprecise_dtypes=True).then_inc(s_iota, 1)
        pool.memset(ones_nt[:], 1.0).then_inc(s_iota, 1)
        pool.wait_ge(s_zero, 16)
        pool.wait_ge(s_route, ROUTE_POS)
        for n in range(NT):
            pool.wait_ge(rows_back[n % RING], 16 * (n // RING + 1))
            pool.indirect_dma_start(out=rows_srt.ap(), out_offset=bass.IndirectOffsetOnAxis(ap=pos[:, n:n + 1], axis=0),
                                    in_=ring[:, n % RING], in_offset=None).then_inc(rows_placed[n % RING], 16)

        def step(k, n, nxt):
            for u in range(n):
                after_tile(pool, "m_out", k, u)
                pool.indirect_dma_start(
                    out=d["out"], out_offset=bass.IndirectOffsetOnAxis(ap=m_skip[:, u, D:].bitcast(U32), axis=0),
                    in_=m_out[:, u], in_offset=None, bounds_check=B * S - 1, oob_is_err=False,
                ).then_inc(mig[u]["m_stored"], 16)

        tile_steps(pool, step)
        for u in range(2):
            pool.wait_ge(mig[u]["m_stored"], 16 * ((TILES_MAX + 1 - u) // 2))

    @block.vector
    def _(dve):
        tt, ts = dve.tensor_tensor, dve.tensor_scalar

        dve.memset(bd[:], 0.0).then_inc(s_bd, 1)
        dve.memset(zrow[:, 2 * D:].bitcast(I32), B * S).then_inc(s_sc, 1)
        dve.wait_ge(s_setup_dma, ALL_LOADED)
        dve.wait_ge(s_bd, 1)
        dve.wait_ge(s_pe_setup, 1)
        ts(bd[:, P:P + S], bank[0][0:H0, 0:S], sc16[:, 0:1], None, ALU.mult).then_inc(s_bd, 1)
        dve.wait_ge(s_bd, 2)
        dve.tensor_tensor_scan(bmax[:, 1:S], bd[:, P + 1:P + S], bd[:, P + 1:P + S], -3.0e38, ALU.max,
                               ALU.max).then_inc(s_bmax, 1)
        dve.tensor_copy(bmax[:, 0:1], bd[:, P + 1:P + 2]).then_inc(s_bmax, 1)
        for c in range(C):
            for w, n in ((w0qk, 0), (w0v, 0), (w01, 1)):
                ts(w[:, c], w[:, c], ln0[:, n, c:c + 1], None, ALU.mult).then_inc(s_w, 1)
        ts(w1q[:], w1q[:], float(D1) ** -0.5, None, ALU.mult).then_inc(s_w, 1)
        dve.memset(qscale[:, :, H0:], 1.0).then_inc(s_sc, 1)
        dve.memset(qscale[0:1, 0, 0:H0], 0.0).then_inc(s_sc, 1)
        dve.wait_ge(s_lam, 1)
        ts(lam[:, 1:2], lam[:, 1:2], 1.0, None, ALU.add).then_inc(s_lam, 1)
        dve.wait_ge(s_lam, 2)
        dve.reciprocal(lam[:, 2:3], lam[:, 1:2]).then_inc(s_lam, 1)
        dve.wait_ge(s_lam, 3)
        ts(lam[:, 0:1], lam[:, 2:3], -1.0, 1.0, ALU.mult, ALU.add).then_inc(s_lam, 1)
        dve.wait_ge(s_lam, 4)
        ts(w1o[:], w1o[:], lam[:, 0:1], None, ALU.mult).then_inc(s_w, 1)
        dve.wait_ge(s_pe_setup, 2)
        ts(cent_t[:].rearrange("p c e -> p (c e)"), bank[1][:, 0:C * E], 2.0, None, ALU.mult).then_inc(s_cent, 1)
        dve.wait_ge(s_cent, 1)
        tt(cent_sq[:], cent_t[:], cent_t[:], ALU.mult).then_inc(s_cent, 1)
        dve.wait_ge(s_pe_setup, 3)
        ts(cnorm[:], bank[2][:, 0:E], 0.25, None, ALU.mult).then_inc(s_cent, 1)
        for half in range(2):
            dve.wait_ge(s_tp, 16 * (3 + half))
            heads = slice(8 * half, 8 * half + 8)
            tt(eb[:, heads, 0:S], eb[:, heads, 0:S], bias_b[:], ALU.subtract).then_inc(s_eb, 1)
            tt(eb[:, heads, S:], eb[:, heads, S:], bias_b[:, :, P:], ALU.subtract).then_inc(s_eb, 1)
        dve.wait_ge(s_cent, 3)

        def stats(x, st, mv, s_stats, s_mv, batch):
            for t in range(T):
                dve.bn_stats(st[:, t], x[:, t]).then_inc(sig[s_stats], 1)
            for t in range(T):
                after(dve, s_stats, batch, t + 1, lone=True)
                dve.bn_aggr(mv[:, t], st[:, t]).then_inc(sig[s_mv], 1)

        def shifted(out, x, mv, scale, name):
            for t in range(T):
                ts(out[:, t], x[:, t], mv[:, t, 0:1], scale[:, t:t + 1], ALU.subtract,
                   ALU.mult).then_inc(sig[name], 1)

        def normalised(it, st, n, rec, y, H, W, batch, name):
            for t in range(T):
                ps = bank[BANK_OF[f"{st}.o{t}"]]
                o = ps[:, 0:H * (W + 1)].rearrange("p (h d) -> p h d", d=W + 1)
                dve.reciprocal(rec[:, t], o[:, :, W]).then_inc(sig[name], 1)
                after(dve, name, batch, t + 1)
                tt(y[:, t].rearrange("p (h d) -> p h d", d=W), o[:, :, 0:W], bc(rec[:, t], W),
                   ALU.mult).then_inc(e_sem(f"{st}.o{t}"), 1)

        def turn(it):
            A, Bb, Cc = (st in it.stages for st in "ABC")
            a, b, c = (it.batch(st) for st in "ABC")
            if Bb:
                after(dve, "b_norm", b)
                shifted(b_xl, x1, b_mv, b_rs[:, 1], "b_xl")
            if A:
                after(dve, "a_loaded", a)
                stats(x_in, a_st, a_mv, "a_stats", "a_mv", a)
            if Cc:
                after(dve, "c_norm", c)
                shifted(c_n, b_f, c_mv, c_rs[:, 1], "c_n")
            if A:
                after(dve, "a_norms", a)
                shifted(a_xn, x_in, a_mv, a_sc[:, 6], "a_xn")
                shifted(a_xl, x_in, a_mv, a_sc[:, 1], "a_xl")
            if Cc:
                after(dve, "c_x2", c)
                stats(c_x2, c_st, c_mv2, "c_stats2", "c_mv2", c)
            if A:
                for t in range(T):
                    after(dve, "a_squares", a, t + 1)
                    dve.tensor_reduce(a_ss[:, t], a_sq[:, t].rearrange("p (h d) -> p h d", d=D0), AX_X,
                                      ALU.add).then_inc(sig["a_sumsq"], 1)
            if Cc:
                after(dve, "c_norms", c)
                after(dve, "c_stored", c - 1)
                shifted(c_rows[:, :, 0:D], c_x2, c_mv2, c_sc[:, 6], "c_xs")
                shifted(c_n, c_x2, c_mv2, c_sc[:, 1], "c_xl")
            if A:
                for t in range(T):
                    after(dve, "a_rn", a, 3 * t + 3)
                    ps = bank[BANK_OF[f"A.qk{t}"]]
                    tt(a_hat[:, t].rearrange("p (h d) -> p h d", d=D0), ps[:].rearrange("p (h d) -> p h d", d=D0),
                       bc(a_rn[:, t], D0), ALU.mult).then_inc(e_sem(f"A.qk{t}"), 1)
            if Bb:
                for n in range(8):
                    ps = full(dve, it, f"B.m{n}")
                    t, j = n // 4, n % 4
                    dve.tensor_reduce(b_nm[:, t, :, j, 0:1], ps[:].rearrange("p (m s) -> p m s", s=S), AX_X,
                                      ALU.max, negate=True).then_inc(e_sem(f"B.m{n}"), 1)
            if A:
                for t in range(T):
                    ps = full(dve, it, f"A.q{t}")
                    dve.tensor_copy(a_qT[:, :, tok(t)], ps[:].bitcast(F16).rearrange("p (g s) -> p g s", s=P)
                                    ).then_inc(e_sem(f"A.q{t}"), 1)
            if Cc:
                after(dve, "c_nx", c)
                for t in range(T):
                    ts(c_tmp[:, t], cnorm[:], c_nx[:, t:t + 1], None, ALU.add).then_inc(sig["c_tmp"], 1)
                after(dve, "c_tmp", c)
                ps = full(dve, it, "C.dist")
                tt(c_nd[:], ps[:, 0:T * E].rearrange("p (t e) -> p t e", e=E), c_tmp[:],
                   ALU.subtract).then_inc(e_sem("C.dist"), 1)
                taken(dve, it, "C.dist", lone=True)
                for t in range(T):
                    dve.max(c_mx[:, t], c_nd[:, t]).then_inc(sig["c_max8"], 1)
                for t in range(T):
                    after(dve, "c_max8", c, t + 1, lone=True)
                    dve.max_index(c_ix[:, t], c_mx[:, t], c_nd[:, t]).then_inc(sig["c_index"], 1)
                after(dve, "c_index", c)
                where = slice(T * c, T * c + T) if isinstance(c, int) else bass.ds(T * c, T)
                dve.tensor_copy(expert_of[:, where], c_ix[:, :, 0]).then_inc(sig["c_expert"], 1)
            for st, h in HEADS:
                if st == "A" and A:
                    taken(dve, it, f"A.s{h}")
                    tt(a_p[:, h % NPR], a_p[:, h % NPR], eb[:, h], ALU.mult).then_inc(sig["a_p"], 1)
                if (st, h) == ("B", H1 - 2) and A:
                    after(dve, "a_p_used", a)
                    normalised(it, "A", 0, a_rec, a_y, H0, D0, a, "a_rec")
            if A:
                ps = full(dve, it, "A.wo")
                tt(a_r[:], ps[:].rearrange("p (t n) -> p t n", n=D), a_xl[:], ALU.add).then_inc(e_sem("A.wo"), 1)
            if Bb:
                after(dve, "b_p_used", b)
                normalised(it, "B", 0, b_rec, b_y, H1, D1, b, "b_rec")
            if A:
                after(dve, "a_rz", a)
                for t in range(T):
                    ts(a_xn[:, t], a_r[:, t], a_rz[:, 1, t:t + 1], None, ALU.mult).then_inc(sig["a_z"], 1)
            if Bb:
                ps = full(dve, it, "B.wo")
                tt(b_q[:], ps[:].rearrange("p (t n) -> p t n", n=D), b_xl[:], ALU.add).then_inc(e_sem("B.wo"), 1)
                taken(dve, it, "B.wo")
                stats(b_q, b_st, b_mv2, "b_stats2", "b_mv2", b)
                after(dve, "b_norm2", b)
                shifted(b_q, b_q, b_mv2, b_rs2[:, 1], "b_n")
            if A:
                ps = full(dve, it, "A.out")
                after(dve, "a_xy", a)
                if Bb:
                    after(dve, "x1_kept", b)
                tt(x1[:], ps[:].rearrange("p (t n) -> p t n", n=D), x_keep[:], ALU.add).then_inc(e_sem("A.out"), 1)
                taken(dve, it, "A.out")
                stats(x1, b_st, b_mv, "b_stats", "b_mv", a)
            if Bb:
                ps = full(dve, it, "B.out")
                after(dve, "b_qb2", b)
                tt(b_f[:], ps[:].rearrange("p (t n) -> p t n", n=D), b_q[:], ALU.add).then_inc(e_sem("B.out"), 1)
                taken(dve, it, "B.out")
                stats(b_f, c_st, c_mv, "c_stats", "c_mv", b)

        dve.wait_ge(s_eb, 8)
        dve.wait_ge(s_const, CONSTS)
        each(dve, turn)

        phase1_over(dve)
        dve.wait_ge(s_iota, 4)
        link = [0]

        def chain(ins):
            ins.then_inc(s_route, 1)
            link[0] += 1
            dve.wait_ge(s_route, link[0])

        def over(ap, n, m):
            return ap.unsqueeze(1).to_broadcast([P, n, m])

        chain(tt(oh[:], bc(expert_of[:], E), over(io_e[:], NT, E), ALU.is_equal))
        dve.wait_ge(s_pp, 1)
        chain(dve.tensor_copy(r_tot[:].rearrange("p n e -> p (n e)"), bank[1][:, 0:NT * E]))
        for e in range(E):
            ins = dve.tensor_tensor_scan(r_cum[:, :, e], ones_nt[:], r_tot[:, :, e], 0.0, ALU.mult, ALU.add)
            if e < E - 1:
                ins.then_inc(s_route, 1)
                link[0] += 1
        chain(ins)
        chain(tt(r_cmp[:], bc(r_cum[:, NT - 1, :], NT), over(io_t[:], E, NT), ALU.is_gt))
        chain(dve.tensor_reduce(r_nt[:], r_cmp[:], AX_X, ALU.add))
        chain(dve.tensor_tensor_scan(r_ct[:], ones_nt[:, 0:E], r_nt[:], 0.0, ALU.mult, ALU.add))
        chain(tt(r_base[:], r_ct[:], r_nt[:], ALU.subtract))
        chain(ts(r_base[:], r_base[:], float(P), None, ALU.mult))
        chain(tt(r_a[:], r_cum[:], r_tot[:], ALU.subtract))
        chain(tt(r_a[:], r_a[:], bank[0][:, 0:NT * E].rearrange("p (n e) -> p n e", e=E), ALU.add))
        chain(tt(r_a[:], r_a[:], over(r_base[:], NT, E), ALU.add))
        chain(tt(r_a[:], r_a[:], oh[:], ALU.mult))
        chain(dve.tensor_reduce(r_posf[:], r_a[:], AX_X, ALU.add))
        chain(dve.tensor_copy(pos[:], r_posf[:]))
        assert link[0] == ROUTE_POS
        chain(tt(r_cmp2[:], bc(io_i[:], E), over(r_ct[:], TILES_MAX, E), ALU.is_ge))
        chain(dve.tensor_reduce(r_te[:], r_cmp2[:], AX_X, ALU.add))
        chain(ts(tile_expert[:, 0:TILES_MAX], r_te[:], float(E - 1), None, ALU.min))
        assert link[0] == ROUTE_ALL

        def step(k, n, nxt):
            for u in range(n):
                after_tile(dve, "m_silu", k, u)
                tt(m_h[:, u], bank[2 + 2 * u][:], m_sg[:, u], ALU.mult).then_inc(mig[u]["m_h"], 1)
            for u in range(n):
                after_tile(dve, "m_down", k, u)
                after_tile(dve, "m_stored", k, u, 0)
                after_tile(dve, "m_skip", k, u)
                tt(m_out[:, u], bank[7][:, 0:D], m_skip[:, u, 0:D], ALU.add).then_inc(mig[u]["m_out"], 1)

        tile_steps(dve, step)

    @block.tensor
    def _(pe):
        mm = nc.tensor.matmul

        def product(out, lhsT, rhs, first=True, last=True, **kw):
            return mm(out, lhsT=lhsT, rhs=rhs, start=first, stop=last, **kw)

        pe.wait_ge(s_setup_dma, ALL_LOADED)
        pe.wait_ge(s_const, CONSTS)
        product(bank[0][0:H0, 0:S], relb[:], onehot[:]).then_inc(s_pe_setup, 1)
        for c in range(C):
            ins = nc.tensor.transpose(bank[1][:, c * E:(c + 1) * E], cent[:, c * P:(c + 1) * P], ident[0:E, 0:E])
        ins.then_inc(s_pe_setup, 1)
        pe.wait_ge(s_cent, 2)
        for c in range(C):
            ins = product(bank[2][:, 0:E], ones[:], cent_sq[:, c], c == 0, c == C - 1)
        ins.then_inc(s_pe_setup, 1)
        pe.wait_ge(s_w, 3 * C + 2)
        pe.wait_ge(s_cent, 3)
        pe.wait_ge(s_eb, 4)

        def transposes(it, job, x):
            ps = claim(pe, it, job)
            for c in range(C):
                for t in range(T):
                    ins = nc.tensor.transpose(ps[:, c * S + t * P:c * S + (t + 1) * P], x[:, t, c * P:(c + 1) * P],
                                              ident[:])
            ins.then_inc(f_sem(job), 1)

        def rows_out(it, job, xT, w, chunks=C):
            ps = claim(pe, it, job)
            for t in range(T):
                for c in range(chunks):
                    ins = product(ps[:, t * D:(t + 1) * D], xT[:, c, tok(t)], w[:, c, :], c == 0, c == chunks - 1)
            ins.then_inc(f_sem(job), 1)

        def cols_out(it, job, xT, w, first_chunk):
            ps = claim(pe, it, job)
            for m in range(2):
                for c in range(C):
                    at = (first_chunk + m) * P
                    ins = product(ps[:, m * S:(m + 1) * S], w[:, c, at:at + P], xT[:, c, :], c == 0, c == C - 1)
            ins.then_inc(f_sem(job), 1)

        def scores(it, st, h):
            job = f"{st}.s{h}"
            ps = claim(pe, it, job)
            if st == "A":
                r, g = 64 * (h % 2), h // 2
                product(ps[:, 0:S], a_kT[r:r + 64, g, 0:P], a_qT[r:r + 64, g, :])
                product(ps[:, S:SCOLS], a_kT[r:r + 64, g, P:], a_qT[r:r + 64, g, P:]).then_inc(f_sem(job), 1)
            else:
                r, m = 32 * (h % 4), h // 4
                for kt in range(T):
                    out = ps[:, kt * S:(kt + 1) * S]
                    product(out, ones_r[r:r + 1, :], b_nmT[r:r + 1, m, :], True, False)
                    ins = product(out, b_kT[r:r + 32, m, tok(kt)], b_qT[r:r + 32, m, :], False, True)
                ins.then_inc(f_sem(job), 1)

        def weigh(it, st, h):
            o = [bank[BANK_OF[f"{st}.o{t}"]] for t in range(T)]
            if h == 0:
                for t in range(T):
                    claim(pe, it, f"{st}.o{t}")
            if st == "A":
                if h == 0:
                    product(o[0][:, 0:H0 * (D0 + 1)], first_col[:], a_v[:, 1].rearrange("p h d -> p (h d)"), True,
                            False, skip_group_check=True)
                after(pe, "a_p", it.batch("A"), h + 1)
                at = slice(h * (D0 + 1), (h + 1) * (D0 + 1))
                p = a_p[:, h % NPR]
                product(o[0][:, at], p[:, 0:P], a_v[:, 0, h], False, h == H0 - 1, skip_group_check=True)
                product(o[1][:, at], p[:, P:S], a_v[:, 0, h], h == 0, False, skip_group_check=True)
                product(o[1][:, at], p[:, S:], a_v[:, 1, h], False, h == H0 - 1,
                        skip_group_check=True).then_inc(sig["a_p_used"], 1)
            else:
                taken(pe, it, f"B.s{h}")
                at = slice(h * (D1 + 1), (h + 1) * (D1 + 1))
                for t in range(T):
                    for kt in range(T):
                        ins = product(o[t][:, at], b_p[:, h % NPR, kt, tok(t)], b_v[:, kt, h],
                                      h == 0 and kt == 0, h == H1 - 1 and kt == T - 1, skip_group_check=True)
                ins.then_inc(sig["b_p_used"], 1)

        def turn(it):
            A, Bb, Cc = (st in it.stages for st in "ABC")
            a, b, c = (it.batch(st) for st in "ABC")
            if A:
                after(pe, "a_xn", a)
                transposes(it, "A.xn", a_xn)
            if Bb:
                after(pe, "b_xl", b)
                transposes(it, "B.x", b_xl)
                after(pe, "b_loaded", b)
                transposes(it, "B.ctx", c_in)
            if A:
                taken(pe, it, "A.xn")
                for t in range(T):
                    ps = claim(pe, it, f"A.qk{t}")
                    for c_ in range(C):
                        ins = product(ps[:], a_xnT[:, c_, tok(t)], w0qk[:, c_, :], c_ == 0, c_ == C - 1)
                    ins.then_inc(f_sem(f"A.qk{t}"), 1)
                rows_out(it, "A.v", a_xnT, w0v)
            if Bb:
                taken(pe, it, "B.ctx")
                cols_out(it, "B.k", b_ctxT, w1k, 0)
                rows_out(it, "B.v", b_ctxT, w1v)
                taken(pe, it, "B.x")
                cols_out(it, "B.q_", b_xT, w1q, 0)
                after(pe, "b_kb", b)
                after(pe, "b_qb", b)
                for n in range(8):
                    t, j = n // 4, n % 4
                    ps = claim(pe, it, f"B.m{n}")
                    for m in range(C):
                        r = 32 * j
                        ins = product(ps[:, m * S:(m + 1) * S], b_qTb[r:r + 32, m, tok(t)], b_kTb[r:r + 32, m, :])
                    ins.then_inc(f_sem(f"B.m{n}"), 1)
            if Cc:
                after(pe, "c_rows", c, 1)
                transposes(it, "C.xn", c_rows)
            if A:
                for t in range(T):
                    for n, name in enumerate(("q", "k")):
                        after(pe, "a_lo", a, 2 * t + 1 + n)
                        ps = claim(pe, it, f"A.{name}{t}")[:].bitcast(F16)
                        for g in range(H0 // 2):
                            h = n * H0 + 2 * g
                            ins = nc.tensor.transpose(
                                ps[:, g * P:(g + 1) * P],
                                a_split[:, t, h:h + 2].rearrange("p h s d -> p (h s d)"), ident16[:])
                        ins.then_inc(f_sem(f"A.{name}{t}"), 1)
            if Cc:
                taken(pe, it, "C.xn")
                ps = claim(pe, it, "C.dist")
                for t in range(T):
                    for c_ in range(C):
                        ins = product(ps[:, t * E:(t + 1) * E], c_xnT[:, c_, tok(t)], cent_t[:, c_], c_ == 0,
                                      c_ == C - 1)
                ins.then_inc(f_sem("C.dist"), 1)
            if Bb:
                taken(pe, it, "B.m6")
                taken(pe, it, "B.m7")
                ps = claim(pe, it, "B.max")
                for m in range(C):
                    for t in range(T):
                        ins = nc.tensor.transpose(ps[:, m * S + t * P:m * S + (t + 1) * P],
                                                  b_nm[:, t, m].rearrange("p j w -> p (j w)"), ident[:])
                ins.then_inc(f_sem("B.max"), 1)
                taken(pe, it, "B.max")
            if A:
                taken(pe, it, f"A.q{T - 1}")
                taken(pe, it, f"A.k{T - 1}")
            heads = [x for x in HEADS if x[0] in it.stages]
            for n in range(len(heads) + 2):
                if n < len(heads):
                    scores(it, *heads[n])
                if n >= 2:
                    weigh(it, *heads[n - 2])
                if A and n >= 2 and heads[n - 2] == (("B", H1 - 3) if Bb else ("A", H0 - 1)):
                    taken(pe, it, "A.o0")
                    taken(pe, it, "A.o1")
                    transposes(it, "A.y", a_y)
                if A and n == len(heads):
                    pass
            if A:
                taken(pe, it, "A.y")
                rows_out(it, "A.wo", a_yT, w0o)
            if Bb:
                taken(pe, it, "B.o0")
                taken(pe, it, "B.o1")
                transposes(it, "B.y", b_y)
                taken(pe, it, "B.y")
                rows_out(it, "B.wo", b_yT, w1o)
            if A:
                after(pe, "a_z", a)
                transposes(it, "A.z", a_xn)
                taken(pe, it, "A.z")
                for n in range(4):
                    cols_out(it, f"A.h{n}", a_xnT, w01, 2 * n)
            if Bb:
                after(pe, "b_q", b)
                transposes(it, "B.q", b_q)
            if A:
                for n in (2, 3):
                    taken(pe, it, f"A.h{n}")
                rows_out(it, "A.out", a_hT, w02, J)
            if Bb:
                taken(pe, it, "B.q")
                for n in range(4):
                    cols_out(it, f"B.h{n}", b_xT, w11, 2 * n)
                for n in (2, 3):
                    taken(pe, it, f"B.h{n}")
                rows_out(it, "B.out", b_hT, w12, J)

        each(pe, turn)

        pe.wait_ge(s_route, 1)
        flat = oh[:].rearrange("p n e -> p (n e)")
        product(bank[0][:, 0:NT * E], tri[:], flat)
        product(bank[1][:, 0:NT * E], ones[:], flat).then_inc(s_pp, 1)

        pe.wait_ge(s_route, ROUTE_ALL)
        pe.wait_ge(s_wmoe, 16 * 2 * E)

        def transpose_in(k, u):
            after_tile(pe, "m_loaded", k, u)
            after_tile(pe, "m_xT", k, u, 0)
            for c in range(C):
                ins = nc.tensor.transpose(bank[u][:, c * P:(c + 1) * P], m_in[:, u, c * P:(c + 1) * P], ident[:])
            ins.then_inc(mig[u]["m_x"], 1)

        transpose_in(0, 0)
        transpose_in(0, 1)

        def step(k, n, nxt):
            expert = []
            for u in range(n):
                i = 2 * k + u
                at = tile_expert[0:1, i:i + 1] if isinstance(i, int) else tile_expert[0:1, bass.ds(i, 1)]
                expert.append(pe.value_load(at, min_val=0, max_val=E - 1))
            for u in range(n):
                after_tile(pe, "m_xT", k, u)
                after_tile(pe, "m_h", k, u, 0)
                for half in range(2):
                    for c in range(C):
                        w = up[:, bass.ds(expert[u], 1), c, half * EH:(half + 1) * EH]
                        ins = product(bank[2 + 2 * u + half][:], m_xT[:, u, c], w.rearrange("p o n -> p (o n)"),
                                      c == 0, c == C - 1)
                ins.then_inc(mig[u]["m_up"], 1)
            for u in range(nxt):
                transpose_in(k + 1, u)
            for u in range(n):
                after_tile(pe, "m_h", k, u)
                after_tile(pe, "m_hT", k, 1 - u, u)
                for j in range(EJ):
                    ins = nc.tensor.transpose(bank[6][:, j * P:(j + 1) * P], m_h[:, u, j * P:(j + 1) * P], ident[:])
                ins.then_inc(mig[u]["m_ht"], 1)
                after_tile(pe, "m_hT", k, u)
                after_tile(pe, "m_out", k, 1 - u, u)
                for j in range(EJ):
                    w = down[:, bass.ds(expert[u], 1), j, :]
                    ins = product(bank[7][:, 0:D], m_hT[:, u, j], w.rearrange("p o n -> p (o n)"), j == 0,
                                  j == EJ - 1)
                ins.then_inc(mig[u]["m_down"], 1)

        tile_steps(pe, step)


_INS = ["x", "ctx_1024", "L0_attn_ln1_w", "L0_attn_Wq", "L0_attn_Wk", "L0_attn_Wv", "L0_attn_rel_bias",
        "L0_attn_scale", "L0_attn_Wo", "L0_attn_ln2_w", "L0_attn_W1", "L0_attn_W2", "L0_xattn_Wq", "L0_xattn_Wk",
        "L0_xattn_Wv", "L0_xattn_Wo", "L0_xattn_lambda_param", "L0_xattn_ln1_g", "L0_xattn_ln1_b",
        "L0_xattn_ln2_g", "L0_xattn_ln2_b", "L0_xattn_ffn_w1", "L0_xattn_ffn_b1", "L0_xattn_ffn_w2",
        "L0_xattn_ffn_b2", "L0_ffn_scale", "L0_ffn_centroids", "L0_ffn_up_w", "L0_ffn_down_w"]


def bucket_onehot():
    dist = np.arange(S)
    exact = BUCKETS // 2
    safe = np.maximum(dist, 1).astype(np.float32)
    ratio = np.log(safe / np.float32(exact)) / np.float32(np.log(128 / exact)) * np.float32(BUCKETS - exact)
    bucket = np.where(dist < exact, dist, np.minimum(exact + ratio.astype(np.int32), BUCKETS - 1))
    return (np.arange(BUCKETS)[:, None] == bucket[None, :]).astype(np.float32)


def kernel(**inputs):
    import concourse.bacc as _bacc
    from concourse.bass_utils import run_bass_kernel_spmd as _run

    nc = _bacc.Bacc("TRN2", target_bir_lowering=False, num_devices=1)
    arrays, d = {}, {}
    for name in _INS:
        a = np.ascontiguousarray(inputs[name])
        if a.ndim == 0:
            a = a.reshape(1, 1)
        arrays[f"in_{name}"] = a
        d[name] = nc.dram_tensor(f"in_{name}", a.shape, mybir.dt.from_np(a.dtype), kind="ExternalInput").ap()
    a = bucket_onehot()
    arrays["in_bucket_onehot"] = a
    d["bucket_onehot"] = nc.dram_tensor("in_bucket_onehot", a.shape, F32, kind="ExternalInput").ap()
    d["out"] = nc.dram_tensor("out_rows", (B * S, D), F32, kind="ExternalOutput").ap()
    build(nc, d)
    r = _run(nc, [arrays], core_ids=[0])
    return r.results[0]["out_rows"].reshape(B, S, D)
```

```python
from contextlib import ExitStack

import numpy as np

import concourse.bass as bass
import concourse.mybir as mybir

F32 = mybir.dt.float32
F32R = mybir.dt.float32r
F16 = mybir.dt.float16
BF16 = mybir.dt.bfloat16
I32 = mybir.dt.int32
U32 = mybir.dt.uint32
ALU = mybir.AluOpType
ACT = mybir.ActivationFunctionType
AX_X = mybir.AxisListType.X

P = 128
B, S, D = 16, 256, 256
T = S // P
C = D // P
H0, D0 = 16, 16
H1, D1 = 8, 32
HID = 1024
J = HID // P
E = 8
EH = 512
EJ = EH // P
BUCKETS = 32
NT = B * T
TILES_MAX = NT + E - 1
RW = 2 * D + 1
ROUTE_POS = 21
ROUTE_ALL = ROUTE_POS + 3
RING = 8

SCOLS = S + P

GROUP = 4
A_HEADS = [8 * c + 2 * j + par for c in range(C) for par in range(2) for j in range(GROUP)]
NPA, NPB = 8, 6


def a_s(n):
    return ("score", "A", n)


def b_s(h):
    return ("score", "B", h)


PLAN = [a_s(0), a_s(1), a_s(2), a_s(3), ("out", "D", 0)]
PLAN += [a_s(4), a_s(5), b_s(0), ("weigh", "A", 0), ("out", "D", 1), a_s(6), a_s(7), b_s(1), ("distances", "C", 0)]
PLAN += [a_s(8), a_s(9), b_s(2), ("weigh", "A", 1), ("out", "D", 2), a_s(10), a_s(11), b_s(3), ("norm", "A", 0)]
PLAN += [("expert", "C", 0), a_s(12), a_s(13), b_s(4), ("weigh", "A", 2), ("out", "D", 3), a_s(14), a_s(15), b_s(5)]
PLAN += [("weigh", "B", 0), ("norm", "B", 0), ("f", "D", 0)]
PLAN += [b_s(6), b_s(7), ("weigh", "A", 3), ("weigh", "B", 1)]

def _banks():
    out = []

    def add(banks, jobs):
        out.extend((job, banks[n % len(banks)]) for n, job in enumerate(jobs))

    out += [("A.xn", 0), ("B.ctx", 1), ("D.q", 0), ("A.qk0", 4), ("A.qk1", 5), ("B.k", 2), ("B.x", 1), ("B.q_", 3)]
    out += [("B.m0", 0), ("B.m1", 1), ("B.m2", 2), ("B.m3", 3), ("A.v", 6), ("D.h0", 0), ("B.m4", 1), ("B.m5", 2)]
    out += [("B.v", 7), ("B.m6", 3), ("B.m7", 0), ("D.h1", 1), ("D.h2", 2), ("A.q0", 3), ("A.k0", 0), ("D.h3", 1)]
    out += [("A.q1", 2), ("A.k1", 3), ("B.max", 0)]
    of = {("A", 0): 4, ("A", 2): 4, ("B", 0): 6, ("B", 1): 7}
    scores = 0
    for what, st, n in PLAN:
        if what == "score":
            out.append((f"{st}.s{n}", (1, 2, 3, 0)[scores % 4]))
            scores += 1
        if what == "weigh" and (st, n) in of:
            out.append((f"{st}.o{n // 2 if st == 'A' else n}", of[st, n]))
        if what == "distances":
            out += [("C.xn", 0), ("C.dist", 6)]
        if (what, n) == ("out", 0):
            out.append(("D.out", 5))
    add((5, 4), ["A.wo", "B.wo"])
    add((0,), ["A.z"])
    add((2, 3), [f"A.h{n}" for n in range(4)])
    add((6,), ["A.out"])
    return out


UNSIGNALLED = ("A.o0", "A.o1", "B.o0", "B.o1")

BANKS, BANK_OF = {}, {}
for _job, _bank in _banks():
    BANK_OF[_job] = _bank
    BANKS.setdefault(_bank, []).append(_job)
PHASES = [(0, 1, "P"), (1, 1, "PA"), (2, 1, "PAB"), (3, 1, "PABD"), (4, B - 4, "PABDC"), (B, 1, "ABDC"),
          (B + 1, 1, "BDC"), (B + 2, 1, "DC"), (B + 3, 1, "C")]


class Turn:

    def __init__(self, phase, k):
        self.first, self.count, self.stages = PHASES[phase]
        self.phase, self.k = phase, k

    def batch(self, stage):
        return self.k + (self.first - "PABDC".index(stage))

    def _before(self, job, counted):
        bank = [j for j in BANKS[BANK_OF[job]] if counted(j)]
        before = sum(n * sum(j[0] in st for j in bank) for _, n, st in PHASES[:self.phase])
        mine = [j for j in bank if j[0] in self.stages]
        return self.k * len(mine) + (before + mine.index(job))

    def used(self, job):
        return self._before(job, lambda j: True)

    def signalled(self, job):
        return self._before(job, lambda j: j not in UNSIGNALLED)


def build(nc, d):
    ctx = ExitStack()
    with ctx:
        _build(nc, d, ctx)


def _build(nc, d, ctx):
    def sem(name):
        return ctx.enter_context(nc.semaphore(name))

    def sbuf(stack, name, shape, dt=F32):
        return stack.enter_context(nc.sbuf_tensor(name, shape, dt))

    LONE = (mybir.EngineType.Pool, mybir.EngineType.SP)
    s_passed = {e: sem(f"waits_passed_{n}") for n, e in enumerate(LONE + (mybir.EngineType.DVE,))}

    def wait(eng, s, value, lone=False):
        if isinstance(value, int):
            if value > 0:
                eng.wait_ge(s, value)
            return
        eng.wait_ge(s, value)
        if lone or eng.engine in LONE:
            eng.sem_inc(s_passed[eng.engine], 1)

    toep = nc.dram_tensor("toep", (H0, P, 4 * P), F32, kind="Internal")
    mrow = nc.dram_tensor("mrow", (H0, S), F32, kind="Internal")
    rows_lin = nc.dram_tensor("rows_lin", (B * S, RW), F32, kind="Internal")
    rows_srt = nc.dram_tensor("rows_srt", (TILES_MAX * P, RW), F32, kind="Internal")

    bank = [ctx.enter_context(nc.psum_tensor(f"bank{n}", [P, 512], F32)) for n in range(8)]
    bank_full = [sem(f"bank_full{n}") for n in range(8)]
    bank_free = [sem(f"bank_free{n}") for n in range(8)]

    def claim(pe, turn, job):
        wait(pe, bank_free[BANK_OF[job]], turn.used(job))
        return bank[BANK_OF[job]]

    def full(eng, turn, job):
        wait(eng, bank_full[BANK_OF[job]], turn.signalled(job) + 1)
        return bank[BANK_OF[job]]

    def taken(eng, turn, job, lone=False):
        wait(eng, bank_free[BANK_OF[job]], turn.used(job) + 1, lone)

    def f_sem(job):
        return bank_full[BANK_OF[job]]

    def e_sem(job):
        return bank_free[BANK_OF[job]]

    ident = sbuf(ctx, "ident", [P, P])
    ident16 = sbuf(ctx, "ident16", [P, P], F16)
    ones = sbuf(ctx, "ones", [P, P])
    ones_r = sbuf(ctx, "ones_r", [P, P], F32R)
    tri = sbuf(ctx, "tri", [P, P])
    halves = sbuf(ctx, "halves", [P, 2, 32])
    mhalf = sbuf(ctx, "mhalf", [P, 64])
    expert_of = sbuf(ctx, "expert_of", [P, NT])
    pos = sbuf(ctx, "pos", [P, NT], I32)
    tile_expert = sbuf(ctx, "tile_expert", [P, 64], I32)

    s_const = sem("const_made")
    s_setup_dma = sem("setup_loaded")
    s_w = sem("weights_scaled")
    s_zero = sem("scratch_cleared")

    p1 = ExitStack()
    w0qk = sbuf(p1, "w0qk", [P, C, 2 * D])
    w0v = sbuf(p1, "w0v", [P, C, D])
    w0o = sbuf(p1, "w0o", [P, C, D])
    w01 = sbuf(p1, "w01", [P, C, HID])
    w02 = sbuf(p1, "w02", [P, J, D])
    w1q = sbuf(p1, "w1q", [P, C, D])
    w1k = sbuf(p1, "w1k", [P, C, D])
    w1v = sbuf(p1, "w1v", [P, C, D])
    w1o = sbuf(p1, "w1o", [P, C, D])
    w11 = sbuf(p1, "w11", [P, C, HID])
    w12 = sbuf(p1, "w12", [P, J, D])
    b11 = sbuf(p1, "b11", [P, J])
    ln0 = sbuf(p1, "ln0", [P, 2, C])
    vecs = sbuf(p1, "vecs", [P, 6, D])
    G1, B1, G2, B2, FB2, FSC = range(6)
    eb = sbuf(p1, "eb", [P, H0, SCOLS])
    qscale = sbuf(p1, "qscale", [P, T, 2 * H0])
    cent = sbuf(p1, "cent", [E, D])
    cent_t = sbuf(p1, "cent_t", [P, C, E])
    cent_sq = sbuf(p1, "cent_sq", [P, C, E])
    cnorm = sbuf(p1, "cnorm", [P, E])
    lam = sbuf(p1, "lam", [P, 3])

    x_in = sbuf(p1, "x_in", [P, T, D])
    x_keep = sbuf(p1, "x_keep", [P, T, D])
    a_xl = sbuf(p1, "a_xl", [P, T, D])
    a_xn = sbuf(p1, "a_xn", [P, T, D])
    a_xnT = sbuf(p1, "a_xnT", [P, C, S])
    a_sq = sbuf(p1, "a_sq", [P, T, 2 * D])
    a_hat = a_sq
    a_split = sbuf(p1, "a_split", [P, T, 2 * H0, 4, D0], F16)
    a_qT = sbuf(p1, "a_qT", [P, H0 // 2, S], F16)
    a_kT = sbuf(p1, "a_kT", [P, H0 // 2, S], F16)
    a_v = sbuf(p1, "a_v", [P, T, 2, H0 // 2, 32])
    a_p = sbuf(p1, "a_p", [P, NPA, SCOLS])
    a_yT = sbuf(p1, "a_yT", [P, C, S])
    a_hT = sbuf(p1, "a_hT", [P, J, S])
    a_st = sbuf(p1, "a_st", [P, T, 6])
    a_mv = sbuf(p1, "a_mv", [P, T, 2])
    a_sc = sbuf(p1, "a_sc", [P, 8, T])
    a_ss = sbuf(p1, "a_ss", [P, T, 2 * H0])
    a_rn = sbuf(p1, "a_rn", [P, T, 2 * H0])
    a_nw = sbuf(p1, "a_nw", [P, 5, T * 2 * H0])
    rec = sbuf(p1, "rec", [P, 2 * C, S])
    a_ms = sbuf(p1, "a_ms", [P, T])
    a_rz = sbuf(p1, "a_rz", [P, 2, T])
    x1 = sbuf(p1, "x1", [P, T, D])
    c_in = sbuf(p1, "c_in", [P, T, D])
    b_ctxT = sbuf(p1, "b_ctxT", [P, C, S])
    b_xl = sbuf(p1, "b_xl", [P, T, D])
    b_xT = sbuf(p1, "b_xT", [P, C, S])
    b_kh, b_kl, b_qh, b_ql = (sbuf(p1, name, [P, C, S], F32R) for name in ("b_kh", "b_kl", "b_qh", "b_ql"))
    b_v = sbuf(p1, "b_v", [P, T, D])
    b_nm = sbuf(p1, "b_nm", [P, T, C, 4, 32])
    b_nmT = sbuf(p1, "b_nmT", [P, C, S], F32R)
    b_p = sbuf(p1, "b_p", [P, NPB, T, S])
    b_zT = sbuf(p1, "b_zT", [P, C, S])
    b_yT = sbuf(p1, "b_yT", [P, C, S])
    b_q = sbuf(p1, "b_q", [P, T, D])
    b_hT = sbuf(p1, "b_hT", [P, J, S])
    b_st = sbuf(p1, "b_st", [P, T, 6])
    b_mv = sbuf(p1, "b_mv", [P, T, 2])
    b_rs = sbuf(p1, "b_rs", [P, 2, T])
    b_mv2 = sbuf(p1, "b_mv2", [P, T, 2])
    b_rs2 = sbuf(p1, "b_rs2", [P, 2, T])
    x1_keep = sbuf(p1, "x1_keep", [P, T, D])
    x1_keep2 = sbuf(p1, "x1_keep2", [P, T, D])
    b_f = sbuf(p1, "b_f", [P, T, D])
    c_n = b_f
    c_rows = sbuf(p1, "c_rows", [P, T, 2 * D])
    c_x2 = c_rows[:, :, D:]
    zrow = b_p[:].rearrange("p n t s -> p (n t s)")[:, 0:RW]
    idcol = sbuf(p1, "idcol", [P, NT], I32)
    c_xnT = sbuf(p1, "c_xnT", [P, C, S])
    c_st = sbuf(p1, "c_st", [P, T, 6])
    c_mv = sbuf(p1, "c_mv", [P, T, 2])
    c_rs = sbuf(p1, "c_rs", [P, 2, T])
    c_mv2 = sbuf(p1, "c_mv2", [P, T, 2])
    c_sc = sbuf(p1, "c_sc", [P, 8, T])
    c_nx = sbuf(p1, "c_nx", [P, T])
    c_tmp = sbuf(p1, "c_tmp", [P, T, E])
    c_nd = sbuf(p1, "c_nd", [P, T, E])
    c_mx = sbuf(p1, "c_mx", [P, T, 8])
    c_ix = sbuf(p1, "c_ix", [P, T, 8], U32)
    bias_b = b_hT
    flat_h = a_hT[:].rearrange("p j s -> p (j s)")
    onehot = flat_h[0:BUCKETS, 0:S]
    relb = sbuf(p1, "relb", [BUCKETS, H0])
    sc16 = sbuf(p1, "sc16", [H0, 1])
    bd = flat_h[0:H0, S:S + 4 * P]
    bmax = flat_h[0:H0, S + 4 * P:2 * S + 4 * P]

    PER_BATCH = {
        "a_loaded": 16, "a_stats": T, "a_mv": T, "a_norms": 7, "a_xn": T, "a_xl": T, "a_kept": 1,
        "a_squares": T, "a_sumsq": T, "a_rn": 14, "a_hi": 2 * T, "a_lo_q": T, "a_lo_k": T, "a_p": H0,
        "a_p_used": H0 // GROUP, "a_rec": C, "a_ms": T, "a_rz": 2, "a_xy": 1, "a_z": T,
        "b_loaded": 16, "b_stats": T, "b_mv": T, "b_norm": 2, "x1_kept": 1, "x1_kept2": 1, "b_xl": T, "b_hi": 2,
        "b_p_used": H1 // GROUP, "b_rec": C, "b_stats2": T, "b_mv2": T, "b_norm2": 2, "b_n": T, "b_gain": 1,
        "b_q": 1, "b_qb2": 1,
        "c_stats": T, "c_mv": T, "c_norm": 2, "c_n": T, "c_gain": 1, "c_out": 1, "c_x2": 1, "c_stats2": T,
        "c_mv2": T, "c_norms": 7, "c_xl": T, "c_xs": T, "c_rows": 2, "c_stored": 16, "c_nx": T, "c_tmp": T,
        "c_max8": T, "c_index": T, "c_expert": 1,
    }
    sig = {name: sem(name) for name in PER_BATCH}

    def after(eng, name, batch, n=None, lone=False):
        per = PER_BATCH[name]
        wait(eng, sig[name], batch * per + (per if n is None else n), lone)

    s_ids, s_toep, s_tp, s_bd, s_bmax, s_eb, s_cent, s_lam, s_pe_setup, s_sc = map(sem, (
        "ids_stored", "toeplitz_written", "toeplitz_read", "bias_by_distance", "bias_prefix_max", "eb_made",
        "centroid_norms", "lambda_chain", "pe_setup", "qscale_made"))

    def bc(ap, n):
        return ap.unsqueeze(len(ap.shape)).to_broadcast(list(ap.shape) + [n])

    def over_t(ap):
        return ap.unsqueeze(1).to_broadcast([P, T, D])

    def tok(t):
        return slice(t * P, (t + 1) * P)

    block = ctx.enter_context(nc.Block())
    ctx.enter_context(nc.allow_non_contiguous_dma(reason="a few vectors laid over partitions, once"))

    def w_view(ap):
        return ap.rearrange("(c p) n -> p c n", p=P)

    def on_all(ap):
        return ap.rearrange("(o n) -> o n", o=1).to_broadcast([P, ap.shape[0]])

    setup_loads = [
        (w0qk[:, :, 0:D], w_view(d["L0_attn_Wq"])), (w0qk[:, :, D:], w_view(d["L0_attn_Wk"])),
        (ln0[:, 0, :], d["L0_attn_ln1_w"].rearrange("(c p) -> p c", p=P)),
        (ln0[:, 1, :], d["L0_attn_ln2_w"].rearrange("(c p) -> p c", p=P)),
        (onehot, d["bucket_onehot"]), (relb[:], d["L0_attn_rel_bias"]),
        (sc16[:], d["L0_attn_scale"].rearrange("(h o) -> h o", o=1)),
        (lam[:, 0:1], d["L0_xattn_lambda_param"].to_broadcast([P, 1])),
        (cent[:], d["L0_ffn_centroids"]),
        (w0v[:], w_view(d["L0_attn_Wv"])), (w0o[:], w_view(d["L0_attn_Wo"])),
        (w01[:], w_view(d["L0_attn_W1"])), (w02[:], w_view(d["L0_attn_W2"])),
        (w1q[:], w_view(d["L0_xattn_Wq"])), (w1k[:], w_view(d["L0_xattn_Wk"])),
        (w1v[:], w_view(d["L0_xattn_Wv"])), (w1o[:], w_view(d["L0_xattn_Wo"])),
        (w11[:], w_view(d["L0_xattn_ffn_w1"])), (w12[:], w_view(d["L0_xattn_ffn_w2"])),
        (b11[:], d["L0_xattn_ffn_b1"].rearrange("(j p) -> p j", p=P)),
    ]
    setup_loads += [(vecs[:, n, :], on_all(d[name])) for n, name in enumerate((
        "L0_xattn_ln1_g", "L0_xattn_ln1_b", "L0_xattn_ln2_g", "L0_xattn_ln2_b", "L0_xattn_ffn_b2", "L0_ffn_scale"))]
    setup_loads += [(qscale[:, t, 0:H0], on_all(d["L0_attn_scale"])) for t in range(T)]
    ALL_LOADED = 16 * len(setup_loads)
    CONSTS = 16

    x_tiles = d["x"].rearrange("b (t p) n -> b p t n", p=P)
    ctx_tiles = d["ctx_1024"].rearrange("b (t p) n -> b p t n", p=P)
    lin_tiles = rows_lin.ap().rearrange("(b t p) n -> b p t n", p=P, t=T)

    def of_batch(tiles, b):
        one = tiles[b:b + 1] if isinstance(b, int) else tiles[bass.ds(b, 1)]
        return one.rearrange("o p t n -> (o p) t n")

    def each(eng, body):
        for phase, (_, count, _) in enumerate(PHASES):
            if count == 1:
                body(Turn(phase, 0))
            else:
                with eng.Fori(0, count) as k:
                    body(Turn(phase, k))

    s_route, s_pp, s_wmoe = map(sem, ("routing_chain", "prefixes_made", "experts_loaded"))
    rows_back = [sem(f"rows_back{n}") for n in range(RING)]
    rows_placed = [sem(f"rows_placed{n}") for n in range(RING)]

    p1.close()
    up = sbuf(ctx, "up", [P, E, C, 2 * EH])
    down = sbuf(ctx, "down", [P, E, EJ, D])
    ring = sbuf(ctx, "ring", [P, RING, RW])
    m_in = sbuf(ctx, "m_in", [P, 2, D])
    m_skip = sbuf(ctx, "m_skip", [P, 2, D + 1])
    m_xT = sbuf(ctx, "m_xT", [P, 2, C, P])
    m_sg = sbuf(ctx, "m_sg", [P, 2, EH])
    m_h = sbuf(ctx, "m_h", [P, 2, EH])
    m_hT = sbuf(ctx, "m_hT", [P, 2, EJ, P])
    m_out = sbuf(ctx, "m_out", [P, 2, D])
    oh = sbuf(ctx, "oh", [P, NT, E])
    r_pp = sbuf(ctx, "r_pp", [P, NT, E])
    r_tot = sbuf(ctx, "r_tot", [P, NT, E])
    r_cum = sbuf(ctx, "r_cum", [P, NT, E])
    r_a = sbuf(ctx, "r_a", [P, NT, E])
    r_cmp = sbuf(ctx, "r_cmp", [P, E, NT])
    r_nt = sbuf(ctx, "r_nt", [P, E])
    r_ct = sbuf(ctx, "r_ct", [P, E])
    r_base = sbuf(ctx, "r_base", [P, E])
    r_cmp2 = sbuf(ctx, "r_cmp2", [P, TILES_MAX, E])
    r_te = sbuf(ctx, "r_te", [P, TILES_MAX])
    r_posf = sbuf(ctx, "r_posf", [P, NT])
    io_e = sbuf(ctx, "io_e", [P, E])
    io_t = sbuf(ctx, "io_t", [P, NT])
    io_i = sbuf(ctx, "io_i", [P, TILES_MAX])
    ones_nt = sbuf(ctx, "ones_nt", [P, NT])
    s_iota = sem("iotas_made")
    BY_TILE = {"m_loaded": 16, "m_skip": 16, "m_x": 1, "m_xT": 1, "m_up": 1, "m_silu": 1, "m_h": 1, "m_ht": 1, "m_hT": 1,
               "m_down": 1, "m_out": 1, "m_stored": 16}
    mig = [{name: sem(f"{name}{u}") for name in BY_TILE} for u in range(2)]

    def after_tile(eng, name, k, u, n=1):
        wait(eng, mig[u][name], (k + n) * BY_TILE[name])

    def phase1_over(eng):
        after(eng, "c_expert", B - 1)
        after(eng, "c_rows", B - 1)
        after(eng, "c_stored", B - 1)

    PAIRS = (TILES_MAX - 1) // 2

    def tile_steps(eng, body):
        body(0, 2, 2)
        with eng.Fori(0, PAIRS - 2) as k:
            body(k + 1, 2, 2)
        body(PAIRS - 1, 2, TILES_MAX - 2 * PAIRS)
        if TILES_MAX > 2 * PAIRS:
            body(PAIRS, 1, 0)

    @block.sync
    def _(sp):
        sp.dma_start(x_in[:], of_batch(x_tiles, 0)).then_inc(sig["a_loaded"], 16)
        for dst, src in setup_loads:
            sp.dma_start(dst, src).then_inc(s_setup_dma, 16)
        sp.wait_ge(s_bd, 2)
        sp.dma_start(toep.ap(), bd.unsqueeze(1).to_broadcast([H0, P, 4 * P])).then_inc(s_toep, 16)
        sp.wait_ge(s_bmax, 2)
        sp.dma_start(mrow.ap(), bmax).then_inc(s_toep, 16)
        sp.wait_ge(s_toep, 32)
        for cols in (slice(0, S), slice(S, SCOLS)):
            shifted = bass.AP(tensor=toep, offset=P, 
                              ap=[[4 * P - 1, P], [4 * P * P, H0], [1, cols.stop - cols.start]])
            sp.dma_start(eb[:, :, cols], shifted).then_inc(s_tp, 16)
        maxima = mrow.ap().rearrange("(o h) q -> o h q", o=1)
        for half in range(2):
            if half == 1:
                sp.wait_ge(s_eb, 2)
            sp.dma_start(bias_b[:], maxima[:, half * 8:(half + 1) * 8, :].to_broadcast([P, 8, S])).then_inc(s_tp, 16)
        sp.wait_ge(s_const, CONSTS)
        sp.dma_start(rows_srt.ap().rearrange("(n p) w -> p n w", p=P),
                     zrow.unsqueeze(1).to_broadcast([P, TILES_MAX, RW])).then_inc(s_zero, 16)
        sp.dma_start(rows_lin.ap().rearrange("(n p) w -> p n w", p=P)[:, :, 2 * D:],
                     idcol[:].bitcast(F32).unsqueeze(2)).then_inc(s_ids, 16)

        def turn(it):
            if "P" in it.stages and it.first > 0:
                b = it.batch("P")
                after(sp, "a_xn", b - 1)
                after(sp, "a_xl", b - 1)
                after(sp, "a_kept", b - 1)
                sp.dma_start(x_in[:], of_batch(x_tiles, b)).then_inc(sig["a_loaded"], 16)
            if "A" in it.stages:
                if "B" in it.stages:
                    taken(sp, it, "B.ctx")
                sp.dma_start(c_in[:], of_batch(ctx_tiles, it.batch("A"))).then_inc(sig["b_loaded"], 16)
            if "C" in it.stages:
                b = it.batch("C")
                after(sp, "c_rows", b)
                sp.dma_start(of_batch(lin_tiles, b)[:, :, 0:2 * D], c_rows[:]).then_inc(sig["c_stored"], 16)

        each(sp, turn)

        phase1_over(sp)
        for e in range(E):
            sp.dma_start(up[:, e], w_view(d["L0_ffn_up_w"][e])).then_inc(s_wmoe, 16)
            sp.dma_start(down[:, e], w_view(d["L0_ffn_down_w"][e])).then_inc(s_wmoe, 16)

        def load_tile(dst, cols, name, k, u):
            tile = rows_srt.ap().rearrange("(n p) w -> n p w", p=P)
            i = 2 * k + u
            one = tile[i:i + 1] if isinstance(i, int) else tile[bass.ds(i, 1)]
            sp.dma_start(dst[:, u], one.rearrange("o p w -> (o p) w")[:, cols]).then_inc(mig[u][name], 16)

        def load_pair(k, n):
            for u in range(n):
                after_tile(sp, "m_x", k, u, 0)
                load_tile(m_in, slice(0, D), "m_loaded", k, u)
            for u in range(n):
                after_tile(sp, "m_stored", k, u, 0)
                load_tile(m_skip, slice(D, RW), "m_skip", k, u)

        for slot in range(RING):
            sp.wait_ge(rows_placed[slot], 16 * (NT // RING))
        load_pair(0, 2)

        def step(k, n, nxt):
            load_pair(k + 1, nxt)

        tile_steps(sp, step)

    @block.scalar
    def _(act):
        copy = nc.scalar.copy

        def load_rows_back():
            phase1_over(act)
            act.wait_ge(s_ids, 16)
            tiles = rows_lin.ap().rearrange("(n p) w -> n p w", p=P)
            for n in range(NT):
                if n >= RING:
                    act.wait_ge(rows_placed[n % RING], 16 * (n // RING))
                act.dma_start(ring[:, n % RING], tiles[n]).then_inc(rows_back[n % RING], 16)

        act.wait_ge(s_setup_dma, ALL_LOADED)
        nc.scalar.activation(lam[:, 1:2], lam[:, 0:1], ACT.Exp, scale=-1.0).then_inc(s_lam, 1)
        act.wait_ge(s_eb, 4)
        nc.scalar.activation(eb[:].rearrange("p h n -> p (h n)"), eb[:].rearrange("p h n -> p (h n)"),
                             ACT.Exp).then_inc(s_eb, 1)

        def evacuate(it, job, dst, view=None):
            src = full(act, it, job)[:]
            copy(dst, src if view is None else view(src)).then_inc(e_sem(job), 1)

        def turn(it):
            A, Bb, Dd, Cc = (st in it.stages for st in "ABDC")
            a, b, dd, c = (it.batch(st) for st in "ABDC")
            if A:
                evacuate(it, "A.xn", a_xnT[:].rearrange("p c s -> p (c s)"))
            if Bb:
                evacuate(it, "B.ctx", b_ctxT[:].rearrange("p c s -> p (c s)"))
            if Dd:
                evacuate(it, "D.q", b_zT[:].rearrange("p c s -> p (c s)"))
            if A:
                for t in range(T):
                    ps = full(act, it, f"A.qk{t}")
                    nc.scalar.activation(a_sq[:, t], ps[:], ACT.Square).then_inc(sig["a_squares"], 1)
            if Bb:
                for job, dst in (("B.k", b_kh), ("B.q_", b_qh)):
                    if job == "B.q_":
                        evacuate(it, "B.x", b_xT[:].rearrange("p c s -> p (c s)"))
                    ps = full(act, it, job)
                    copy(dst[:].rearrange("p c s -> p (c s)"), ps[:]).then_inc(sig["b_hi"], 1)
            if A:
                ps = full(act, it, "A.v")[:].rearrange("p (t i h d) -> p t i h d", t=T, h=2, d=D0)
                copy(a_v[:, :, 0, :, 0:D0], ps[:, :, :, 0])
                copy(a_v[:, :, 1, :, D0:], ps[:, :, :, 1]).then_inc(e_sem("A.v"), 1)

            def hidden(n):
                ps = full(act, it, f"D.h{n}")
                nc.scalar.activation(b_hT[:, 2 * n], ps[:, 0:S], ACT.Relu, bias=b11[:, 2 * n:2 * n + 1])
                nc.scalar.activation(b_hT[:, 2 * n + 1], ps[:, S:], ACT.Relu,
                                     bias=b11[:, 2 * n + 1:2 * n + 2]).then_inc(e_sem(f"D.h{n}"), 1)

            if Dd:
                hidden(0)
            if Bb:
                evacuate(it, "B.v", b_v[:].rearrange("p t n -> p (t n)"))
            if A:
                if not isinstance(a, int) or a > 0:
                    after(act, "b_mv", a - 1)
                copy(x_keep[:], x_in[:]).then_inc(sig["a_kept"], 1)
                for t in range(T):
                    taken(act, it, f"A.qk{t}")
                    hat = a_hat[:, t].rearrange("p (h o d) -> p h o d", o=1, d=D0)
                    for lo, hi, slots in ((0, H0, slice(0, 4, 2)), (H0, 2 * H0, slice(0, 2))):
                        copy(a_split[:, t, lo:hi, slots, :],
                             hat[:, lo:hi].to_broadcast([P, H0, 2, D0])).then_inc(sig["a_hi"], 1)
            if Dd:
                hidden(1)
                hidden(2)
            for t in range(T):
                if A:
                    evacuate(it, f"A.k{t}", a_kT[:, :, tok(t)],
                             lambda x: x.bitcast(F16).rearrange("p (g s) -> p g s", s=P))
                if Dd and t == 0:
                    hidden(3)
            if Bb:
                evacuate(it, "B.max", b_nmT[:].rearrange("p c s -> p (c s)"))
            if Dd:
                if Cc:
                    after(act, "c_x2", c)
                copy(x1_keep2[:], x1_keep[:]).then_inc(sig["x1_kept2"], 1)
            if Bb:
                if Dd:
                    after(act, "x1_kept2", dd)
                copy(x1_keep[:], x1[:]).then_inc(sig["x1_kept"], 1)
            for what, st, n in PLAN:
                if st not in it.stages:
                    continue
                if what == "distances":
                    after(act, "c_rows", c, 1)
                    for t in range(T):
                        nc.scalar.activation(c_xnT[:, t], c_rows[:, t, 0:D], ACT.Square,
                                             accum_out=c_nx[:, t:t + 1]).then_inc(sig["c_nx"], 1)
                    after(act, "c_nx", c)
                    evacuate(it, "C.xn", c_xnT[:].rearrange("p c s -> p (c s)"))
                if what != "score":
                    continue
                ps = full(act, it, f"{st}.s{n}")
                if st == "A":
                    after(act, "a_p_used", a, n // GROUP + 1 - NPA // GROUP)
                    nc.scalar.activation(a_p[:, n % NPA], ps[:, 0:SCOLS], ACT.Exp).then_inc(e_sem(f"A.s{n}"), 1)
                else:
                    before = b * (H1 // GROUP) + (n - NPB) // GROUP + 1 if n >= NPB else b * (H1 // GROUP)
                    wait(act, sig["b_p_used"], before)
                    nc.scalar.activation(b_p[:, n % NPB].rearrange("p t s -> p (t s)"), ps[:],
                                         ACT.Exp).then_inc(e_sem(f"B.s{n}"), 1)
            if A:
                taken(act, it, "A.wo")
                for t in range(T):
                    nc.scalar.activation(a_hT[:, t], a_xl[:, t], ACT.Square,
                                         accum_out=a_ms[:, t:t + 1]).then_inc(sig["a_ms"], 1)
                evacuate(it, "A.z", a_xnT[:].rearrange("p c s -> p (c s)"))
                for n in range(4):
                    ps = full(act, it, f"A.h{n}")
                    nc.scalar.activation(a_hT[:, 2 * n:2 * n + 2].rearrange("p j s -> p (j s)"), ps[:],
                                         ACT.Relu).then_inc(e_sem(f"A.h{n}"), 1)
        act.wait_ge(s_zero, 16)
        each(act, turn)
        load_rows_back()

        def transposed(k, u):
            after_tile(act, "m_x", k, u)
            copy(m_xT[:, u].rearrange("p c s -> p (c s)"), bank[u][:, 0:C * P]).then_inc(mig[u]["m_xT"], 1)

        def step(k, n, nxt):
            for u in range(n):
                after_tile(act, "m_up", k, u)
                nc.scalar.activation(m_sg[:, u], bank[3 + 2 * u][:], ACT.Silu).then_inc(mig[u]["m_silu"], 1)
            for u in range(nxt):
                transposed(k + 1, u)
            for u in range(n):
                after_tile(act, "m_ht", k, u)
                copy(m_hT[:, u].rearrange("p j s -> p (j s)"), bank[6][:]).then_inc(mig[u]["m_hT"], 1)

        transposed(0, 0)
        transposed(0, 1)
        tile_steps(act, step)

    @block.gpsimd
    def _(pool):
        done = [0]

        def const(ins):
            ins.then_inc(s_const, 1)
            done[0] += 1

        const(pool.memset(ident[:], 0.0))
        const(pool.memset(ident16[:], 0.0))
        const(pool.memset(ones[:], 1.0))
        const(pool.memset(halves[:], 0.0))
        pool.wait_ge(s_const, 4)
        for m in (ident, ident16):
            const(pool.affine_select(out=m[:], in_=m[:], compare_op=ALU.not_equal, fill=1.0, base=0,
                                     pattern=[[-1, P]], channel_multiplier=1))
        const(pool.affine_select(out=tri[:], in_=ones[:], compare_op=ALU.is_gt, fill=0.0, base=0,
                                 pattern=[[1, P]], channel_multiplier=-1))
        const(pool.memset(halves[:, 0, 0:D0], 1.0))
        const(pool.memset(halves[:, 1, D0:], 1.0))
        const(pool.tensor_copy(ones_r[:], ones[:]))
        const(pool.memset(mhalf[:], -0.5))
        const(pool.memset(a_v[:, :, 0, :, D0:], 0.0))
        const(pool.memset(a_v[:, :, 1, :, 0:D0], 0.0))
        const(pool.memset(b_nm[:], 0.0))
        const(pool.memset(zrow[:, 0:2 * D], 0.0))
        const(pool.iota(idcol[:], pattern=[[P, NT]], base=0, channel_multiplier=1))
        assert done[0] == CONSTS
        pool.wait_ge(s_eb, 5)
        pool.affine_select(out=eb[:, :, 0:S], in_=eb[:, :, 0:S], compare_op=ALU.is_gt, fill=0.0, base=0,
                           pattern=[[0, H0], [1, S]], channel_multiplier=-1).then_inc(s_eb, 1)
        pool.affine_select(out=eb[:, :, S:], in_=eb[:, :, S:], compare_op=ALU.is_gt, fill=0.0, base=0,
                           pattern=[[0, H0], [1, P]], channel_multiplier=-1).then_inc(s_eb, 1)
        pool.wait_ge(s_eb, 7)
        pool.memset(eb[:, :, 0:1], 1.0).then_inc(s_eb, 1)

        def power(out, in_, name):
            pool.tensor_tensor(out, in_, mhalf[:, 0:out.shape[-1]], ALU.pow).then_inc(sig[name], 1)

        def layer_then_rms(mv, sc, name, batch, eps):
            var = mv[:, :, 1]
            pool.tensor_scalar(sc[:, 0], var, eps, None, ALU.add).then_inc(sig[name], 1)
            after(pool, name, batch, 1)
            power(sc[:, 1], sc[:, 0], name)
            after(pool, name, batch, 2)
            pool.tensor_tensor(sc[:, 2], var, sc[:, 1], ALU.mult).then_inc(sig[name], 1)
            after(pool, name, batch, 3)
            pool.tensor_tensor(sc[:, 3], sc[:, 2], sc[:, 1], ALU.mult).then_inc(sig[name], 1)
            after(pool, name, batch, 4)
            pool.tensor_scalar(sc[:, 4], sc[:, 3], 1e-6, None, ALU.add).then_inc(sig[name], 1)
            after(pool, name, batch, 5)
            power(sc[:, 5], sc[:, 4], name)
            after(pool, name, batch, 6)
            pool.tensor_tensor(sc[:, 6], sc[:, 5], sc[:, 1], ALU.mult).then_inc(sig[name], 1)

        def layer(mv, rs, name, batch, eps):
            pool.tensor_scalar(rs[:, 0], mv[:, :, 1], eps, None, ALU.add).then_inc(sig[name], 1)
            after(pool, name, batch, 1)
            power(rs[:, 1], rs[:, 0], name)

        def turn(it):
            A, Bb, Dd, Cc = (st in it.stages for st in "ABDC")
            a, b, dd, c = (it.batch(st) for st in "ABDC")
            if Cc:
                after(pool, "c_mv", c)
                layer(c_mv, c_rs, "c_norm", c, 1e-5)
                after(pool, "c_n", c)
                pool.tensor_tensor(c_n[:], c_n[:], over_t(vecs[:, G2]), ALU.mult).then_inc(sig["c_gain"], 1)
                after(pool, "c_gain", c)
                pool.tensor_tensor(c_n[:], c_n[:], over_t(vecs[:, B2]), ALU.add).then_inc(sig["c_out"], 1)
                after(pool, "c_out", c)
                after(pool, "c_stored", c - 1)
                pool.tensor_tensor(c_x2, x1_keep2[:], c_n[:], ALU.add).then_inc(sig["c_x2"], 1)
            if Dd:
                taken(pool, it, "D.q")
                pool.tensor_tensor(b_q[:], b_q[:], over_t(vecs[:, FB2]), ALU.add).then_inc(sig["b_qb2"], 1)
            if Cc:
                after(pool, "c_mv2", c)
                layer_then_rms(c_mv2, c_sc, "c_norms", c, 1e-5)
            if A:
                for t in range(T):
                    after(pool, "a_hi", a, 2 * t + 2)
                    hat = a_hat[:, t].rearrange("p (h d) -> p h d", d=D0)
                    for slot in (2, 3):
                        ins = pool.tensor_tensor(a_split[:, t, H0:, slot, :], hat[:, H0:], a_split[:, t, H0:, 0, :],
                                                 ALU.subtract)
                    ins.then_inc(sig["a_lo_k"], 1)
            if Cc:
                after(pool, "c_xs", c)
                pool.tensor_tensor(c_rows[:, :, 0:D], c_rows[:, :, 0:D], over_t(vecs[:, FSC]),
                                   ALU.mult).then_inc(sig["c_rows"], 1)
                after(pool, "c_xl", c)
                pool.tensor_tensor(c_x2, c_x2, c_n[:], ALU.add).then_inc(sig["c_rows"], 1)
            if A:
                after(pool, "a_ms", a)
                pool.tensor_scalar(a_rz[:, 0], a_ms[:], 1.0 / D, 1e-6, ALU.mult, ALU.add).then_inc(sig["a_rz"], 1)
                after(pool, "a_rz", a, 1)
                power(a_rz[:, 1], a_rz[:, 0], "a_rz")
                after(pool, "a_kept", a)
                pool.tensor_tensor(x_keep[:], x_keep[:], a_xl[:], ALU.add).then_inc(sig["a_xy"], 1)
            if Bb:
                after(pool, "b_mv2", b)
                layer(b_mv2, b_rs2, "b_norm2", b, 1e-5)
            if "P" in it.stages:
                p = it.batch("P")
                after(pool, "a_mv", p)
                layer_then_rms(a_mv, a_sc, "a_norms", p, 1e-5)
            if Bb:
                after(pool, "b_n", b)
                pool.tensor_tensor(b_q[:], b_q[:], over_t(vecs[:, G1]), ALU.mult).then_inc(sig["b_gain"], 1)
                after(pool, "b_gain", b)
                pool.tensor_tensor(b_q[:], b_q[:], over_t(vecs[:, B1]), ALU.add).then_inc(sig["b_q"], 1)
            if A:
                after(pool, "b_mv", a)
                layer(b_mv, b_rs, "b_norm", a, 1e-5)

        pool.wait_ge(s_setup_dma, ALL_LOADED)
        pool.wait_ge(s_sc, 2)
        each(pool, turn)

        phase1_over(pool)
        pool.iota(io_e[:], pattern=[[1, E]], base=0, channel_multiplier=0,
                  allow_small_or_imprecise_dtypes=True).then_inc(s_iota, 1)
        pool.iota(io_t[:], pattern=[[P, NT]], base=0, channel_multiplier=0,
                  allow_small_or_imprecise_dtypes=True).then_inc(s_iota, 1)
        pool.iota(io_i[:], pattern=[[1, TILES_MAX]], base=0, channel_multiplier=0,
                  allow_small_or_imprecise_dtypes=True).then_inc(s_iota, 1)
        pool.memset(ones_nt[:], 1.0).then_inc(s_iota, 1)
        pool.wait_ge(s_zero, 16)
        pool.wait_ge(s_route, ROUTE_POS)
        for n in range(NT):
            pool.wait_ge(rows_back[n % RING], 16 * (n // RING + 1))
            pool.indirect_dma_start(out=rows_srt.ap(), out_offset=bass.IndirectOffsetOnAxis(ap=pos[:, n:n + 1], axis=0),
                                    in_=ring[:, n % RING], in_offset=None).then_inc(rows_placed[n % RING], 16)

        def step(k, n, nxt):
            for u in range(n):
                after_tile(pool, "m_out", k, u)
                pool.indirect_dma_start(
                    out=d["out"], out_offset=bass.IndirectOffsetOnAxis(ap=m_skip[:, u, D:].bitcast(U32), axis=0),
                    in_=m_out[:, u], in_offset=None, bounds_check=B * S - 1, oob_is_err=False,
                ).then_inc(mig[u]["m_stored"], 16)

        tile_steps(pool, step)
        for u in range(2):
            pool.wait_ge(mig[u]["m_stored"], 16 * ((TILES_MAX + 1 - u) // 2))

    @block.vector
    def _(dve):
        tt, ts = dve.tensor_tensor, dve.tensor_scalar

        dve.memset(bd, 0.0).then_inc(s_bd, 1)
        dve.memset(zrow[:, 2 * D:].bitcast(I32), B * S).then_inc(s_sc, 1)
        dve.wait_ge(s_setup_dma, ALL_LOADED)
        dve.wait_ge(s_bd, 1)
        dve.wait_ge(s_pe_setup, 1)
        ts(bd[:, P:P + S], bank[0][0:H0, 0:S], sc16[:, 0:1], None, ALU.mult).then_inc(s_bd, 1)
        dve.wait_ge(s_bd, 2)
        dve.tensor_tensor_scan(bmax[:, 1:S], bd[:, P + 1:P + S], bd[:, P + 1:P + S], -3.0e38, ALU.max,
                               ALU.max).then_inc(s_bmax, 1)
        dve.tensor_copy(bmax[:, 0:1], bd[:, P + 1:P + 2]).then_inc(s_bmax, 1)
        for c in range(C):
            for w, n in ((w0qk, 0), (w0v, 0), (w01, 1)):
                ts(w[:, c], w[:, c], ln0[:, n, c:c + 1], None, ALU.mult).then_inc(s_w, 1)
        ts(w1q[:], w1q[:], float(D1) ** -0.5, None, ALU.mult).then_inc(s_w, 1)
        dve.memset(qscale[:, :, H0:], 1.0).then_inc(s_sc, 1)
        dve.memset(qscale[0:1, 0, 0:H0], 0.0).then_inc(s_sc, 1)
        dve.wait_ge(s_lam, 1)
        ts(lam[:, 1:2], lam[:, 1:2], 1.0, None, ALU.add).then_inc(s_lam, 1)
        dve.wait_ge(s_lam, 2)
        dve.reciprocal(lam[:, 2:3], lam[:, 1:2]).then_inc(s_lam, 1)
        dve.wait_ge(s_lam, 3)
        ts(lam[:, 0:1], lam[:, 2:3], -1.0, 1.0, ALU.mult, ALU.add).then_inc(s_lam, 1)
        dve.wait_ge(s_lam, 4)
        ts(w1o[:], w1o[:], lam[:, 0:1], None, ALU.mult).then_inc(s_w, 1)
        dve.wait_ge(s_pe_setup, 2)
        ts(cent_t[:].rearrange("p c e -> p (c e)"), bank[1][:, 0:C * E], 2.0, None, ALU.mult).then_inc(s_cent, 1)
        dve.wait_ge(s_cent, 1)
        tt(cent_sq[:], cent_t[:], cent_t[:], ALU.mult).then_inc(s_cent, 1)
        dve.wait_ge(s_pe_setup, 3)
        ts(cnorm[:], bank[2][:, 0:E], 0.25, None, ALU.mult).then_inc(s_cent, 1)
        for half in range(2):
            dve.wait_ge(s_tp, 16 * (3 + half))
            heads = slice(8 * half, 8 * half + 8)
            tt(eb[:, heads, 0:S], eb[:, heads, 0:S], bias_b[:], ALU.subtract).then_inc(s_eb, 1)
            tt(eb[:, heads, S:], eb[:, heads, S:], bias_b[:, :, P:], ALU.subtract).then_inc(s_eb, 1)
        dve.wait_ge(s_cent, 3)

        def stats(x, st, mv, s_stats, s_mv, batch):
            for t in range(T):
                dve.bn_stats(st[:, t], x[:, t]).then_inc(sig[s_stats], 1)
            for t in range(T):
                after(dve, s_stats, batch, t + 1, lone=True)
                dve.bn_aggr(mv[:, t], st[:, t]).then_inc(sig[s_mv], 1)

        def shifted(out, x, mv, scale, name):
            for t in range(T):
                ts(out[:, t], x[:, t], mv[:, t, 0:1], scale[:, t:t + 1], ALU.subtract,
                   ALU.mult).then_inc(sig[name], 1)

        def normalised(it, st, n, yT):
            ps = bank[BANK_OF[f"{st}.o{n}"]]
            used, name = ("a_p_used", "a_rec") if st == "A" else ("b_p_used", "b_rec")
            batch = it.batch(st)
            after(dve, used, batch, 2 * n + 2 if st == "A" else n + 1)
            r = rec[:, n + C * (st == "B")]
            dve.reciprocal(r, ps[:, S:]).then_inc(sig[name], 1)
            after(dve, name, batch, n + 1)
            tt(yT[:, n], ps[:, 0:S], r, ALU.mult).then_inc(e_sem(f"{st}.o{n}"), 1)

        def turn(it):
            A, Bb, Dd, Cc = (st in it.stages for st in "ABDC")
            a, b, dd, c = (it.batch(st) for st in "ABDC")
            if Cc:
                after(dve, "c_norm", c)
                shifted(c_n, b_f, c_mv, c_rs[:, 1], "c_n")

            def nearest():
                after(dve, "c_nx", c)
                for t in range(T):
                    ts(c_tmp[:, t], cnorm[:], c_nx[:, t:t + 1], None, ALU.add).then_inc(sig["c_tmp"], 1)
                after(dve, "c_tmp", c)
                ps = full(dve, it, "C.dist")
                tt(c_nd[:], ps[:, 0:T * E].rearrange("p (t e) -> p t e", e=E), c_tmp[:],
                   ALU.subtract).then_inc(e_sem("C.dist"), 1)
                taken(dve, it, "C.dist", lone=True)
                for t in range(T):
                    dve.max(c_mx[:, t], c_nd[:, t]).then_inc(sig["c_max8"], 1)
                for t in range(T):
                    after(dve, "c_max8", c, t + 1, lone=True)
                    dve.max_index(c_ix[:, t], c_mx[:, t], c_nd[:, t]).then_inc(sig["c_index"], 1)
                after(dve, "c_index", c)
                where = slice(T * c, T * c + T) if isinstance(c, int) else bass.ds(T * c, T)
                dve.tensor_copy(expert_of[:, where], c_ix[:, :, 0]).then_inc(sig["c_expert"], 1)

            def low(job, n, lo, hi):
                after(dve, "b_hi", b, n)
                tt(lo[:].rearrange("p c s -> p (c s)"), bank[BANK_OF[job]][:],
                   hi[:].bitcast(F32).rearrange("p c s -> p (c s)"), ALU.subtract).then_inc(e_sem(job), 1)

            def inverse_lengths(a):
                x, xh, y, u, w = (a_nw[:, n] for n in range(5))
                step = [0]

                def link(ins, ready=True):
                    ins.then_inc(sig["a_rn"], 1)
                    step[0] += 1
                    if ready:
                        after(dve, "a_rn", a, step[0])

                after(dve, "a_sumsq", a)
                link(ts(x, a_ss[:].rearrange("p t h -> p (t h)"), 1e-6, None, ALU.add))
                link(ts(xh, x, -0.5, None, ALU.mult), False)
                link(ts(u.bitcast(I32), x.bitcast(I32), 1, None, ALU.logical_shift_right))
                link(ts(y.bitcast(I32), u.bitcast(I32), -1.0, float(0x5f3759df), ALU.mult, ALU.add))
                for _ in range(3):
                    link(tt(u, xh, y, ALU.mult))
                    link(tt(w, u, y, ALU.mult))
                    link(dve.scalar_tensor_tensor(y, w, 1.5, y, ALU.add, ALU.mult))
                link(tt(a_rn[:].rearrange("p t h -> p (t h)"), y, qscale[:].rearrange("p t h -> p (t h)"),
                        ALU.mult), False)

            if A:
                for t in range(T):
                    after(dve, "a_squares", a, t + 1)
                    dve.tensor_reduce(a_ss[:, t], a_sq[:, t].rearrange("p (h d) -> p h d", d=D0), AX_X,
                                      ALU.add).then_inc(sig["a_sumsq"], 1)
                inverse_lengths(a)
            if Bb:
                low("B.k", 1, b_kl, b_kh)
                low("B.q_", 2, b_ql, b_qh)
            if A:
                after(dve, "a_rn", a)
                for t in range(T):
                    ps = bank[BANK_OF[f"A.qk{t}"]]
                    tt(a_hat[:, t].rearrange("p (h d) -> p h d", d=D0), ps[:].rearrange("p (h d) -> p h d", d=D0),
                       bc(a_rn[:, t], D0), ALU.mult).then_inc(e_sem(f"A.qk{t}"), 1)
            if Cc:
                after(dve, "c_x2", c)
                stats(c_x2, c_st, c_mv2, "c_stats2", "c_mv2", c)
            for t in range(T):
                if Bb:
                    for j in range(4):
                        ps = full(dve, it, f"B.m{4 * t + j}")
                        dve.tensor_reduce(b_nm[:, t, :, j, 0:1], ps[:].rearrange("p (m s) -> p m s", s=S), AX_X,
                                          ALU.max, negate=True).then_inc(e_sem(f"B.m{4 * t + j}"), 1)
                if A:
                    after(dve, "a_hi", a, 2 * t + 1)
                    hat = a_hat[:, t].rearrange("p (h o d) -> p h o d", o=1, d=D0)[:, 0:H0]
                    tt(a_split[:, t, 0:H0, 1::2, :], hat.to_broadcast([P, H0, 2, D0]),
                       a_split[:, t, 0:H0, 0:1, :].to_broadcast([P, H0, 2, D0]), ALU.subtract
                       ).then_inc(sig["a_lo_q"], 1)
            if Cc:
                after(dve, "c_norms", c)
                shifted(c_rows[:, :, 0:D], c_x2, c_mv2, c_sc[:, 6], "c_xs")
                shifted(c_n, c_x2, c_mv2, c_sc[:, 1], "c_xl")
            if A:
                for t in range(T):
                    ps = full(dve, it, f"A.q{t}")
                    dve.tensor_copy(a_qT[:, :, tok(t)], ps[:].bitcast(F16).rearrange("p (g s) -> p g s", s=P)
                                    ).then_inc(e_sem(f"A.q{t}"), 1)
            for what, st, n in PLAN:
                if st not in it.stages:
                    continue
                if what == "score" and st == "A":
                    taken(dve, it, f"A.s{n}")
                    tt(a_p[:, n % NPA], a_p[:, n % NPA], eb[:, A_HEADS[n]], ALU.mult).then_inc(sig["a_p"], 1)
                if what == "expert":
                    nearest()
                if what == "f":
                    ps = full(dve, it, "D.out")
                    after(dve, "b_qb2", dd)
                    if Cc:
                        after(dve, "c_rows", c)
                    tt(b_f[:], ps[:].rearrange("p (t n) -> p t n", n=D), b_q[:], ALU.add).then_inc(e_sem("D.out"), 1)
                    taken(dve, it, "D.out")
                    stats(b_f, c_st, c_mv, "c_stats", "c_mv", dd)
                if what == "norm":
                    normalised(it, st, n, a_yT if st == "A" else b_yT)
            if A:
                normalised(it, "A", 1, a_yT)
            if Bb:
                normalised(it, "B", 1, b_yT)
            if A:
                ps = full(dve, it, "A.wo")
                tt(a_xl[:], ps[:].rearrange("p (t n) -> p t n", n=D), a_xl[:], ALU.add).then_inc(e_sem("A.wo"), 1)
                after(dve, "a_rz", a)
                for t in range(T):
                    ts(a_xn[:, t], a_xl[:, t], a_rz[:, 1, t:t + 1], None, ALU.mult).then_inc(sig["a_z"], 1)
            if Bb:
                ps = full(dve, it, "B.wo")
                tt(b_q[:], ps[:].rearrange("p (t n) -> p t n", n=D), b_xl[:], ALU.add).then_inc(e_sem("B.wo"), 1)
                taken(dve, it, "B.wo")
                stats(b_q, b_st, b_mv2, "b_stats2", "b_mv2", b)
            if "P" in it.stages:
                p = it.batch("P")
                after(dve, "a_loaded", p)
                stats(x_in, a_st, a_mv, "a_stats", "a_mv", p)
            if Bb:
                after(dve, "b_norm2", b)
                shifted(b_q, b_q, b_mv2, b_rs2[:, 1], "b_n")
            if "P" in it.stages:
                after(dve, "a_norms", p)
                if A:
                    taken(dve, it, "A.z")
                    after(dve, "a_xy", a)
                shifted(a_xn, x_in, a_mv, a_sc[:, 6], "a_xn")
                shifted(a_xl, x_in, a_mv, a_sc[:, 1], "a_xl")
            if A:
                ps = full(dve, it, "A.out")
                after(dve, "a_xy", a)
                if Bb:
                    after(dve, "x1_kept", b)
                tt(x1[:], ps[:].rearrange("p (t n) -> p t n", n=D), x_keep[:], ALU.add).then_inc(e_sem("A.out"), 1)
                taken(dve, it, "A.out")
                stats(x1, b_st, b_mv, "b_stats", "b_mv", a)
                after(dve, "b_norm", a)
                shifted(b_xl, x1, b_mv, b_rs[:, 1], "b_xl")
        dve.wait_ge(s_eb, 8)
        dve.wait_ge(s_const, CONSTS)
        each(dve, turn)

        phase1_over(dve)
        dve.wait_ge(s_iota, 4)
        link = [0]

        def chain(ins):
            ins.then_inc(s_route, 1)
            link[0] += 1
            dve.wait_ge(s_route, link[0])

        def over(ap, n, m):
            return ap.unsqueeze(1).to_broadcast([P, n, m])

        chain(tt(oh[:], bc(expert_of[:], E), over(io_e[:], NT, E), ALU.is_equal))
        dve.wait_ge(s_pp, 1)
        chain(dve.tensor_copy(r_tot[:].rearrange("p n e -> p (n e)"), bank[1][:, 0:NT * E]))
        for e in range(E):
            ins = dve.tensor_tensor_scan(r_cum[:, :, e], ones_nt[:], r_tot[:, :, e], 0.0, ALU.mult, ALU.add)
            if e < E - 1:
                ins.then_inc(s_route, 1)
                link[0] += 1
        chain(ins)
        chain(tt(r_cmp[:], bc(r_cum[:, NT - 1, :], NT), over(io_t[:], E, NT), ALU.is_gt))
        chain(dve.tensor_reduce(r_nt[:], r_cmp[:], AX_X, ALU.add))
        chain(dve.tensor_tensor_scan(r_ct[:], ones_nt[:, 0:E], r_nt[:], 0.0, ALU.mult, ALU.add))
        chain(tt(r_base[:], r_ct[:], r_nt[:], ALU.subtract))
        chain(ts(r_base[:], r_base[:], float(P), None, ALU.mult))
        chain(tt(r_a[:], r_cum[:], r_tot[:], ALU.subtract))
        chain(tt(r_a[:], r_a[:], bank[0][:, 0:NT * E].rearrange("p (n e) -> p n e", e=E), ALU.add))
        chain(tt(r_a[:], r_a[:], over(r_base[:], NT, E), ALU.add))
        chain(tt(r_a[:], r_a[:], oh[:], ALU.mult))
        chain(dve.tensor_reduce(r_posf[:], r_a[:], AX_X, ALU.add))
        chain(dve.tensor_copy(pos[:], r_posf[:]))
        assert link[0] == ROUTE_POS
        chain(tt(r_cmp2[:], bc(io_i[:], E), over(r_ct[:], TILES_MAX, E), ALU.is_ge))
        chain(dve.tensor_reduce(r_te[:], r_cmp2[:], AX_X, ALU.add))
        chain(ts(tile_expert[:, 0:TILES_MAX], r_te[:], float(E - 1), None, ALU.min))
        assert link[0] == ROUTE_ALL

        def step(k, n, nxt):
            for u in range(n):
                after_tile(dve, "m_silu", k, u)
                tt(m_h[:, u], bank[2 + 2 * u][:], m_sg[:, u], ALU.mult).then_inc(mig[u]["m_h"], 1)
            for u in range(n):
                after_tile(dve, "m_down", k, u)
                after_tile(dve, "m_stored", k, u, 0)
                after_tile(dve, "m_skip", k, u)
                tt(m_out[:, u], bank[7][:, 0:D], m_skip[:, u, 0:D], ALU.add).then_inc(mig[u]["m_out"], 1)

        tile_steps(dve, step)

    @block.tensor
    def _(pe):
        mm = nc.tensor.matmul

        def product(out, lhsT, rhs, first=True, last=True, **kw):
            return mm(out, lhsT=lhsT, rhs=rhs, start=first, stop=last, **kw)

        pe.wait_ge(s_setup_dma, ALL_LOADED)
        pe.wait_ge(s_const, CONSTS)
        product(bank[0][0:H0, 0:S], relb[:], onehot).then_inc(s_pe_setup, 1)
        for c in range(C):
            ins = nc.tensor.transpose(bank[1][:, c * E:(c + 1) * E], cent[:, c * P:(c + 1) * P], ident[0:E, 0:E])
        ins.then_inc(s_pe_setup, 1)
        pe.wait_ge(s_cent, 2)
        for c in range(C):
            ins = product(bank[2][:, 0:E], ones[:], cent_sq[:, c], c == 0, c == C - 1)
        ins.then_inc(s_pe_setup, 1)
        pe.wait_ge(s_w, 3 * C + 2)
        pe.wait_ge(s_cent, 3)
        pe.wait_ge(s_eb, 4)

        def transposes(it, job, x):
            ps = claim(pe, it, job)
            for c in range(C):
                for t in range(T):
                    ins = nc.tensor.transpose(ps[:, c * S + t * P:c * S + (t + 1) * P], x[:, t, c * P:(c + 1) * P],
                                              ident[:])
            ins.then_inc(f_sem(job), 1)

        def rows_out(it, job, xT, w, chunks=C):
            ps = claim(pe, it, job)
            for t in range(T):
                for c in range(chunks):
                    ins = product(ps[:, t * D:(t + 1) * D], xT[:, c, tok(t)], w[:, c, :], c == 0, c == chunks - 1)
            ins.then_inc(f_sem(job), 1)

        def cols_out(it, job, xT, w, first_chunk):
            ps = claim(pe, it, job)
            for m in range(2):
                for c in range(C):
                    at = (first_chunk + m) * P
                    ins = product(ps[:, m * S:(m + 1) * S], w[:, c, at:at + P], xT[:, c, :], c == 0, c == C - 1)
            ins.then_inc(f_sem(job), 1)

        def scores(it, st, n):
            job = f"{st}.s{n}"
            ps = claim(pe, it, job)
            if st == "A":
                h = A_HEADS[n]
                r, g = 64 * (h % 2), h // 2
                product(ps[:, 0:S], a_kT[r:r + 64, g, 0:P], a_qT[r:r + 64, g, :])
                product(ps[:, S:SCOLS], a_kT[r:r + 64, g, P:], a_qT[r:r + 64, g, P:]).then_inc(f_sem(job), 1)
            else:
                r, m = 32 * (n % 4), n // 4
                for kt in range(T):
                    out = ps[:, kt * S:(kt + 1) * S]
                    product(out, ones_r[r:r + 1, :], b_nmT[r:r + 1, m, :], True, False)
                    parts = ((b_kh, b_qh), (b_kh, b_ql), (b_kl, b_qh))
                    for i, (k, q) in enumerate(parts):
                        ins = product(out, k[r:r + 32, m, tok(kt)], q[r:r + 32, m, :], False, i == len(parts) - 1)
                ins.then_inc(f_sem(job), 1)

        def weigh(it, st, n):
            if st == "A":
                c_, par = n // 2, n % 2
                job = f"A.o{c_}"
                ps = claim(pe, it, job) if par == 0 else bank[BANK_OF[job]]
                after(pe, "a_p", it.batch("A"), GROUP * (n + 1))
                slot = GROUP * n % NPA
                ones_half = halves[:, par]
                for kt, queries, cols in ((0, slice(0, S), slice(0, S)), (1, slice(P, S), slice(S, SCOLS))):
                    for half in range(2):
                        at = slice(half * S + queries.start, half * S + queries.stop)
                        for j in range(GROUP):
                            lhs = ones_half if half else a_v[:, kt, par, GROUP * c_ + j]
                            ins = product(ps[32 * j:32 * j + 32, at], lhs, a_p[:, slot + j, cols],
                                          par == 0 and kt == 0 and half == 0, False, skip_group_check=True,
                                          tile_position=(0, 32 * j))
                ins.then_inc(sig["a_p_used"], 1)
                if par == 0:
                    for p_ in range(2):
                        v = a_v[:, 1, p_, GROUP * c_:GROUP * (c_ + 1)].rearrange("p j d -> p (j d)")
                        product(ps[:, 0:1], v, ones[:, 0:1], False, False, skip_group_check=True)
                    product(ps[:, S:S + 1], ones[:], ones[:, 0:1], False, False, skip_group_check=True)
            else:
                job = f"B.o{n}"
                ps = claim(pe, it, job)
                taken(pe, it, f"B.s{GROUP * n + GROUP - 1}")
                for kt in range(T):
                    for half in range(2):
                        for j in range(GROUP):
                            h = GROUP * n + j
                            lhs = ones[:, 0:D1] if half else b_v[:, kt, h * D1:(h + 1) * D1]
                            ins = product(ps[32 * j:32 * j + 32, half * S:(half + 1) * S], lhs, b_p[:, h % NPB, kt],
                                          kt == 0 and half == 0, False, skip_group_check=True,
                                          tile_position=(0, 32 * j))
                ins.then_inc(sig["b_p_used"], 1)

        def turn(it):
            A, Bb, Dd, Cc = (st in it.stages for st in "ABDC")
            a, b, dd, c = (it.batch(st) for st in "ABDC")
            if A:
                after(pe, "a_xn", a)
                transposes(it, "A.xn", a_xn)
            if Bb:
                after(pe, "b_loaded", b)
                transposes(it, "B.ctx", c_in)
            if Dd:
                after(pe, "b_q", dd)
                transposes(it, "D.q", b_q)
            if A:
                taken(pe, it, "A.xn")
                for t in range(T):
                    ps = claim(pe, it, f"A.qk{t}")
                    for c_ in range(C):
                        ins = product(ps[:], a_xnT[:, c_, tok(t)], w0qk[:, c_, :], c_ == 0, c_ == C - 1)
                    ins.then_inc(f_sem(f"A.qk{t}"), 1)
            if Bb:
                taken(pe, it, "B.ctx")
                cols_out(it, "B.k", b_ctxT, w1k, 0)
                after(pe, "b_xl", b)
                transposes(it, "B.x", b_xl)
                taken(pe, it, "B.x")
                cols_out(it, "B.q_", b_xT, w1q, 0)

            def rough(jobs):
                for n in jobs:
                    t, r = n // 4, 32 * (n % 4)
                    ps = claim(pe, it, f"B.m{n}")
                    for m in range(C):
                        ins = product(ps[:, m * S:(m + 1) * S], b_qh[r:r + 32, m, tok(t)], b_kh[r:r + 32, m, :])
                    ins.then_inc(f_sem(f"B.m{n}"), 1)

            if Bb:
                after(pe, "b_hi", b)
                rough(range(4))
            if A:
                rows_out(it, "A.v", a_xnT, w0v)
            if Dd:
                taken(pe, it, "D.q")
                cols_out(it, "D.h0", b_zT, w11, 0)
            if Bb:
                rough((4, 5))
                rows_out(it, "B.v", b_ctxT, w1v)
                rough((6, 7))
            if Dd:
                cols_out(it, "D.h1", b_zT, w11, 2)
                cols_out(it, "D.h2", b_zT, w11, 4)
            for t in range(T):
                if A:
                    for n, name in enumerate(("q", "k")):
                        after(pe, f"a_lo_{name}", a, t + 1)
                        ps = claim(pe, it, f"A.{name}{t}")[:].bitcast(F16)
                        for g in range(H0 // 2):
                            h = n * H0 + 2 * g
                            ins = nc.tensor.transpose(
                                ps[:, g * P:(g + 1) * P],
                                a_split[:, t, h:h + 2].rearrange("p h s d -> p (h s d)"), ident16[:])
                        ins.then_inc(f_sem(f"A.{name}{t}"), 1)
                if Dd and t == 0:
                    cols_out(it, "D.h3", b_zT, w11, 6)
            if Bb:
                for n in (4, 5, 6, 7):
                    taken(pe, it, f"B.m{n}")
                ps = claim(pe, it, "B.max")
                for m in range(C):
                    for t in range(T):
                        ins = nc.tensor.transpose(ps[:, m * S + t * P:m * S + (t + 1) * P],
                                                  b_nm[:, t, m].rearrange("p j w -> p (j w)"), ident[:])
                ins.then_inc(f_sem("B.max"), 1)
            if A:
                taken(pe, it, f"A.q{T - 1}")
                taken(pe, it, f"A.k{T - 1}")
                taken(pe, it, "A.v")
            if Bb:
                maxima_taken = [False]
            for what, st, n in PLAN:
                if st not in it.stages:
                    continue
                if what == "score":
                    if st == "B" and not maxima_taken[0]:
                        taken(pe, it, "B.max")
                        taken(pe, it, "B.v")
                        taken(pe, it, "B.k")
                        taken(pe, it, "B.q_")
                        maxima_taken[0] = True
                    scores(it, st, n)
                if what == "weigh":
                    weigh(it, st, n)
                if what == "out":
                    if n == 0:
                        claim(pe, it, "D.out")
                        for m in range(4):
                            taken(pe, it, f"D.h{m}")
                    t, ps = n // 2, bank[BANK_OF["D.out"]]
                    for j in range(4 * (n % 2), 4 * (n % 2) + 4):
                        ins = product(ps[:, t * D:(t + 1) * D], b_hT[:, j, tok(t)], w12[:, j, :], j == 0, j == J - 1)
                    if n == 3:
                        ins.then_inc(f_sem("D.out"), 1)
                if what == "distances":
                    after(pe, "c_rows", c, 1)
                    transposes(it, "C.xn", c_rows)
                    taken(pe, it, "C.xn")
                    ps = claim(pe, it, "C.dist")
                    for t in range(T):
                        for c_ in range(C):
                            ins = product(ps[:, t * E:(t + 1) * E], c_xnT[:, c_, tok(t)], cent_t[:, c_], c_ == 0,
                                          c_ == C - 1)
                    ins.then_inc(f_sem("C.dist"), 1)
            if A:
                taken(pe, it, "A.o0")
                taken(pe, it, "A.o1")
                rows_out(it, "A.wo", a_yT, w0o)
            if Bb:
                taken(pe, it, "B.o0")
                taken(pe, it, "B.o1")
                rows_out(it, "B.wo", b_yT, w1o)
            if A:
                after(pe, "a_z", a)
                transposes(it, "A.z", a_xn)
                taken(pe, it, "A.z")
                for n in range(4):
                    cols_out(it, f"A.h{n}", a_xnT, w01, 2 * n)
            if A:
                for n in (2, 3):
                    taken(pe, it, f"A.h{n}")
                rows_out(it, "A.out", a_hT, w02, J)
        each(pe, turn)

        pe.wait_ge(s_route, 1)
        flat = oh[:].rearrange("p n e -> p (n e)")
        product(bank[0][:, 0:NT * E], tri[:], flat)
        product(bank[1][:, 0:NT * E], ones[:], flat).then_inc(s_pp, 1)

        pe.wait_ge(s_route, ROUTE_ALL)
        pe.wait_ge(s_wmoe, 16 * 2 * E)

        def transpose_in(k, u):
            after_tile(pe, "m_loaded", k, u)
            after_tile(pe, "m_xT", k, u, 0)
            for c in range(C):
                ins = nc.tensor.transpose(bank[u][:, c * P:(c + 1) * P], m_in[:, u, c * P:(c + 1) * P], ident[:])
            ins.then_inc(mig[u]["m_x"], 1)

        transpose_in(0, 0)
        transpose_in(0, 1)

        def step(k, n, nxt):
            expert = []
            for u in range(n):
                i = 2 * k + u
                at = tile_expert[0:1, i:i + 1] if isinstance(i, int) else tile_expert[0:1, bass.ds(i, 1)]
                expert.append(pe.value_load(at, min_val=0, max_val=E - 1))
            for u in range(n):
                after_tile(pe, "m_xT", k, u)
                after_tile(pe, "m_h", k, u, 0)
                for half in range(2):
                    for c in range(C):
                        w = up[:, bass.ds(expert[u], 1), c, half * EH:(half + 1) * EH]
                        ins = product(bank[2 + 2 * u + half][:], m_xT[:, u, c], w.rearrange("p o n -> p (o n)"),
                                      c == 0, c == C - 1)
                ins.then_inc(mig[u]["m_up"], 1)
            for u in range(nxt):
                transpose_in(k + 1, u)
            for u in range(n):
                after_tile(pe, "m_h", k, u)
                after_tile(pe, "m_hT", k, 1 - u, u)
                for j in range(EJ):
                    ins = nc.tensor.transpose(bank[6][:, j * P:(j + 1) * P], m_h[:, u, j * P:(j + 1) * P], ident[:])
                ins.then_inc(mig[u]["m_ht"], 1)
                after_tile(pe, "m_hT", k, u)
                after_tile(pe, "m_out", k, 1 - u, u)
                for j in range(EJ):
                    w = down[:, bass.ds(expert[u], 1), j, :]
                    ins = product(bank[7][:, 0:D], m_hT[:, u, j], w.rearrange("p o n -> p (o n)"), j == 0,
                                  j == EJ - 1)
                ins.then_inc(mig[u]["m_down"], 1)

        tile_steps(pe, step)


_INS = ["x", "ctx_1024", "L0_attn_ln1_w", "L0_attn_Wq", "L0_attn_Wk", "L0_attn_Wv", "L0_attn_rel_bias",
        "L0_attn_scale", "L0_attn_Wo", "L0_attn_ln2_w", "L0_attn_W1", "L0_attn_W2", "L0_xattn_Wq", "L0_xattn_Wk",
        "L0_xattn_Wv", "L0_xattn_Wo", "L0_xattn_lambda_param", "L0_xattn_ln1_g", "L0_xattn_ln1_b",
        "L0_xattn_ln2_g", "L0_xattn_ln2_b", "L0_xattn_ffn_w1", "L0_xattn_ffn_b1", "L0_xattn_ffn_w2",
        "L0_xattn_ffn_b2", "L0_ffn_scale", "L0_ffn_centroids", "L0_ffn_up_w", "L0_ffn_down_w"]


def bucket_onehot():
    dist = np.arange(S)
    exact = BUCKETS // 2
    safe = np.maximum(dist, 1).astype(np.float32)
    ratio = np.log(safe / np.float32(exact)) / np.float32(np.log(128 / exact)) * np.float32(BUCKETS - exact)
    bucket = np.where(dist < exact, dist, np.minimum(exact + ratio.astype(np.int32), BUCKETS - 1))
    return (np.arange(BUCKETS)[:, None] == bucket[None, :]).astype(np.float32)


def kernel(**inputs):
    import concourse.bacc as _bacc
    from concourse.bass_utils import run_bass_kernel_spmd as _run

    nc = _bacc.Bacc("TRN2", target_bir_lowering=False, num_devices=1)
    arrays, d = {}, {}
    for name in _INS:
        a = np.ascontiguousarray(inputs[name])
        if a.ndim == 0:
            a = a.reshape(1, 1)
        arrays[f"in_{name}"] = a
        d[name] = nc.dram_tensor(f"in_{name}", a.shape, mybir.dt.from_np(a.dtype), kind="ExternalInput").ap()
    a = bucket_onehot()
    arrays["in_bucket_onehot"] = a
    d["bucket_onehot"] = nc.dram_tensor("in_bucket_onehot", a.shape, F32, kind="ExternalInput").ap()
    d["out"] = nc.dram_tensor("out_rows", (B * S, D), F32, kind="ExternalOutput").ap()
    build(nc, d)
    r = _run(nc, [arrays], core_ids=[0])
    return r.results[0]["out_rows"].reshape(B, S, D)
```

```python
from contextlib import ExitStack

import numpy as np

import concourse.bass as bass
import concourse.mybir as mybir

F32 = mybir.dt.float32
F32R = mybir.dt.float32r
F16 = mybir.dt.float16
BF16 = mybir.dt.bfloat16
I32 = mybir.dt.int32
U32 = mybir.dt.uint32
ALU = mybir.AluOpType
ACT = mybir.ActivationFunctionType
AX_X = mybir.AxisListType.X

P = 128
B, S, D = 16, 256, 256
T = S // P
C = D // P
H0, D0 = 16, 16
H1, D1 = 8, 32
HID = 1024
J = HID // P
E = 8
EH = 512
EJ = EH // P
BUCKETS = 32
NT = B * T
TILES_MAX = NT + E - 1
SHARED = 22980
QUARTERS = 4
ROUTE_IN_TILE = 25
ROUTE_EXPERTS = ROUTE_IN_TILE + QUARTERS + 3
ROUTE_ALL = ROUTE_EXPERTS + 6
RN_STEPS = 14

SCOLS = S + P

GROUP = 4
A_HEADS = [8 * c + 2 * j + par for c in range(C) for par in range(2) for j in range(GROUP)]
NPA, NPB = 8, 6


def a_s(n):
    return ("score", "A", n)


def b_s(h):
    return ("score", "B", h)


PLAN = [a_s(0), a_s(1), a_s(2), a_s(3), ("out", "D", 0), ("out", "D", 1)]
PLAN += [a_s(4), a_s(5), b_s(0), ("weigh", "A", 0), ("out", "D", 2), ("rows", "C", 0), a_s(6), a_s(7), b_s(1), ("distances", "C", 0), ("out", "D", 3)]
PLAN += [a_s(8), a_s(9), b_s(2), ("weigh", "A", 1), ("out", "D", 4), a_s(10), a_s(11), b_s(3), ("norm", "A", 0)]
PLAN += [("expert", "C", 0), a_s(12), a_s(13), b_s(4), ("weigh", "A", 2), a_s(14), a_s(15), b_s(5)]
PLAN += [("weigh", "B", 0), ("norm", "B", 0)]
PLAN += [b_s(6), b_s(7), ("weigh", "A", 3), ("weigh", "B", 1)]

def _banks():
    out = []

    def add(banks, jobs):
        out.extend((job, banks[n % len(banks)]) for n, job in enumerate(jobs))

    out += [("A.xn", 0), ("B.ctx", 1), ("D.q", 2), ("A.qk0", 4), ("A.qk1", 5), ("B.k", 2), ("B.x", 1), ("A.v", 6)]
    out += [("B.q_", 3), ("D.h0", 7), ("B.m0", 1), ("B.m1", 2), ("B.m2", 3), ("B.m3", 0), ("B.v", 7), ("B.m4", 1)]
    out += [("B.m5", 2), ("D.h1", 4), ("B.m6", 0), ("B.m7", 1), ("D.h2", 5), ("A.q0", 3), ("A.k0", 0), ("A.q1", 1)]
    out += [("A.k1", 2), ("D.h3", 4), ("B.max", 6)]
    of = {("A", 0): 4, ("A", 2): 7, ("B", 0): 6, ("B", 1): 4}
    scores = 0
    for what, st, n in PLAN:
        if what == "score":
            out.append((f"{st}.s{n}", (1, 2, 3, 0)[scores % 4]))
            scores += 1
        if what == "weigh" and (st, n) in of:
            out.append((f"{st}.o{n // 2 if st == 'A' else n}", of[st, n]))
        if what == "distances":
            out.append(("C.dist", 6))
        if what == "rows":
            out.append(("C.xn", 7))
        if (what, n) == ("out", 0):
            out.append(("D.out", 5))
    add((7, 6), ["A.wo", "B.wo"])
    add((0,), ["A.z"])
    add((2, 3), [f"A.h{n}" for n in range(4)])
    add((4,), ["A.out"])
    return out


UNSIGNALLED = ("A.o0", "A.o1", "B.o0", "B.o1")

BANKS, BANK_OF = {}, {}
for _job, _bank in _banks():
    BANK_OF[_job] = _bank
    BANKS.setdefault(_bank, []).append(_job)
PHASES = [(0, 1, "P"), (1, 1, "PA"), (2, 1, "PAB"), (3, 1, "PABD"), (4, B - 4, "PABDC"), (B, 1, "ABDC"),
          (B + 1, 1, "BDC"), (B + 2, 1, "DC"), (B + 3, 1, "C")]


class Turn:

    def __init__(self, phase, k):
        self.first, self.count, self.stages = PHASES[phase]
        self.phase, self.k = phase, k

    def batch(self, stage):
        return self.k + (self.first - "PABDC".index(stage))

    def _before(self, job, counted):
        bank = [j for j in BANKS[BANK_OF[job]] if counted(j)]
        before = sum(n * sum(j[0] in st for j in bank) for _, n, st in PHASES[:self.phase])
        mine = [j for j in bank if j[0] in self.stages]
        return self.k * len(mine) + (before + mine.index(job))

    def used(self, job):
        return self._before(job, lambda j: True)

    def signalled(self, job):
        return self._before(job, lambda j: j not in UNSIGNALLED)


def build(nc, d):
    ctx = ExitStack()
    with ctx:
        _build(nc, d, ctx)


def _build(nc, d, ctx):
    def sem(name):
        return ctx.enter_context(nc.semaphore(name))

    def sbuf(stack, name, shape, dt=F32):
        return stack.enter_context(nc.sbuf_tensor(name, shape, dt))

    LONE = (mybir.EngineType.Pool, mybir.EngineType.SP)
    s_passed = {e: sem(f"waits_passed_{n}") for n, e in enumerate(LONE + (mybir.EngineType.DVE,))}

    def wait(eng, s, value, lone=False):
        if isinstance(value, int):
            if value > 0:
                eng.wait_ge(s, value)
            return
        eng.wait_ge(s, value)
        if lone or eng.engine in LONE:
            eng.sem_inc(s_passed[eng.engine], 1)

    toep = nc.dram_tensor("toep", (H0, P, 3 * P), F32, kind="Internal")
    mrow = nc.dram_tensor("mrow", (H0, S), F32, kind="Internal")
    rows_x = nc.dram_tensor("rows_x", (B * S, D), F32, kind="Internal")
    rows_skip = nc.dram_tensor("rows_skip", (B * S, D), F32, kind="Internal")

    bank = [ctx.enter_context(nc.psum_tensor(f"bank{n}", [P, 512], F32)) for n in range(8)]
    bank_full = [sem(f"bank_full{n}") for n in range(8)]
    bank_free = [sem(f"bank_free{n}") for n in range(8)]

    def claim(pe, turn, job):
        wait(pe, bank_free[BANK_OF[job]], turn.used(job))
        return bank[BANK_OF[job]]

    def full(eng, turn, job):
        wait(eng, bank_full[BANK_OF[job]], turn.signalled(job) + 1)
        return bank[BANK_OF[job]]

    def taken(eng, turn, job, lone=False):
        wait(eng, bank_free[BANK_OF[job]], turn.used(job) + 1, lone)

    def f_sem(job):
        return bank_full[BANK_OF[job]]

    def e_sem(job):
        return bank_free[BANK_OF[job]]

    ident = sbuf(ctx, "ident", [P, P])
    ident16 = sbuf(ctx, "ident16", [P, P], F16)
    ones = sbuf(ctx, "ones", [P, P])
    ones_r = sbuf(ctx, "ones_r", [P, P], F32R)
    halves = sbuf(ctx, "halves", [P, 2, 32])
    mhalf = sbuf(ctx, "mhalf", [P, 64])
    expert_of = sbuf(ctx, "expert_of", [P, NT])
    sorted_row = sbuf(ctx, "sorted_row", [P, TILES_MAX], U32)
    tile_expert = sbuf(ctx, "tile_expert", [P, 64], I32)

    s_const = sem("const_made")
    s_setup_dma = sem("setup_loaded")
    s_qk = sem("qk_weights_loaded")
    s_v = sem("v_and_o_weights_loaded")
    s_a_loaded = sem("stage_a_weights_loaded")
    s_later = sem("other_weights_loaded")
    s_exp, s_masked, s_tp2 = sem("bias_exp"), sem("bias_masked"), sem("second_maxima_read")
    s_w = sem("weights_scaled")

    shared = sbuf(ctx, "shared", [P, SHARED])

    def carver():
        at = [0]

        def carve(name, shape, dt=F32):
            n = int(np.prod(shape[1:]))
            words = n if dt not in (F16, BF16) else n // 2
            at[0] += words
            assert at[0] <= SHARED, f"{name} finds no room"
            view = shared[0:shape[0], at[0] - words:at[0]]
            if dt != F32:
                view = view.bitcast(dt)
            dims = "abcd"[:len(shape) - 1]
            return view.rearrange(f"p ({' '.join(dims)}) -> p {' '.join(dims)}", **dict(zip(dims, shape[1:])))

        return carve

    p1 = carver()
    w1q = p1("w1q", [P, C, D])
    w1k = p1("w1k", [P, C, D])
    w1v = p1("w1v", [P, C, D])
    w1o = p1("w1o", [P, C, D])
    w11 = p1("w11", [P, C, HID])
    w12 = p1("w12", [P, J, D])
    b11 = p1("b11", [P, J])
    vecs = p1("vecs", [P, 6, D])
    G1, B1, G2, B2, FB2, FSC = range(6)
    cent = p1("cent", [E, D])
    cent_t = p1("cent_t", [P, C, E])
    cent_sq = p1("cent_sq", [P, C, E])
    cnorm = p1("cnorm", [P, E])
    lam = p1("lam", [P, 3])

    rec = p1("rec", [P, 2 * C, S])
    x1 = p1("x1", [P, T, D])
    c_in = p1("c_in", [P, T, D])
    b_ctxT = p1("b_ctxT", [P, C, S])
    b_xl = p1("b_xl", [P, T, D])
    b_xT = p1("b_xT", [P, C, S])
    b_kh, b_kl, b_qh, b_ql = (sbuf(ctx, name, [P, C, S], F32R) for name in ("b_kh", "b_kl", "b_qh", "b_ql"))
    b_v = p1("b_v", [P, T, D])
    b_nm = p1("b_nm", [P, T, C, 4, 32])
    b_nmT = sbuf(ctx, "b_nmT", [P, C, S], F32R)
    b_p = p1("b_p", [P, NPB, T, S])
    b_zT = p1("b_zT", [P, C, S])
    b_yT = p1("b_yT", [P, C, S])
    b_q = p1("b_q", [P, T, D])
    b_hT = p1("b_hT", [P, J, S])
    b_st = p1("b_st", [P, T, 6])
    b_mv = p1("b_mv", [P, T, 2])
    b_rs = p1("b_rs", [P, 2, T])
    b_mv2 = p1("b_mv2", [P, T, 2])
    b_rs2 = p1("b_rs2", [P, 2, T])
    d_q = p1("d_q", [P, T, D])
    x1_keep = p1("x1_keep", [P, T, D])
    x1_keep2 = p1("x1_keep2", [P, T, D])
    b_f = p1("b_f", [P, T, D])
    c_n = b_f
    c_rows = p1("c_rows", [P, T, 2 * D])
    c_x2 = c_rows[:, :, D:]
    c_xnT = p1("c_xnT", [P, C, S])
    c_st = p1("c_st", [P, T, 6])
    c_mv = p1("c_mv", [P, T, 2])
    c_rs = p1("c_rs", [P, 2, T])
    c_mv2 = p1("c_mv2", [P, T, 2])
    c_sc = p1("c_sc", [P, 8, T])
    c_nx = p1("c_nx", [P, T])
    c_tmp = p1("c_tmp", [P, T, E])
    c_nd = p1("c_nd", [P, T, E])
    c_mx = p1("c_mx", [P, T, 8])
    c_ix = p1("c_ix", [P, T, 8], U32)
    bias_max = [b_hT[:], b_p[:].rearrange("p n t s -> p (n t) s")[:, 0:H0 // 2]]

    pa = ExitStack()
    w0qk = sbuf(pa, "w0qk", [P, C, 2 * D])
    w0v = sbuf(pa, "w0v", [P, C, D])
    w0o = sbuf(pa, "w0o", [P, C, D])
    w01 = sbuf(pa, "w01", [P, C, HID])
    w02 = sbuf(pa, "w02", [P, J, D])
    ln0 = sbuf(pa, "ln0", [P, 2, C])
    eb = sbuf(pa, "eb", [P, H0, SCOLS])
    qscale = sbuf(pa, "qscale", [P, T, 2 * H0])
    x_in = sbuf(pa, "x_in", [P, T, D])
    x_keep = sbuf(pa, "x_keep", [P, T, D])
    a_xl = sbuf(pa, "a_xl", [P, T, D])
    a_xn = sbuf(pa, "a_xn", [P, T, D])
    a_xnT = sbuf(pa, "a_xnT", [P, C, S])
    a_sq = sbuf(pa, "a_sq", [P, T, 2 * D])
    a_hat = a_sq
    a_split = sbuf(pa, "a_split", [P, T, 2 * H0, 4, D0], F16)
    a_qT = sbuf(pa, "a_qT", [P, H0 // 2, S], F16)
    a_kT = sbuf(pa, "a_kT", [P, H0 // 2, S], F16)
    a_v = sbuf(pa, "a_v", [P, T, 2, H0 // 2, 32])
    a_p = sbuf(pa, "a_p", [P, NPA, SCOLS])
    a_yT = sbuf(pa, "a_yT", [P, C, S])
    a_hT = sbuf(pa, "a_hT", [P, J, S])
    a_st = sbuf(pa, "a_st", [P, T, 6])
    a_mv = sbuf(pa, "a_mv", [P, T, 2])
    a_sc = sbuf(pa, "a_sc", [P, 8, T])
    a_ss = sbuf(pa, "a_ss", [P, T, 2 * H0])
    a_rn = sbuf(pa, "a_rn", [P, T, 2 * H0])
    a_nw = a_split[:].rearrange("p t h s d -> p (t h s d)").bitcast(F32)[:, 0:5 * T * 2 * H0].rearrange(
        "p (n h) -> p n h", n=5)
    a_ms = sbuf(pa, "a_ms", [P, T])
    a_rz = sbuf(pa, "a_rz", [P, 2, T])
    flat_h = a_hT[:].rearrange("p j s -> p (j s)")
    onehot = flat_h[0:BUCKETS, 0:S]
    relb = sbuf(pa, "relb", [BUCKETS, H0])
    sc16 = sbuf(pa, "sc16", [H0, 1])
    bd = flat_h[0:H0, S:S + 3 * P]
    bmax = flat_h[0:H0, S + 3 * P:2 * S + 3 * P]

    PER_BATCH = {
        "a_loaded": 16, "a_stats": T, "a_mv": T, "a_norms": 7, "a_xn": T, "a_xl": T, "a_kept": 1,
        "a_squares": T, "a_sumsq": T, "a_rn": RN_STEPS, "a_hi": 2 * T, "a_lo_q": T, "a_lo_k": T, "a_p": H0,
        "a_p_used": H0 // GROUP, "a_rec": C, "a_ms": T, "a_rz": 2, "a_xy": 1, "a_z": T,
        "b_loaded": 16, "b_stats": T, "b_mv": T, "b_norm": 2, "x1_kept": 1, "x1_kept2": 1, "b_xl": T, "b_hi": 2,
        "b_p_used": H1 // GROUP, "b_rec": C, "b_stats2": T, "b_mv2": T, "b_norm2": 2, "b_gain": T,
        "b_q": T, "b_qb2": 1,
        "c_stats": T, "c_mv": T, "c_norm": 2, "c_gain": T, "c_n": T, "c_x2": 1, "c_stats2": T,
        "c_mv2": T, "c_norms": 7, "c_xl": T, "c_xs": T, "c_rows": 2, "c_stored": 32, "c_nx": T, "c_tmp": T,
        "c_max8": T, "c_index": T, "c_expert": 1,
    }
    sig = {name: sem(name) for name in PER_BATCH}

    def after(eng, name, batch, n=None, lone=False):
        per = PER_BATCH[name]
        wait(eng, sig[name], batch * per + (per if n is None else n), lone)

    s_toep, s_tp, s_bd, s_bmax, s_eb, s_cent, s_lam, s_pe_setup, s_sc = map(sem, (
        "toeplitz_written", "toeplitz_read", "bias_by_distance", "bias_prefix_max", "eb_made",
        "centroid_norms", "lambda_chain", "pe_setup", "qscale_made"))

    def bc(ap, n):
        return ap.unsqueeze(len(ap.shape)).to_broadcast(list(ap.shape) + [n])

    def over_t(ap):
        return ap.unsqueeze(1).to_broadcast([P, T, D])

    def tok(t):
        return slice(t * P, (t + 1) * P)

    block = ctx.enter_context(nc.Block())
    ctx.enter_context(nc.allow_non_contiguous_dma(reason="a few vectors laid over partitions, once"))

    def w_view(ap):
        return ap.rearrange("(c p) n -> p c n", p=P)

    def on_all(ap):
        return ap.rearrange("(o n) -> o n", o=1).to_broadcast([P, ap.shape[0]])

    setup_loads = [
        (onehot, d["bucket_onehot"]), (relb[:], d["L0_attn_rel_bias"]),
        (sc16[:], d["L0_attn_scale"].rearrange("(h o) -> h o", o=1)),
        (lam[:, 0:1], d["L0_xattn_lambda_param"].to_broadcast([P, 1])),
        (cent[:], d["L0_ffn_centroids"]),
        (ln0[:, 0, :], d["L0_attn_ln1_w"].rearrange("(c p) -> p c", p=P)),
        (ln0[:, 1, :], d["L0_attn_ln2_w"].rearrange("(c p) -> p c", p=P)),
    ]
    setup_loads += [(qscale[:, t, 0:H0], on_all(d["L0_attn_scale"])) for t in range(T)]
    qk_loads = [(w0qk[:, :, 0:D], w_view(d["L0_attn_Wq"])), (w0qk[:, :, D:], w_view(d["L0_attn_Wk"]))]
    v_loads = [(w0v[:], w_view(d["L0_attn_Wv"])), (w0o[:], w_view(d["L0_attn_Wo"]))]
    a_loads = [
        (w01[:], w_view(d["L0_attn_W1"])), (w02[:], w_view(d["L0_attn_W2"])),
    ]
    later_loads = [
        (w1q[:], w_view(d["L0_xattn_Wq"])), (w1k[:], w_view(d["L0_xattn_Wk"])),
        (w1v[:], w_view(d["L0_xattn_Wv"])), (w1o[:], w_view(d["L0_xattn_Wo"])),
        (w11[:], w_view(d["L0_xattn_ffn_w1"])), (w12[:], w_view(d["L0_xattn_ffn_w2"])),
        (b11[:], d["L0_xattn_ffn_b1"].rearrange("(j p) -> p j", p=P)),
    ]
    later_loads += [(vecs[:, n, :], on_all(d[name])) for n, name in enumerate((
        "L0_xattn_ln1_g", "L0_xattn_ln1_b", "L0_xattn_ln2_g", "L0_xattn_ln2_b", "L0_xattn_ffn_b2", "L0_ffn_scale"))]
    ALL_LOADED, QK_LOADED, V_LOADED, A_LOADED, LATER_LOADED = (
        16 * len(loads) for loads in (setup_loads, qk_loads, v_loads, a_loads, later_loads))
    CONSTS = 13

    x_tiles = d["x"].rearrange("b (t p) n -> b p t n", p=P)
    ctx_tiles = d["ctx_1024"].rearrange("b (t p) n -> b p t n", p=P)
    x_rows, skip_rows = (t.ap().rearrange("(b t p) n -> b p t n", p=P, t=T) for t in (rows_x, rows_skip))

    def of_batch(tiles, b):
        one = tiles[b:b + 1] if isinstance(b, int) else tiles[bass.ds(b, 1)]
        return one.rearrange("o p t n -> (o p) t n")

    def each(eng, body, skip=0):
        for phase, (_, count, _) in list(enumerate(PHASES))[skip:]:
            if count == 1:
                body(Turn(phase, 0))
            else:
                with eng.Fori(0, count) as k:
                    body(Turn(phase, k))

    s_route, s_pp, s_wmoe = map(sem, ("routing_chain", "prefixes_made", "experts_loaded"))
    pa.close()
    up = sbuf(ctx, "up", [P, E, C, 2 * EH])
    down = sbuf(ctx, "down", [P, E, EJ, D])
    p3 = carver()
    m_row = p3("m_row", [P, 2, 2, 1], U32)
    m_token = p3("m_token", [P, 2, 1], U32)
    m_in = p3("m_in", [P, 2, D])
    m_skip = p3("m_skip", [P, 2, D])
    m_xT = p3("m_xT", [P, 2, C, P])
    m_sg = p3("m_sg", [P, 2, EH])
    m_h = p3("m_h", [P, 2, EH])
    m_hT = p3("m_hT", [P, 2, EJ, P])
    m_out = p3("m_out", [P, 2, D])
    oh = p3("oh", [P, NT, E])
    r_pp = p3("r_pp", [P, NT, E])
    r_tot = p3("r_tot", [P, NT, E])
    r_cum = p3("r_cum", [P, NT, E])
    r_a = p3("r_a", [P, NT, E])
    r_cmp = p3("r_cmp", [P, E, NT])
    r_nt = p3("r_nt", [P, E])
    r_ct = p3("r_ct", [P, E])
    r_base = p3("r_base", [P, E])
    r_cmp2 = p3("r_cmp2", [P, TILES_MAX, E])
    r_te = p3("r_te", [P, TILES_MAX])
    r_posf = p3("r_posf", [P, NT])
    r_pos = p3("r_pos", [P, 3, NT], I32)
    r_place = p3("r_place", [P, 2, NT])
    in_row = p3("in_row", [P, NT, P], F16)
    in_tile = p3("in_tile", [P, NT, TILES_MAX])
    number = p3("number", [P, NT, 2, TILES_MAX], F16)
    r_id = p3("r_id", [P, 4, TILES_MAX])
    io_p = p3("io_p", [P, 1])
    io_r = p3("io_r", [P, P])
    io_n = p3("io_n", [P, NT])
    io_e = p3("io_e", [P, E])
    io_t = p3("io_t", [P, NT])
    io_i = p3("io_i", [P, TILES_MAX])
    tri = p3("tri", [P, P])
    ones_nt = p3("ones_nt", [P, NT])
    s_iota, s_numbered = sem("iotas_made"), sem("one_hot_numbered")
    BY_TILE = {"m_loaded": 16, "m_skip": 16, "m_row": 1, "m_x": 1, "m_xT": 1, "m_up": 1, "m_silu": 1,
               "m_h": 1, "m_ht": 1, "m_hT": 1, "m_down": 1, "m_out": 1, "m_stored": 16}
    mig = [{name: sem(f"{name}{u}") for name in BY_TILE} for u in range(2)]

    def after_tile(eng, name, k, u, n=1):
        wait(eng, mig[u][name], (k + n) * BY_TILE[name])

    def phase1_over(eng):
        after(eng, "c_expert", B - 1)
        after(eng, "c_rows", B - 1)
        after(eng, "c_stored", B - 1)

    PAIRS = (TILES_MAX - 1) // 2

    H_BANK, DOWN_BANK = (6, 2), (7, 4)

    def tile_steps(eng, body):
        body(0, 2, 2)
        with eng.Fori(0, PAIRS - 2) as k:
            body(k + 1, 2, 2)
        body(PAIRS - 1, 2, TILES_MAX - 2 * PAIRS)
        if TILES_MAX > 2 * PAIRS:
            body(PAIRS, 1, 0)

    @block.sync
    def _(sp):
        sp.dma_start(x_in[:], of_batch(x_tiles, 0)).then_inc(sig["a_loaded"], 16)
        for dst, src in setup_loads:
            sp.dma_start(dst, src).then_inc(s_setup_dma, 16)
        for dst, src in qk_loads:
            sp.dma_start(dst, src).then_inc(s_qk, 16)
        sp.wait_ge(s_bd, 2)
        sp.dma_start(toep.ap(), bd.unsqueeze(1).to_broadcast([H0, P, 3 * P])).then_inc(s_toep, 16)
        sp.wait_ge(s_bmax, 2)
        sp.dma_start(mrow.ap(), bmax).then_inc(s_toep, 16)
        for dst, src in v_loads:
            sp.dma_start(dst, src).then_inc(s_v, 16)
        sp.wait_ge(s_toep, 32)
        shifted = bass.AP(tensor=toep, offset=P, ap=[[3 * P - 1, P], [3 * P * P, H0], [1, S]])
        sp.dma_start(eb[:, :, 0:S], shifted).then_inc(s_tp, 16)
        maxima = mrow.ap().rearrange("(o h) q -> o h q", o=1)
        for half, loaded in enumerate((s_tp, s_tp2)):
            sp.dma_start(bias_max[half], maxima[:, half * 8:(half + 1) * 8, :].to_broadcast([P, 8, S])
                         ).then_inc(loaded, 16)
        for dst, src in a_loads:
            sp.dma_start(dst, src).then_inc(s_a_loaded, 16)
        for dst, src in later_loads:
            sp.dma_start(dst, src).then_inc(s_later, 16)

        def load_experts():
            after(sp, "b_xl", B - 1)
            for e in range(E):
                sp.dma_start(up[:, e], w_view(d["L0_ffn_up_w"][e])).then_inc(s_wmoe, 16)
                sp.dma_start(down[:, e], w_view(d["L0_ffn_down_w"][e])).then_inc(s_wmoe, 16)

        def turn(it):
            if it.first == B + 1:
                load_experts()
            if "P" in it.stages and it.first > 0:
                b = it.batch("P")
                after(sp, "a_xn", b - 1)
                after(sp, "a_xl", b - 1)
                after(sp, "a_kept", b - 1)
                sp.dma_start(x_in[:], of_batch(x_tiles, b)).then_inc(sig["a_loaded"], 16)
            if "A" in it.stages:
                if "B" in it.stages:
                    taken(sp, it, "B.ctx")
                sp.dma_start(c_in[:], of_batch(ctx_tiles, it.batch("A"))).then_inc(sig["b_loaded"], 16)
            if "C" in it.stages:
                b = it.batch("C")
                after(sp, "c_rows", b)
                sp.dma_start(of_batch(x_rows, b), c_rows[:, :, 0:D]).then_inc(sig["c_stored"], 16)
                sp.dma_start(of_batch(skip_rows, b), c_rows[:, :, D:]).then_inc(sig["c_stored"], 16)

        each(sp, turn)

    @block.scalar
    def _(act):
        copy = nc.scalar.copy

        act.wait_ge(s_setup_dma, ALL_LOADED)
        nc.scalar.activation(lam[:, 1:2], lam[:, 0:1], ACT.Exp, scale=-1.0).then_inc(s_lam, 1)

        def bias_exp():
            for half in range(2):
                act.wait_ge(s_eb, 2 * half + 2)
                part = eb[:, 8 * half:8 * half + 8].rearrange("p h n -> p (h n)")
                nc.scalar.activation(part, part, ACT.Exp).then_inc(s_exp, 1)

        def evacuate(it, job, dst, view=None):
            src = full(act, it, job)[:]
            copy(dst, src if view is None else view(src)).then_inc(e_sem(job), 1)

        def turn(it):
            A, Bb, Dd, Cc = (st in it.stages for st in "ABDC")
            a, b, dd, c = (it.batch(st) for st in "ABDC")
            if A:
                evacuate(it, "A.xn", a_xnT[:].rearrange("p c s -> p (c s)"))
            if Bb:
                evacuate(it, "B.ctx", b_ctxT[:].rearrange("p c s -> p (c s)"))
            if Dd:
                evacuate(it, "D.q", b_zT[:].rearrange("p c s -> p (c s)"))
            if A:
                for t in range(T):
                    ps = full(act, it, f"A.qk{t}")
                    nc.scalar.activation(a_sq[:, t], ps[:], ACT.Square).then_inc(sig["a_squares"], 1)
            def high(job, dst):
                ps = full(act, it, job)
                copy(dst[:].rearrange("p c s -> p (c s)"), ps[:]).then_inc(sig["b_hi"], 1)

            if Bb:
                high("B.k", b_kh)
                evacuate(it, "B.x", b_xT[:].rearrange("p c s -> p (c s)"))
            if Bb:
                high("B.q_", b_qh)

            def hidden(n):
                ps = full(act, it, f"D.h{n}")
                nc.scalar.activation(b_hT[:, 2 * n], ps[:, 0:S], ACT.Relu, bias=b11[:, 2 * n:2 * n + 1])
                nc.scalar.activation(b_hT[:, 2 * n + 1], ps[:, S:], ACT.Relu,
                                     bias=b11[:, 2 * n + 1:2 * n + 2]).then_inc(e_sem(f"D.h{n}"), 1)

            if Dd:
                hidden(0)
            if A:
                for t in range(T):
                    taken(act, it, f"A.qk{t}")
                    hat = a_hat[:, t].rearrange("p (h o d) -> p h o d", o=1, d=D0)
                    for lo, hi, slots in ((0, H0, slice(0, 4, 2)), (H0, 2 * H0, slice(0, 2))):
                        copy(a_split[:, t, lo:hi, slots, :],
                             hat[:, lo:hi].to_broadcast([P, H0, 2, D0])).then_inc(sig["a_hi"], 1)
            if it.first == 1:
                bias_exp()
            if A:
                ps = full(act, it, "A.v")[:].rearrange("p (t i h d) -> p t i h d", t=T, h=2, d=D0)
                copy(a_v[:, :, 0, :, 0:D0], ps[:, :, :, 0])
                copy(a_v[:, :, 1, :, D0:], ps[:, :, :, 1]).then_inc(e_sem("A.v"), 1)
            if Bb:
                evacuate(it, "B.v", b_v[:].rearrange("p t n -> p (t n)"))
            if A:
                if not isinstance(a, int) or a > 0:
                    after(act, "b_mv", a - 1)
                copy(x_keep[:], x_in[:]).then_inc(sig["a_kept"], 1)
            if Dd:
                hidden(1)
                hidden(2)
            for t in range(T):
                if A:
                    evacuate(it, f"A.k{t}", a_kT[:, :, tok(t)],
                             lambda x: x.bitcast(F16).rearrange("p (g s) -> p g s", s=P))
            if Dd:
                hidden(3)
            if Bb:
                evacuate(it, "B.max", b_nmT[:].rearrange("p c s -> p (c s)"))
            if Dd:
                if Cc:
                    after(act, "c_x2", c)
                copy(x1_keep2[:], x1_keep[:]).then_inc(sig["x1_kept2"], 1)
            if Bb:
                if Dd:
                    after(act, "x1_kept2", dd)
                copy(x1_keep[:], x1[:]).then_inc(sig["x1_kept"], 1)
            for what, st, n in PLAN:
                if st not in it.stages:
                    continue
                if what == "distances":
                    after(act, "c_rows", c, 1)
                    for t in range(T):
                        nc.scalar.activation(b_zT[:, t], c_rows[:, t, 0:D], ACT.Square,
                                             accum_out=c_nx[:, t:t + 1]).then_inc(sig["c_nx"], 1)
                if what == "rows":
                    evacuate(it, "C.xn", c_xnT[:].rearrange("p c s -> p (c s)"))
                if what != "score":
                    continue
                ps = full(act, it, f"{st}.s{n}")
                if st == "A":
                    after(act, "a_p_used", a, n // GROUP + 1 - NPA // GROUP)
                    nc.scalar.activation(a_p[:, n % NPA], ps[:, 0:SCOLS], ACT.Exp).then_inc(e_sem(f"A.s{n}"), 1)
                else:
                    before = b * (H1 // GROUP) + (n - NPB) // GROUP + 1 if n >= NPB else b * (H1 // GROUP)
                    wait(act, sig["b_p_used"], before)
                    nc.scalar.activation(b_p[:, n % NPB].rearrange("p t s -> p (t s)"), ps[:],
                                         ACT.Exp).then_inc(e_sem(f"B.s{n}"), 1)
            if A:
                taken(act, it, "A.wo")
                for t in range(T):
                    nc.scalar.activation(a_hT[:, t], a_xl[:, t], ACT.Square,
                                         accum_out=a_ms[:, t:t + 1]).then_inc(sig["a_ms"], 1)
                evacuate(it, "A.z", a_xnT[:].rearrange("p c s -> p (c s)"))
                for n in range(4):
                    ps = full(act, it, f"A.h{n}")
                    nc.scalar.activation(a_hT[:, 2 * n:2 * n + 2].rearrange("p j s -> p (j s)"), ps[:],
                                         ACT.Relu).then_inc(e_sem(f"A.h{n}"), 1)

        each(act, turn)

        act.wait_ge(s_iota, 8)
        act.wait_ge(s_route, ROUTE_IN_TILE)
        nc.scalar.activation(number[:, :, 1], in_tile[:], ACT.Copy, scale=io_p[:, 0:1]).then_inc(s_numbered, 1)

        def transposed(k, u):
            after_tile(act, "m_x", k, u)
            copy(m_xT[:, u].rearrange("p c s -> p (c s)"), bank[u][:, 0:C * P]).then_inc(mig[u]["m_xT"], 1)

        def step(k, n, nxt):
            for u in range(n):
                after_tile(act, "m_up", k, u)
                nc.scalar.activation(m_sg[:, u], bank[3 + 2 * u][:], ACT.Silu).then_inc(mig[u]["m_silu"], 1)
            for u in range(nxt):
                transposed(k + 1, u)
            for u in range(n):
                after_tile(act, "m_ht", k, u)
                copy(m_hT[:, u].rearrange("p j s -> p (j s)"), bank[H_BANK[u]][:]).then_inc(mig[u]["m_hT"], 1)

        transposed(0, 0)
        transposed(0, 1)
        tile_steps(act, step)

    @block.gpsimd
    def _(pool):
        done = [0]

        def const(ins):
            ins.then_inc(s_const, 1)
            done[0] += 1

        const(pool.memset(ident[:], 0.0))
        const(pool.memset(ident16[:], 0.0))
        const(pool.memset(ones[:], 1.0))
        const(pool.memset(halves[:], 0.0))
        pool.wait_ge(s_const, 4)
        for m in (ident, ident16):
            const(pool.affine_select(out=m[:], in_=m[:], compare_op=ALU.not_equal, fill=1.0, base=0,
                                     pattern=[[-1, P]], channel_multiplier=1))
        const(pool.memset(halves[:, 0, 0:D0], 1.0))
        const(pool.memset(halves[:, 1, D0:], 1.0))
        const(pool.tensor_copy(ones_r[:], ones[:]))
        const(pool.memset(mhalf[:], -0.5))
        const(pool.memset(a_v[:, :, 0, :, D0:], 0.0))
        const(pool.memset(a_v[:, :, 1, :, 0:D0], 0.0))
        const(pool.memset(b_nm[:], 0.0))
        assert done[0] == CONSTS
        def mask_bias():
            for half in range(2):
                pool.wait_ge(s_exp, half + 1)
                for cols, n in ((slice(0, S), S), (slice(S, SCOLS), P)):
                    part = eb[:, 8 * half:8 * half + 8, cols]
                    pool.affine_select(out=part, in_=part, compare_op=ALU.is_gt, fill=0.0, base=0,
                                       pattern=[[0, 8], [1, n]], channel_multiplier=-1).then_inc(s_masked, 1)
            pool.wait_ge(s_masked, 4)
            pool.memset(eb[:, :, 0:1], 1.0).then_inc(s_masked, 1)
            pool.wait_ge(s_later, LATER_LOADED)

        def power(out, in_, name):
            pool.tensor_tensor(out, in_, mhalf[:, 0:out.shape[-1]], ALU.pow).then_inc(sig[name], 1)

        def layer_then_rms(mv, sc, name, batch, eps):
            var = mv[:, :, 1]
            pool.tensor_scalar(sc[:, 0], var, eps, None, ALU.add).then_inc(sig[name], 1)
            after(pool, name, batch, 1)
            power(sc[:, 1], sc[:, 0], name)
            after(pool, name, batch, 2)
            pool.tensor_tensor(sc[:, 2], var, sc[:, 1], ALU.mult).then_inc(sig[name], 1)
            after(pool, name, batch, 3)
            pool.tensor_tensor(sc[:, 3], sc[:, 2], sc[:, 1], ALU.mult).then_inc(sig[name], 1)
            after(pool, name, batch, 4)
            pool.tensor_scalar(sc[:, 4], sc[:, 3], 1e-6, None, ALU.add).then_inc(sig[name], 1)
            after(pool, name, batch, 5)
            power(sc[:, 5], sc[:, 4], name)
            after(pool, name, batch, 6)
            pool.tensor_tensor(sc[:, 6], sc[:, 5], sc[:, 1], ALU.mult).then_inc(sig[name], 1)

        def layer(mv, rs, name, batch, eps):
            pool.tensor_scalar(rs[:, 0], mv[:, :, 1], eps, None, ALU.add).then_inc(sig[name], 1)
            after(pool, name, batch, 1)
            power(rs[:, 1], rs[:, 0], name)

        def turn(it):
            A, Bb, Dd, Cc = (st in it.stages for st in "ABDC")
            a, b, dd, c = (it.batch(st) for st in "ABDC")
            if Cc:
                after(pool, "c_mv", c)
                layer(c_mv, c_rs, "c_norm", c, 1e-5)
            if Dd:
                if Cc:
                    after(pool, "c_stats", c)
                after(pool, "b_q", dd)
                pool.tensor_tensor(d_q[:], b_q[:], over_t(vecs[:, FB2]), ALU.add).then_inc(sig["b_qb2"], 1)
            if Cc:
                after(pool, "c_mv2", c)
                layer_then_rms(c_mv2, c_sc, "c_norms", c, 1e-5)
            if A:
                for t in range(T):
                    after(pool, "a_hi", a, 2 * t + 2)
                    hat = a_hat[:, t].rearrange("p (h d) -> p h d", d=D0)
                    for slot in (2, 3):
                        ins = pool.tensor_tensor(a_split[:, t, H0:, slot, :], hat[:, H0:], a_split[:, t, H0:, 0, :],
                                                 ALU.subtract)
                    ins.then_inc(sig["a_lo_k"], 1)
            if Cc:
                after(pool, "c_xs", c)
                pool.tensor_tensor(c_rows[:, :, 0:D], c_rows[:, :, 0:D], over_t(vecs[:, FSC]),
                                   ALU.mult).then_inc(sig["c_rows"], 1)
                after(pool, "c_xl", c)
                pool.tensor_tensor(c_x2, c_x2, c_n[:], ALU.add).then_inc(sig["c_rows"], 1)
            if it.first == 1:
                mask_bias()
            if A:
                after(pool, "a_ms", a)
                pool.tensor_scalar(a_rz[:, 0], a_ms[:], 1.0 / D, 1e-6, ALU.mult, ALU.add).then_inc(sig["a_rz"], 1)
                after(pool, "a_rz", a, 1)
                power(a_rz[:, 1], a_rz[:, 0], "a_rz")
                after(pool, "a_kept", a)
                pool.tensor_tensor(x_keep[:], x_keep[:], a_xl[:], ALU.add).then_inc(sig["a_xy"], 1)
            if Bb:
                after(pool, "b_mv2", b)
                layer(b_mv2, b_rs2, "b_norm2", b, 1e-5)
            if "P" in it.stages:
                p = it.batch("P")
                after(pool, "a_mv", p)
                layer_then_rms(a_mv, a_sc, "a_norms", p, 1e-5)
            if A:
                after(pool, "b_mv", a)
                layer(b_mv, b_rs, "b_norm", a, 1e-5)

        each(pool, turn)

        phase1_over(pool)
        for io, pattern, base, by_partition in (
                (io_e, [[1, E]], 0, 0), (io_t, [[P, NT]], 0, 0), (io_i, [[1, TILES_MAX]], 0, 0), (io_n, [[1, NT]], 0, 0),
                (io_r, [[1, P]], 0, 0), (io_p, [[1, 1]], 1, 1)):
            pool.iota(io[:], pattern=pattern, base=base, channel_multiplier=by_partition,
                      allow_small_or_imprecise_dtypes=True).then_inc(s_iota, 1)
        pool.memset(ones_nt[:], 1.0).then_inc(s_iota, 1)
        pool.affine_select(out=tri[:], in_=ones[:], compare_op=ALU.is_gt, fill=0.0, base=0, pattern=[[1, P]],
                           channel_multiplier=-1).then_inc(s_iota, 1)

        pool.wait_ge(s_iota, 8)
        pool.wait_ge(s_route, ROUTE_IN_TILE)
        pool.tensor_tensor(number[:, :, 0], in_tile[:], io_n[:].unsqueeze(2).to_broadcast([P, NT, TILES_MAX]),
                           ALU.mult).then_inc(s_numbered, 1)

        def gather(dst, src, rows, name, u):
            pool.indirect_dma_start(out=dst[:, u], out_offset=None, in_=src.ap(),
                                    in_offset=bass.IndirectOffsetOnAxis(ap=rows, axis=0)
                                    ).then_inc(mig[u][name], 16)

        pool.wait_ge(s_route, ROUTE_ALL)
        for u in range(2):
            gather(m_in, rows_x, sorted_row[:, u:u + 1], "m_loaded", u)
        for u in range(2):
            gather(m_skip, rows_skip, sorted_row[:, u:u + 1], "m_skip", u)

        def step(k, n, nxt):
            for u in range(nxt):
                after_tile(pool, "m_x", k, u)
                after_tile(pool, "m_row", k, u)
                gather(m_in, rows_x, m_row[:, 0, u], "m_loaded", u)
            for u in range(n):
                after_tile(pool, "m_out", k, u)
                pool.indirect_dma_start(
                    out=d["out"], out_offset=bass.IndirectOffsetOnAxis(ap=m_token[:, u], axis=0),
                    in_=m_out[:, u], in_offset=None, bounds_check=B * S - 1, oob_is_err=False,
                ).then_inc(mig[u]["m_stored"], 16)
                if u < nxt:
                    gather(m_skip, rows_skip, m_row[:, 1, u], "m_skip", u)

        tile_steps(pool, step)
        for u in range(2):
            pool.wait_ge(mig[u]["m_stored"], 16 * ((TILES_MAX + 1 - u) // 2))

    @block.vector
    def _(dve):
        tt, ts = dve.tensor_tensor, dve.tensor_scalar

        def scale_rows(w, n, loaded, value):
            dve.wait_ge(loaded, value)
            for c in range(C):
                ts(w[:, c], w[:, c], ln0[:, n, c:c + 1], None, ALU.mult).then_inc(s_w, 1)

        def scale_b_weights():
            dve.wait_ge(s_later, LATER_LOADED)
            ts(w1q[:], w1q[:], float(D1) ** -0.5, None, ALU.mult).then_inc(s_w, 1)
            dve.wait_ge(s_lam, 4)
            ts(w1o[:], w1o[:], lam[:, 0:1], None, ALU.mult).then_inc(s_w, 1)

        def subtract_maxima():
            for half in range(2):
                dve.wait_ge(s_tp, 32)
                if half == 1:
                    dve.wait_ge(s_tp2, 16)
                heads = slice(8 * half, 8 * half + 8)
                tt(eb[:, heads, S:], eb[:, heads, 0:P], bias_max[half][:, :, P:], ALU.subtract).then_inc(s_eb, 1)
                dve.wait_ge(s_eb, 2 * half + 1)
                tt(eb[:, heads, 0:S], eb[:, heads, 0:S], bias_max[half], ALU.subtract).then_inc(s_eb, 1)

        def stats(x, st, mv, s_stats, s_mv, batch):
            for t in range(T):
                dve.bn_stats(st[:, t], x[:, t]).then_inc(sig[s_stats], 1)
            for t in range(T):
                after(dve, s_stats, batch, t + 1, lone=True)
                dve.bn_aggr(mv[:, t], st[:, t]).then_inc(sig[s_mv], 1)

        def shifted(out, x, mv, scale, name):
            for t in range(T):
                ts(out[:, t], x[:, t], mv[:, t, 0:1], scale[:, t:t + 1], ALU.subtract,
                   ALU.mult).then_inc(sig[name], 1)

        def normed(out, x, mv, scale, g, bias, gained, done, batch):
            for t in range(T):
                dve.scalar_tensor_tensor(out[:, t], x[:, t], mv[:, t, 0:1], vecs[:, g], ALU.subtract,
                                         ALU.mult).then_inc(sig[gained], 1)
            for t in range(T):
                after(dve, gained, batch, t + 1)
                dve.scalar_tensor_tensor(out[:, t], out[:, t], scale[:, t:t + 1], vecs[:, bias], ALU.mult,
                                         ALU.add).then_inc(sig[done], 1)

        def normalised(it, st, n, yT):
            ps = bank[BANK_OF[f"{st}.o{n}"]]
            used, name = ("a_p_used", "a_rec") if st == "A" else ("b_p_used", "b_rec")
            batch = it.batch(st)
            after(dve, used, batch, 2 * n + 2 if st == "A" else n + 1)
            r = rec[:, n + C * (st == "B")]
            dve.reciprocal(r, ps[:, S:]).then_inc(sig[name], 1)
            after(dve, name, batch, n + 1)
            tt(yT[:, n], ps[:, 0:S], r, ALU.mult).then_inc(e_sem(f"{st}.o{n}"), 1)

        def turn(it):
            A, Bb, Dd, Cc = (st in it.stages for st in "ABDC")
            a, b, dd, c = (it.batch(st) for st in "ABDC")
            if Cc:
                after(dve, "c_norm", c)
                normed(c_n, b_f, c_mv, c_rs[:, 1], G2, B2, "c_gain", "c_n", c)
                after(dve, "c_n", c)
                after(dve, "c_stored", c - 1)
                tt(c_x2, x1_keep2[:], c_n[:], ALU.add).then_inc(sig["c_x2"], 1)

            def nearest():
                after(dve, "c_nx", c)
                for t in range(T):
                    ts(c_tmp[:, t], cnorm[:], c_nx[:, t:t + 1], None, ALU.add).then_inc(sig["c_tmp"], 1)
                after(dve, "c_tmp", c)
                ps = full(dve, it, "C.dist")
                tt(c_nd[:], ps[:, 0:T * E].rearrange("p (t e) -> p t e", e=E), c_tmp[:],
                   ALU.subtract).then_inc(e_sem("C.dist"), 1)
                taken(dve, it, "C.dist", lone=True)
                for t in range(T):
                    dve.max(c_mx[:, t], c_nd[:, t]).then_inc(sig["c_max8"], 1)
                for t in range(T):
                    after(dve, "c_max8", c, t + 1, lone=True)
                    dve.max_index(c_ix[:, t], c_mx[:, t], c_nd[:, t]).then_inc(sig["c_index"], 1)
                after(dve, "c_index", c)
                where = slice(T * c, T * c + T) if isinstance(c, int) else bass.ds(T * c, T)
                dve.tensor_copy(expert_of[:, where], c_ix[:, :, 0]).then_inc(sig["c_expert"], 1)

            def low(job, n, lo, hi):
                after(dve, "b_hi", b, n)
                tt(lo[:].rearrange("p c s -> p (c s)"), bank[BANK_OF[job]][:],
                   hi[:].bitcast(F32).rearrange("p c s -> p (c s)"), ALU.subtract).then_inc(e_sem(job), 1)

            def inverse_lengths(a):
                x, xh, y, u, w = (a_nw[:, n] for n in range(5))
                step = [0]

                def link(ins, ready=True):
                    ins.then_inc(sig["a_rn"], 1)
                    step[0] += 1
                    if ready:
                        after(dve, "a_rn", a, step[0])

                after(dve, "a_sumsq", a)
                link(ts(x, a_ss[:].rearrange("p t h -> p (t h)"), 1e-6, None, ALU.add))
                link(ts(xh, x, -0.5, None, ALU.mult), False)
                link(ts(u.bitcast(I32), x.bitcast(I32), 1, None, ALU.logical_shift_right))
                link(ts(y.bitcast(I32), u.bitcast(I32), -1.0, float(0x5f3759df), ALU.mult, ALU.add))
                for _ in range(3):
                    link(tt(u, xh, y, ALU.mult))
                    link(tt(w, u, y, ALU.mult))
                    link(dve.scalar_tensor_tensor(y, w, 1.5, y, ALU.add, ALU.mult))
                link(tt(a_rn[:].rearrange("p t h -> p (t h)"), y, qscale[:].rearrange("p t h -> p (t h)"),
                        ALU.mult), False)

            if A:
                for t in range(T):
                    after(dve, "a_squares", a, t + 1)
                    dve.tensor_reduce(a_ss[:, t], a_sq[:, t].rearrange("p (h d) -> p h d", d=D0), AX_X,
                                      ALU.add).then_inc(sig["a_sumsq"], 1)
                inverse_lengths(a)
            if Bb:
                low("B.k", 1, b_kl, b_kh)
                low("B.q_", 2, b_ql, b_qh)
            if A:
                after(dve, "a_rn", a)
                for t in range(T):
                    ps = bank[BANK_OF[f"A.qk{t}"]]
                    tt(a_hat[:, t].rearrange("p (h d) -> p h d", d=D0), ps[:].rearrange("p (h d) -> p h d", d=D0),
                       bc(a_rn[:, t], D0), ALU.mult).then_inc(e_sem(f"A.qk{t}"), 1)
            if Cc:
                after(dve, "c_x2", c)
                stats(c_x2, c_st, c_mv2, "c_stats2", "c_mv2", c)
            for t in range(T):
                if Bb:
                    for j in range(4):
                        ps = full(dve, it, f"B.m{4 * t + j}")
                        dve.tensor_reduce(b_nm[:, t, :, j, 0:1], ps[:].rearrange("p (m s) -> p m s", s=S), AX_X,
                                          ALU.max, negate=True).then_inc(e_sem(f"B.m{4 * t + j}"), 1)
            if A:
                for t in range(T):
                    after(dve, "a_hi", a, 2 * t + 1)
                    hat = a_hat[:, t].rearrange("p (h o d) -> p h o d", o=1, d=D0)[:, 0:H0]
                    tt(a_split[:, t, 0:H0, 1::2, :], hat.to_broadcast([P, H0, 2, D0]),
                       a_split[:, t, 0:H0, 0:1, :].to_broadcast([P, H0, 2, D0]), ALU.subtract
                       ).then_inc(sig["a_lo_q"], 1)
            if it.first == 1:
                subtract_maxima()
                scale_rows(w0v, 0, s_v, V_LOADED)
            if Cc:
                after(dve, "c_norms", c)
                shifted(c_rows[:, :, 0:D], c_x2, c_mv2, c_sc[:, 6], "c_xs")
                shifted(c_n, c_x2, c_mv2, c_sc[:, 1], "c_xl")
            if A:
                for t in range(T):
                    ps = full(dve, it, f"A.q{t}")
                    dve.tensor_copy(a_qT[:, :, tok(t)], ps[:].bitcast(F16).rearrange("p (g s) -> p g s", s=P)
                                    ).then_inc(e_sem(f"A.q{t}"), 1)
            if it.first == 1:
                dve.wait_ge(s_masked, 5)
            for what, st, n in PLAN:
                if st not in it.stages:
                    continue
                if what == "score" and st == "A":
                    taken(dve, it, f"A.s{n}")
                    tt(a_p[:, n % NPA], a_p[:, n % NPA], eb[:, A_HEADS[n]], ALU.mult).then_inc(sig["a_p"], 1)
                if what == "expert":
                    nearest()
                if what == "norm":
                    normalised(it, st, n, a_yT if st == "A" else b_yT)
            if it.first == 1:
                scale_rows(w01, 1, s_a_loaded, A_LOADED)
                scale_b_weights()
            if A:
                normalised(it, "A", 1, a_yT)
            if Bb:
                normalised(it, "B", 1, b_yT)
            if A:
                ps = full(dve, it, "A.wo")
                tt(a_xl[:], ps[:].rearrange("p (t n) -> p t n", n=D), a_xl[:], ALU.add).then_inc(e_sem("A.wo"), 1)
                after(dve, "a_rz", a)
                for t in range(T):
                    ts(a_xn[:, t], a_xl[:, t], a_rz[:, 1, t:t + 1], None, ALU.mult).then_inc(sig["a_z"], 1)
            if Bb:
                ps = full(dve, it, "B.wo")
                if Dd:
                    after(dve, "b_qb2", dd)
                tt(b_q[:], ps[:].rearrange("p (t n) -> p t n", n=D), b_xl[:], ALU.add).then_inc(e_sem("B.wo"), 1)
                taken(dve, it, "B.wo")
                stats(b_q, b_st, b_mv2, "b_stats2", "b_mv2", b)
            if "P" in it.stages:
                p = it.batch("P")
                after(dve, "a_loaded", p)
                stats(x_in, a_st, a_mv, "a_stats", "a_mv", p)
            if Bb:
                after(dve, "b_norm2", b)
                normed(b_q, b_q, b_mv2, b_rs2[:, 1], G1, B1, "b_gain", "b_q", b)
            if Dd:
                ps = full(dve, it, "D.out")
                after(dve, "b_qb2", dd)
                if Cc:
                    after(dve, "c_rows", c)
                tt(b_f[:], ps[:].rearrange("p (t n) -> p t n", n=D), d_q[:], ALU.add).then_inc(e_sem("D.out"), 1)
                taken(dve, it, "D.out")
                stats(b_f, c_st, c_mv, "c_stats", "c_mv", dd)
            if "P" in it.stages:
                after(dve, "a_norms", p)
                if A:
                    taken(dve, it, "A.z")
                    after(dve, "a_xy", a)
                shifted(a_xn, x_in, a_mv, a_sc[:, 6], "a_xn")
                shifted(a_xl, x_in, a_mv, a_sc[:, 1], "a_xl")
            if A:
                ps = full(dve, it, "A.out")
                after(dve, "a_xy", a)
                if Bb:
                    after(dve, "x1_kept", b)
                tt(x1[:], ps[:].rearrange("p (t n) -> p t n", n=D), x_keep[:], ALU.add).then_inc(e_sem("A.out"), 1)
                taken(dve, it, "A.out")
                stats(x1, b_st, b_mv, "b_stats", "b_mv", a)
                after(dve, "b_norm", a)
                shifted(b_xl, x1, b_mv, b_rs[:, 1], "b_xl")
        dve.memset(bd, 0.0).then_inc(s_bd, 1)
        dve.memset(qscale[:, :, H0:], 1.0).then_inc(s_sc, 1)
        dve.wait_ge(s_setup_dma, ALL_LOADED)
        dve.wait_ge(s_bd, 1)
        dve.wait_ge(s_pe_setup, 1)
        ts(bd[:, P:P + S], bank[0][0:H0, 0:S], sc16[:, 0:1], None, ALU.mult).then_inc(s_bd, 1)
        dve.wait_ge(s_bd, 2)
        dve.tensor_tensor_scan(bmax[:, 1:S], bd[:, P + 1:P + S], bd[:, P + 1:P + S], -3.0e38, ALU.max,
                               ALU.max).then_inc(s_bmax, 1)
        dve.tensor_copy(bmax[:, 0:1], bd[:, P + 1:P + 2]).then_inc(s_bmax, 1)
        dve.memset(qscale[0:1, 0, 0:H0], 0.0).then_inc(s_sc, 1)
        dve.wait_ge(s_lam, 1)
        ts(lam[:, 1:2], lam[:, 1:2], 1.0, None, ALU.add).then_inc(s_lam, 1)
        dve.wait_ge(s_lam, 2)
        dve.reciprocal(lam[:, 2:3], lam[:, 1:2]).then_inc(s_lam, 1)
        dve.wait_ge(s_lam, 3)
        ts(lam[:, 0:1], lam[:, 2:3], -1.0, 1.0, ALU.mult, ALU.add).then_inc(s_lam, 1)
        dve.wait_ge(s_pe_setup, 2)
        ts(cent_t[:].rearrange("p c e -> p (c e)"), bank[1][:, 0:C * E], 2.0, None, ALU.mult).then_inc(s_cent, 1)
        dve.wait_ge(s_cent, 1)
        tt(cent_sq[:], cent_t[:], cent_t[:], ALU.mult).then_inc(s_cent, 1)
        dve.wait_ge(s_pe_setup, 3)
        ts(cnorm[:], bank[2][:, 0:E], 0.25, None, ALU.mult).then_inc(s_cent, 1)
        dve.wait_ge(s_cent, 3)
        dve.wait_ge(s_sc, 2)
        dve.wait_ge(s_qk, QK_LOADED)
        for c in range(C):
            ts(w0qk[:, c], w0qk[:, c], ln0[:, 0, c:c + 1], None, ALU.mult).then_inc(s_w, 1)
        dve.wait_ge(s_const, CONSTS)
        turn(Turn(0, 0))
        each(dve, turn, skip=1)

        phase1_over(dve)
        dve.wait_ge(s_iota, 8)
        link = [0]

        def chain(ins):
            ins.then_inc(s_route, 1)
            link[0] += 1
            dve.wait_ge(s_route, link[0])

        def over(ap, n, m):
            return ap.unsqueeze(1).to_broadcast([P, n, m])

        chain(tt(oh[:], bc(expert_of[:], E), over(io_e[:], NT, E), ALU.is_equal))
        dve.wait_ge(s_pp, 1)
        chain(dve.tensor_copy(r_tot[:].rearrange("p n e -> p (n e)"), bank[1][:, 0:NT * E]))
        for e in range(E):
            ins = dve.tensor_tensor_scan(r_cum[:, :, e], ones_nt[:], r_tot[:, :, e], 0.0, ALU.mult, ALU.add)
            if e < E - 1:
                ins.then_inc(s_route, 1)
                link[0] += 1
        chain(ins)
        chain(tt(r_cmp[:], bc(r_cum[:, NT - 1, :], NT), over(io_t[:], E, NT), ALU.is_gt))
        chain(dve.tensor_reduce(r_nt[:], r_cmp[:], AX_X, ALU.add))
        chain(dve.tensor_tensor_scan(r_ct[:], ones_nt[:, 0:E], r_nt[:], 0.0, ALU.mult, ALU.add))
        chain(tt(r_base[:], r_ct[:], r_nt[:], ALU.subtract))
        chain(ts(r_base[:], r_base[:], float(P), None, ALU.mult))
        chain(tt(r_a[:], r_cum[:], r_tot[:], ALU.subtract))
        chain(tt(r_a[:], r_a[:], bank[0][:, 0:NT * E].rearrange("p (n e) -> p n e", e=E), ALU.add))
        chain(tt(r_a[:], r_a[:], over(r_base[:], NT, E), ALU.add))
        chain(tt(r_a[:], r_a[:], oh[:], ALU.mult))
        chain(dve.tensor_reduce(r_posf[:], r_a[:], AX_X, ALU.add))
        chain(dve.tensor_copy(r_pos[:, 0], r_posf[:]))
        chain(ts(r_pos[:, 1], r_pos[:, 0], 7, None, ALU.arith_shift_right))
        chain(ts(r_pos[:, 2], r_pos[:, 0], P - 1, None, ALU.bitwise_and))
        chain(dve.tensor_copy(r_place[:], r_pos[:, 1:3]))
        chain(tt(in_tile[:], bc(r_place[:, 0], TILES_MAX), over(io_i[:], NT, TILES_MAX), ALU.is_equal))
        assert link[0] == ROUTE_IN_TILE
        for q in range(QUARTERS):
            part = slice(q * NT // QUARTERS, (q + 1) * NT // QUARTERS)
            chain(tt(in_row[:, part], bc(r_place[:, 1, part], P), over(io_r[:], NT // QUARTERS, P), ALU.is_equal))
        chain(tt(r_cmp2[:], bc(io_i[:], E), over(r_ct[:], TILES_MAX, E), ALU.is_ge))
        chain(dve.tensor_reduce(r_te[:], r_cmp2[:], AX_X, ALU.add))
        chain(ts(tile_expert[:, 0:TILES_MAX], r_te[:], float(E - 1), None, ALU.min))
        assert link[0] == ROUTE_EXPERTS
        dve.wait_ge(s_pp, 2)
        found = bank[2][:, 0:2 * TILES_MAX].rearrange("p (w i) -> p w i", w=2)
        chain(ts(r_id[:, 0], found[:, 1], 0.0, float(B * S + 1), ALU.is_equal, ALU.mult))
        chain(ts(r_id[:, 1], found[:, 0], float(P), -1.0, ALU.mult, ALU.add))
        chain(tt(r_id[:, 2], r_id[:, 0], found[:, 1], ALU.add))
        chain(tt(r_id[:, 2], r_id[:, 2], r_id[:, 1], ALU.add))
        chain(ts(r_id[:, 3], r_id[:, 2], float(B * S - 1), None, ALU.min))
        chain(dve.tensor_copy(sorted_row[:], r_id[:, 3]))
        assert link[0] == ROUTE_ALL

        def of_tile(which, i):
            return r_id[:, which, i:i + 1] if isinstance(i, int) else r_id[:, which, bass.ds(i, 1)]

        def step(k, n, nxt):
            for u in range(nxt):
                after_tile(dve, "m_loaded", k, u)
                ts(m_row[:, 0, u], of_tile(3, 2 * k + 2 + u), 1.0, None, ALU.mult).then_inc(mig[u]["m_row"], 1)
            for u in range(n):
                after_tile(dve, "m_silu", k, u)
                tt(m_h[:, u], bank[2 + 2 * u][:], m_sg[:, u], ALU.mult).then_inc(mig[u]["m_h"], 1)
            for u in range(n):
                after_tile(dve, "m_stored", k, u, 0)
                ts(m_token[:, u], of_tile(2, 2 * k + u), 1.0, None, ALU.mult)
                after_tile(dve, "m_down", k, u)
                after_tile(dve, "m_skip", k, u)
                if u < nxt:
                    ts(m_row[:, 1, u], of_tile(3, 2 * k + 2 + u), 1.0, None, ALU.mult)
                tt(m_out[:, u], bank[DOWN_BANK[u]][:, 0:D], m_skip[:, u], ALU.add).then_inc(mig[u]["m_out"], 1)

        tile_steps(dve, step)

    @block.tensor
    def _(pe):
        mm = nc.tensor.matmul

        def product(out, lhsT, rhs, first=True, last=True, **kw):
            return mm(out, lhsT=lhsT, rhs=rhs, start=first, stop=last, **kw)

        pe.wait_ge(s_setup_dma, ALL_LOADED)
        pe.wait_ge(s_const, CONSTS)
        product(bank[0][0:H0, 0:S], relb[:], onehot).then_inc(s_pe_setup, 1)
        for c in range(C):
            ins = nc.tensor.transpose(bank[1][:, c * E:(c + 1) * E], cent[:, c * P:(c + 1) * P], ident[0:E, 0:E])
        ins.then_inc(s_pe_setup, 1)
        pe.wait_ge(s_cent, 2)
        for c in range(C):
            ins = product(bank[2][:, 0:E], ones[:], cent_sq[:, c], c == 0, c == C - 1)
        ins.then_inc(s_pe_setup, 1)
        pe.wait_ge(s_w, C)
        pe.wait_ge(s_cent, 3)

        def transposes(it, job, x):
            ps = claim(pe, it, job)
            for c in range(C):
                for t in range(T):
                    ins = nc.tensor.transpose(ps[:, c * S + t * P:c * S + (t + 1) * P], x[:, t, c * P:(c + 1) * P],
                                              ident[:])
            ins.then_inc(f_sem(job), 1)

        def rows_out(it, job, xT, w, chunks=C):
            ps = claim(pe, it, job)
            for t in range(T):
                for c in range(chunks):
                    ins = product(ps[:, t * D:(t + 1) * D], xT[:, c, tok(t)], w[:, c, :], c == 0, c == chunks - 1)
            ins.then_inc(f_sem(job), 1)

        def cols_out(it, job, xT, w, first_chunk):
            ps = claim(pe, it, job)
            for m in range(2):
                for c in range(C):
                    at = (first_chunk + m) * P
                    ins = product(ps[:, m * S:(m + 1) * S], w[:, c, at:at + P], xT[:, c, :], c == 0, c == C - 1)
            ins.then_inc(f_sem(job), 1)

        def scores(it, st, n):
            job = f"{st}.s{n}"
            ps = claim(pe, it, job)
            if st == "A":
                h = A_HEADS[n]
                r, g = 64 * (h % 2), h // 2
                product(ps[:, 0:S], a_kT[r:r + 64, g, 0:P], a_qT[r:r + 64, g, :])
                product(ps[:, S:SCOLS], a_kT[r:r + 64, g, P:], a_qT[r:r + 64, g, P:]).then_inc(f_sem(job), 1)
            else:
                r, m = 32 * (n % 4), n // 4
                for kt in range(T):
                    out = ps[:, kt * S:(kt + 1) * S]
                    product(out, ones_r[r:r + 1, :], b_nmT[r:r + 1, m, :], True, False)
                    parts = ((b_kh, b_qh), (b_kh, b_ql), (b_kl, b_qh))
                    for i, (k, q) in enumerate(parts):
                        ins = product(out, k[r:r + 32, m, tok(kt)], q[r:r + 32, m, :], False, i == len(parts) - 1)
                ins.then_inc(f_sem(job), 1)

        def weigh(it, st, n):
            if st == "A":
                c_, par = n // 2, n % 2
                job = f"A.o{c_}"
                ps = claim(pe, it, job) if par == 0 else bank[BANK_OF[job]]
                after(pe, "a_p", it.batch("A"), GROUP * (n + 1))
                slot = GROUP * n % NPA
                ones_half = halves[:, par]
                for kt, queries, cols in ((0, slice(0, S), slice(0, S)), (1, slice(P, S), slice(S, SCOLS))):
                    for half in range(2):
                        at = slice(half * S + queries.start, half * S + queries.stop)
                        for j in range(GROUP):
                            lhs = ones_half if half else a_v[:, kt, par, GROUP * c_ + j]
                            ins = product(ps[32 * j:32 * j + 32, at], lhs, a_p[:, slot + j, cols],
                                          par == 0 and kt == 0 and half == 0, False, skip_group_check=True,
                                          tile_position=(0, 32 * j))
                ins.then_inc(sig["a_p_used"], 1)
                if par == 0:
                    for p_ in range(2):
                        v = a_v[:, 1, p_, GROUP * c_:GROUP * (c_ + 1)].rearrange("p j d -> p (j d)")
                        product(ps[:, 0:1], v, ones[:, 0:1], False, False, skip_group_check=True)
                    product(ps[:, S:S + 1], ones[:], ones[:, 0:1], False, False, skip_group_check=True)
            else:
                job = f"B.o{n}"
                ps = claim(pe, it, job)
                taken(pe, it, f"B.s{GROUP * n + GROUP - 1}")
                for kt in range(T):
                    for half in range(2):
                        for j in range(GROUP):
                            h = GROUP * n + j
                            lhs = ones[:, 0:D1] if half else b_v[:, kt, h * D1:(h + 1) * D1]
                            ins = product(ps[32 * j:32 * j + 32, half * S:(half + 1) * S], lhs, b_p[:, h % NPB, kt],
                                          kt == 0 and half == 0, False, skip_group_check=True,
                                          tile_position=(0, 32 * j))
                ins.then_inc(sig["b_p_used"], 1)

        def turn(it):
            A, Bb, Dd, Cc = (st in it.stages for st in "ABDC")
            a, b, dd, c = (it.batch(st) for st in "ABDC")
            if A:
                after(pe, "a_xn", a)
                transposes(it, "A.xn", a_xn)
            if it.first == 2:
                pe.wait_ge(s_later, LATER_LOADED)
                pe.wait_ge(s_w, 3 * C + 2)
            if Bb:
                after(pe, "b_loaded", b)
                transposes(it, "B.ctx", c_in)
            if Dd:
                after(pe, "b_q", dd)
                transposes(it, "D.q", b_q)
            if A:
                taken(pe, it, "A.xn")
                for t in range(T):
                    ps = claim(pe, it, f"A.qk{t}")
                    for c_ in range(C):
                        ins = product(ps[:], a_xnT[:, c_, tok(t)], w0qk[:, c_, :], c_ == 0, c_ == C - 1)
                    ins.then_inc(f_sem(f"A.qk{t}"), 1)
            if Bb:
                taken(pe, it, "B.ctx")
                cols_out(it, "B.k", b_ctxT, w1k, 0)
                after(pe, "b_xl", b)
                transposes(it, "B.x", b_xl)
            if A and it.first > 1:
                rows_out(it, "A.v", a_xnT, w0v)
            if Bb:
                taken(pe, it, "B.x")
                cols_out(it, "B.q_", b_xT, w1q, 0)
            if Dd:
                taken(pe, it, "D.q")
                cols_out(it, "D.h0", b_zT, w11, 0)

            def rough(jobs):
                for n in jobs:
                    t, r = n // 4, 32 * (n % 4)
                    ps = claim(pe, it, f"B.m{n}")
                    for m in range(C):
                        ins = product(ps[:, m * S:(m + 1) * S], b_qh[r:r + 32, m, tok(t)], b_kh[r:r + 32, m, :])
                    ins.then_inc(f_sem(f"B.m{n}"), 1)

            if Bb:
                after(pe, "b_hi", b)
                rough(range(4))
            if Bb:
                rows_out(it, "B.v", b_ctxT, w1v)
                rough((4, 5))
            if Dd:
                cols_out(it, "D.h1", b_zT, w11, 2)
            if Bb:
                rough((6, 7))
            if Dd:
                cols_out(it, "D.h2", b_zT, w11, 4)
            for t in range(T):
                if A:
                    for n, name in enumerate(("q", "k")):
                        after(pe, f"a_lo_{name}", a, t + 1)
                        ps = claim(pe, it, f"A.{name}{t}")[:].bitcast(F16)
                        for g in range(H0 // 2):
                            h = n * H0 + 2 * g
                            ins = nc.tensor.transpose(
                                ps[:, g * P:(g + 1) * P],
                                a_split[:, t, h:h + 2].rearrange("p h s d -> p (h s d)"), ident16[:])
                        ins.then_inc(f_sem(f"A.{name}{t}"), 1)
            if Dd:
                cols_out(it, "D.h3", b_zT, w11, 6)
            if it.first == 1:
                pe.wait_ge(s_v, V_LOADED)
                pe.wait_ge(s_w, 2 * C)
                rows_out(it, "A.v", a_xnT, w0v)
            if Bb:
                for n in (4, 5, 6, 7):
                    taken(pe, it, f"B.m{n}")
                ps = claim(pe, it, "B.max")
                for m in range(C):
                    for t in range(T):
                        ins = nc.tensor.transpose(ps[:, m * S + t * P:m * S + (t + 1) * P],
                                                  b_nm[:, t, m].rearrange("p j w -> p (j w)"), ident[:])
                ins.then_inc(f_sem("B.max"), 1)
            if A:
                taken(pe, it, f"A.q{T - 1}")
                taken(pe, it, f"A.k{T - 1}")
                taken(pe, it, "A.v")
            def out_eighth(n):
                if n == 0:
                    claim(pe, it, "D.out")
                t, ps = n // 4, bank[BANK_OF["D.out"]]
                for j in range(2 * (n % 4), 2 * (n % 4) + 2):
                    if t == 0 and j % 2 == 0:
                        taken(pe, it, f"D.h{j // 2}")
                    ins = product(ps[:, t * D:(t + 1) * D], b_hT[:, j, tok(t)], w12[:, j, :], j == 0, j == J - 1)
                if n == 7:
                    ins.then_inc(f_sem("D.out"), 1)

            for what, st, n in PLAN:
                if st not in it.stages:
                    continue
                if what == "score":
                    if st == "B" and n == 0:
                        taken(pe, it, "B.max")
                        taken(pe, it, "B.v")
                        taken(pe, it, "B.k")
                        taken(pe, it, "B.q_")
                    scores(it, st, n)
                if what == "weigh":
                    weigh(it, st, n)
                if what == "out":
                    out_eighth(n)
                if what == "rows":
                    after(pe, "c_rows", c, 1)
                    transposes(it, "C.xn", c_rows)
                if what == "distances":
                    taken(pe, it, "C.xn")
                    ps = claim(pe, it, "C.dist")
                    for t in range(T):
                        for c_ in range(C):
                            ins = product(ps[:, t * E:(t + 1) * E], c_xnT[:, c_, tok(t)], cent_t[:, c_], c_ == 0,
                                          c_ == C - 1)
                    ins.then_inc(f_sem("C.dist"), 1)
            if A:
                taken(pe, it, "A.o0")
                taken(pe, it, "A.o1")
                rows_out(it, "A.wo", a_yT, w0o)
            if Dd:
                out_eighth(5)
            if Bb:
                taken(pe, it, "B.o0")
                taken(pe, it, "B.o1")
                rows_out(it, "B.wo", b_yT, w1o)
            if Dd:
                out_eighth(6)
            if A:
                after(pe, "a_z", a)
                transposes(it, "A.z", a_xn)
            if Dd:
                out_eighth(7)
            if A:
                taken(pe, it, "A.z")
                if it.first == 1:
                    pe.wait_ge(s_a_loaded, A_LOADED)
                    pe.wait_ge(s_w, 3 * C)
                for n in range(4):
                    cols_out(it, f"A.h{n}", a_xnT, w01, 2 * n)
                ps = claim(pe, it, "A.out")
                for t in range(T):
                    for j in range(J):
                        if t == 0 and j % 2 == 0:
                            taken(pe, it, f"A.h{j // 2}")
                        ins = product(ps[:, t * D:(t + 1) * D], a_hT[:, j, tok(t)], w02[:, j, :], j == 0, j == J - 1)
                ins.then_inc(f_sem("A.out"), 1)

        each(pe, turn)

        pe.wait_ge(s_route, 1)
        flat = oh[:].rearrange("p n e -> p (n e)")
        product(bank[0][:, 0:NT * E], tri[:], flat)
        product(bank[1][:, 0:NT * E], ones[:], flat).then_inc(s_pp, 1)
        pe.wait_ge(s_numbered, 2)
        for n in range(NT):
            if n % (NT // QUARTERS) == 0:
                pe.wait_ge(s_route, ROUTE_IN_TILE + 1 + n // (NT // QUARTERS))
            ins = product(bank[2][:, 0:2 * TILES_MAX], in_row[:, n], number[:, n].rearrange("p w i -> p (w i)"),
                          n == 0, n == NT - 1)
        ins.then_inc(s_pp, 1)

        pe.wait_ge(s_route, ROUTE_ALL)
        pe.wait_ge(s_wmoe, 16 * 2 * E)

        def transpose_in(k, u):
            after_tile(pe, "m_loaded", k, u)
            after_tile(pe, "m_xT", k, u, 0)
            for c in range(C):
                ins = nc.tensor.transpose(bank[u][:, c * P:(c + 1) * P], m_in[:, u, c * P:(c + 1) * P], ident[:])
            ins.then_inc(mig[u]["m_x"], 1)

        transpose_in(0, 0)
        transpose_in(0, 1)

        def step(k, n, nxt):
            expert = []
            for u in range(n):
                i = 2 * k + u
                at = tile_expert[0:1, i:i + 1] if isinstance(i, int) else tile_expert[0:1, bass.ds(i, 1)]
                expert.append(pe.value_load(at, min_val=0, max_val=E - 1))
            for u in range(n):
                after_tile(pe, "m_xT", k, u)
                after_tile(pe, "m_h", k, u, 0)
                if u == 0:
                    after_tile(pe, "m_hT", k, 1, 0)
                else:
                    after_tile(pe, "m_out", k, 1, 0)
                for half in range(2):
                    for c in range(C):
                        w = up[:, bass.ds(expert[u], 1), c, half * EH:(half + 1) * EH]
                        ins = product(bank[2 + 2 * u + half][:], m_xT[:, u, c], w.rearrange("p o n -> p (o n)"),
                                      c == 0, c == C - 1)
                ins.then_inc(mig[u]["m_up"], 1)
            for u in range(nxt):
                transpose_in(k + 1, u)
            for u in range(n):
                after_tile(pe, "m_h", k, u)
                if u == 0:
                    after_tile(pe, "m_hT", k, 0, 0)
                for j in range(EJ):
                    ins = nc.tensor.transpose(bank[H_BANK[u]][:, j * P:(j + 1) * P], m_h[:, u, j * P:(j + 1) * P],
                                              ident[:])
                ins.then_inc(mig[u]["m_ht"], 1)
            for u in range(n):
                after_tile(pe, "m_hT", k, u)
                if u == 0:
                    after_tile(pe, "m_out", k, 0, 0)
                for j in range(EJ):
                    w = down[:, bass.ds(expert[u], 1), j, :]
                    ins = product(bank[DOWN_BANK[u]][:, 0:D], m_hT[:, u, j], w.rearrange("p o n -> p (o n)"), j == 0,
                                  j == EJ - 1)
                ins.then_inc(mig[u]["m_down"], 1)

        tile_steps(pe, step)


_INS = ["x", "ctx_1024", "L0_attn_ln1_w", "L0_attn_Wq", "L0_attn_Wk", "L0_attn_Wv", "L0_attn_rel_bias",
        "L0_attn_scale", "L0_attn_Wo", "L0_attn_ln2_w", "L0_attn_W1", "L0_attn_W2", "L0_xattn_Wq", "L0_xattn_Wk",
        "L0_xattn_Wv", "L0_xattn_Wo", "L0_xattn_lambda_param", "L0_xattn_ln1_g", "L0_xattn_ln1_b",
        "L0_xattn_ln2_g", "L0_xattn_ln2_b", "L0_xattn_ffn_w1", "L0_xattn_ffn_b1", "L0_xattn_ffn_w2",
        "L0_xattn_ffn_b2", "L0_ffn_scale", "L0_ffn_centroids", "L0_ffn_up_w", "L0_ffn_down_w"]


def bucket_onehot():
    dist = np.arange(S)
    exact = BUCKETS // 2
    safe = np.maximum(dist, 1).astype(np.float32)
    ratio = np.log(safe / np.float32(exact)) / np.float32(np.log(128 / exact)) * np.float32(BUCKETS - exact)
    bucket = np.where(dist < exact, dist, np.minimum(exact + ratio.astype(np.int32), BUCKETS - 1))
    return (np.arange(BUCKETS)[:, None] == bucket[None, :]).astype(np.float32)


def kernel(**inputs):
    import concourse.bacc as _bacc
    from concourse.bass_utils import run_bass_kernel_spmd as _run

    nc = _bacc.Bacc("TRN2", target_bir_lowering=False, num_devices=1)
    arrays, d = {}, {}
    for name in _INS:
        a = np.ascontiguousarray(inputs[name])
        if a.ndim == 0:
            a = a.reshape(1, 1)
        arrays[f"in_{name}"] = a
        d[name] = nc.dram_tensor(f"in_{name}", a.shape, mybir.dt.from_np(a.dtype), kind="ExternalInput").ap()
    a = bucket_onehot()
    arrays["in_bucket_onehot"] = a
    d["bucket_onehot"] = nc.dram_tensor("in_bucket_onehot", a.shape, F32, kind="ExternalInput").ap()
    d["out"] = nc.dram_tensor("out_rows", (B * S, D), F32, kind="ExternalOutput").ap()
    build(nc, d)
    r = _run(nc, [arrays], core_ids=[0])
    return r.results[0]["out_rows"].reshape(B, S, D)
```
